# Optimizing a Trainium2 kernel written in Bass

```python
import numpy as np
import jax
import jax.numpy as jnp

def _softmax(x, axis=-1):
    return jax.nn.softmax(x, axis=axis)

def _gelu(x):
    return jax.nn.gelu(x, approximate=True)

def _silu(x):
    return jax.nn.silu(x)

def _sigmoid(x):
    return jax.nn.sigmoid(x)

def _layernorm(x, axis=-1, eps=1e-05):
    m = jnp.mean(x, axis=axis, keepdims=True)
    v = jnp.var(x, axis=axis, keepdims=True)
    return (x - m) / jnp.sqrt(v + eps)

def _scatter_add(tgt, idx, src, axis=0):
    return tgt.at[idx].add(src)

def _segment_sum(src, seg, n):
    return jax.ops.segment_sum(src, seg, n)
kernel_name = 'mk_perceiver_d2_seqx_r8_8bb12e'

def setup_inputs(seed: int=0):
    np.random.seed(seed)
    _w = jnp.asarray

    def _rec_inputs():
        import jax
        import jax.numpy as jnp
        _rk = jax.random.key(seed)
        x = 7.22e-05 + 1 * jax.random.normal(jax.random.fold_in(_rk, 1), (2, 128, 256), jnp.float32)
        _lenS = 128 - jax.random.randint(jax.random.fold_in(_rk, 7), (2,), 0, max(1, 128 // 4) + 1, jnp.int32)
        _lenS2 = 2048 - jax.random.randint(jax.random.fold_in(_rk, 8), (2,), 0, max(1, 2048 // 4) + 1, jnp.int32)
        _ctx_512P = jax.random.normal(jax.random.fold_in(_rk, 11), (2, 16, 64), jnp.float32)
        _ctx_512c = jax.random.dirichlet(jax.random.fold_in(_rk, 511), 0.3 * jnp.ones((16,), jnp.float32), (2, 2048))
        _ctx_512t = jnp.einsum('bsk,bkd->bsd', _ctx_512c, _ctx_512P)
        _ctx_512t = _ctx_512t * jax.lax.rsqrt(jnp.mean(jnp.square(_ctx_512t)) + 1e-12) * 0.953939
        ctx_512 = -0.000514642 + 1.00011 * (_ctx_512t + 0.3 * jax.random.normal(jax.random.fold_in(_rk, 611), (2, 2048, 64), jnp.float32))
        return (x, ctx_512)
    x, ctx_512 = _rec_inputs()

    def _L0_xattn_setup():
        import jax, jax.numpy as jnp
        import numpy as np
        B, S, H, NH, L = (2, 256, 256, 16, 64)
        HD = H // NH
        key = jax.random.key(seed)
        k1, k2, k3, k4, k5 = jax.random.split(key, 5)
        scale = 0.02
        return {'q': jax.random.normal(k1, (B, S, H), dtype=jnp.float32), 'latent_kv': jax.random.normal(k2, (B, S, L), dtype=jnp.float32), 'Wq': jax.random.normal(k3, (H, H), dtype=jnp.float32) * scale, 'Wkv_expand': jax.random.normal(k4, (2 * H, L), dtype=jnp.float32) * scale, 'Wout': jax.random.normal(k5, (H, H), dtype=jnp.float32) * scale}
    _L0_xattn_all = _L0_xattn_setup()
    _L0_xattn_in = {k: v for k, v in _L0_xattn_all.items() if k in ('Wq', 'Wkv_expand', 'Wout')}
    del _L0_xattn_all

    def _L0_attn_setup():
        import jax, jax.numpy as jnp
        import numpy as np
        B, S, D = (2, 256, 256)
        HQK, HV, HD = (16, 32, 128)
        K = 4
        CHUNK = 64
        EPS = 1e-06

        def _rmsnorm(x, eps=EPS):
            return x * jax.lax.rsqrt(jnp.mean(x * x, axis=-1, keepdims=True) + eps)

        def _chunk_gated_delta_rule(q, k, v, g, beta):
            inv = HD ** (-0.5)
            q = _rmsnorm(q) * inv
            k = _rmsnorm(k) * inv
            tr = lambda t: jnp.swapaxes(t, 1, 2).astype(jnp.float32)
            q, k, v = (tr(q), tr(k), tr(v))
            g, beta = (tr(g), tr(beta))
            Bq, H, S0 = (q.shape[0], q.shape[1], q.shape[2])
            pad = -S0 % CHUNK
            if pad:
                pz4 = [(0, 0), (0, 0), (0, pad), (0, 0)]
                q, k, v = (jnp.pad(q, pz4), jnp.pad(k, pz4), jnp.pad(v, pz4))
                pz3 = [(0, 0), (0, 0), (0, pad)]
                g, beta = (jnp.pad(g, pz3), jnp.pad(beta, pz3))
            Sp = S0 + pad
            NC = Sp // CHUNK
            q = q * HD ** (-0.5)
            v_beta = v * beta[..., None]
            k_beta = k * beta[..., None]
            rs = lambda t: t.reshape(Bq, H, NC, CHUNK, -1)
            q, k, v, k_beta, v_beta = (rs(q), rs(k), rs(v), rs(k_beta), rs(v_beta))
            g = jnp.cumsum(g.reshape(Bq, H, NC, CHUNK), axis=-1)
            tril = jnp.tril(jnp.ones((CHUNK, CHUNK), bool))
            stril = jnp.tril(jnp.ones((CHUNK, CHUNK), bool), -1)
            decay = jnp.where(tril, jnp.exp(g[..., :, None] - g[..., None, :]), 0.0)
            M = jnp.where(stril, jnp.einsum('bhncd,bhnmd->bhncm', k_beta, k) * decay, 0.0)
            eye = jnp.eye(CHUNK, dtype=q.dtype)
            T = jax.scipy.linalg.solve_triangular(eye + M, jnp.broadcast_to(eye, M.shape), lower=True)
            v_c = jnp.einsum('bhnij,bhnjd->bhnid', T, v_beta)
            k_cumdecay = jnp.einsum('bhnij,bhnjd->bhnid', T, k_beta * jnp.exp(g)[..., None])

            def step(state, inp):
                q_i, k_i, v_i, g_i, dec_i, kcd_i = inp
                attn = jnp.einsum('bhcd,bhed->bhce', q_i, k_i) * dec_i
                v_new = v_i - jnp.einsum('bhcd,bhde->bhce', kcd_i, state)
                out_i = jnp.einsum('bhcd,bhde->bhce', q_i * jnp.exp(g_i)[..., None], state) + jnp.einsum('bhce,bhed->bhcd', attn, v_new)
                g_last = g_i[..., -1]
                state = state * jnp.exp(g_last)[..., None, None] + jnp.einsum('bhcd,bhce->bhde', k_i * jnp.exp(g_last[..., None] - g_i)[..., None], v_new)
                return (state, out_i)
            mv = lambda t: jnp.moveaxis(t, 2, 0)
            init = jnp.zeros((Bq, H, HD, HD), q.dtype)
            _, out = jax.lax.scan(step, init, (mv(q), mv(k), mv(v_c), mv(g), mv(decay), mv(k_cumdecay)))
            out = jnp.moveaxis(out, 0, 2).reshape(Bq, H, Sp, HD)[:, :, :S0]
            return jnp.swapaxes(out, 1, 2)
        key = jax.random.key(seed)
        ks = jax.random.split(key, 8)
        qkvz_dim = (2 * HQK + 2 * HV) * HD
        ba_dim = 2 * HV
        conv_dim = (2 * HQK + HV) * HD
        f32 = jnp.float32
        return {'x': jax.random.normal(ks[0], (B, S, D), f32), 'W_qkvz': jax.random.normal(ks[1], (qkvz_dim, D), f32) * 0.02, 'W_ba': jax.random.normal(ks[2], (ba_dim, D), f32) * 0.02, 'conv_w': jax.random.normal(ks[3], (conv_dim, K), f32) * 0.3, 'dt_bias': jnp.ones((HV,), f32), 'A_log': jax.random.uniform(ks[4], (HV,), f32, minval=0.0, maxval=2.0), 'norm_w': jnp.ones((HD,), f32), 'W_out': jax.random.normal(ks[5], (D, HV * HD), f32) * 0.02}
    _L0_attn_all = _L0_attn_setup()
    _L0_attn_in = {k: v for k, v in _L0_attn_all.items() if k in ('W_qkvz', 'W_ba', 'conv_w', 'dt_bias', 'A_log', 'norm_w', 'W_out')}
    del _L0_attn_all

    def _L0_ffn_setup():
        import jax, jax.numpy as jnp
        import numpy as np
        DIM = 256
        INNER = 4 * DIM
        EPS = 1e-05

        def simple_rms_norm(x):
            d = x.shape[-1]
            n = jnp.linalg.norm(x, axis=-1, keepdims=True)
            return x / jnp.maximum(n, 1e-12) * jnp.sqrt(jnp.asarray(d, x.dtype))

        def activation_quant(x):
            scale = 127.0 / jnp.clip(jnp.max(jnp.abs(x), axis=-1, keepdims=True), EPS)
            return jnp.clip(jnp.round(x * scale), -128, 127) / scale

        def weight_quant(w):
            scale = 1.0 / jnp.clip(jnp.mean(jnp.abs(w)), EPS)
            return jnp.clip(jnp.round(w * scale), -1, 1) / scale

        def ste(x, q):
            return x + jax.lax.stop_gradient(q - x)

        def bitlinear158(x, w):
            xn = simple_rms_norm(x)
            xq = ste(xn, activation_quant(xn))
            wq = ste(w, weight_quant(w))
            return jnp.einsum('bsi,oi->bso', xq, wq)
        key = jax.random.key(seed)
        k1, k2, k3 = jax.random.split(key, 3)
        x = jax.random.normal(k1, (4, 256, DIM), dtype=jnp.float32)
        w1 = jax.random.normal(k2, (INNER, DIM), dtype=jnp.float32) * DIM ** (-0.5)
        w2 = jax.random.normal(k3, (DIM, INNER), dtype=jnp.float32) * INNER ** (-0.5)
        return {'x': x, 'w1': w1, 'w2': w2}
    _L0_ffn_all = _L0_ffn_setup()
    _L0_ffn_in = {k: v for k, v in _L0_ffn_all.items() if k in ('w1', 'w2')}
    del _L0_ffn_all

    def _L1_xattn_setup():
        import jax, jax.numpy as jnp
        import numpy as np
        B, S, L = (2, 128, 128)
        DIM_Q, H, K, D_C, D_CQ, R = (256, 16, 128, 64, 192, 64)

        def _rope_tables(length, dim):
            inv = 1.0 / 10000.0 ** (jnp.arange(0, dim, 2, dtype=jnp.float32) / dim)
            f = jnp.arange(length, dtype=jnp.float32)[:, None] * inv[None, :]
            sin = jnp.repeat(jnp.sin(f), 2, axis=-1)
            cos = jnp.repeat(jnp.cos(f), 2, axis=-1)
            return (sin, cos)

        def _rotate_half(x):
            half = x.shape[-1] // 2
            return jnp.concatenate([-x[..., half:], x[..., :half]], axis=-1)

        def _apply_rope(x, sin, cos):
            return x * cos + _rotate_half(x) * sin
        key = jax.random.key(seed)
        ks = jax.random.split(key, 8)
        return {'hidden_q': jax.random.normal(ks[0], (B, S, DIM_Q), jnp.float32), 'kv_c': jax.random.normal(ks[1], (B, L, D_C), jnp.float32), 'Wq': jax.random.normal(ks[2], (H * K, DIM_Q), jnp.float32) / np.sqrt(DIM_Q).astype(np.float32), 'w_kc_q': jax.random.normal(ks[3], (H, K, D_CQ), jnp.float32) / np.sqrt(K).astype(np.float32), 'w_kc_kv': jax.random.normal(ks[4], (H, K, D_C), jnp.float32) / np.sqrt(K).astype(np.float32), 'W_qr': jax.random.normal(ks[5], (H, D_CQ, R), jnp.float32) / np.float32(np.sqrt(D_CQ) * np.sqrt(R)), 'W_kr': jax.random.normal(ks[6], (H, D_C, R), jnp.float32) / np.sqrt(D_C).astype(np.float32), 'Wo': jax.random.normal(ks[7], (DIM_Q, H * K), jnp.float32) / np.sqrt(H * K).astype(np.float32)}
    _L1_xattn_all = _L1_xattn_setup()
    _L1_xattn_in = {k: v for k, v in _L1_xattn_all.items() if k in ('Wq', 'w_kc_q', 'w_kc_kv', 'W_qr', 'W_kr', 'Wo')}
    del _L1_xattn_all

    def _L1_attn_setup():
        import jax, jax.numpy as jnp
        import numpy as np
        DIM = 256
        H = 16
        HKV = 4
        NREP = H // HKV
        ROPE_D = 64
        NOPE_D = 128
        V_D = 128
        QK_D = ROPE_D + NOPE_D
        KV_RANK = 64
        Q_RANK = 192
        B, T = (2, 256)

        def _rope_cache(seq_len, head_dim, dtype=jnp.float32):
            theta = 1.0 / 10000.0 ** (jnp.arange(0, head_dim, 2, dtype=dtype) / head_dim)
            pos = jnp.arange(seq_len, dtype=dtype)
            ang = jnp.outer(pos, theta)
            ang = jnp.concatenate([ang, ang], axis=-1)
            return (jnp.cos(ang), jnp.sin(ang))

        def _rotate_half(x):
            half = x.shape[-1] // 2
            return jnp.concatenate([-x[..., half:], x[..., :half]], axis=-1)

        def _apply_rope(x, cos, sin):
            return x * cos[None, :, None, :] + _rotate_half(x) * sin[None, :, None, :]
        key = jax.random.key(seed)
        ks = jax.random.split(key, 9)
        s = 0.02
        return {'x': jax.random.normal(ks[0], (B, T, DIM), jnp.float32), 'W_kv_down': jax.random.normal(ks[1], (DIM, KV_RANK), jnp.float32) * s, 'W_k_nope': jax.random.normal(ks[2], (KV_RANK, HKV * NOPE_D), jnp.float32) * s, 'W_k_rope': jax.random.normal(ks[3], (KV_RANK, HKV * ROPE_D), jnp.float32) * s, 'W_v': jax.random.normal(ks[4], (KV_RANK, HKV * V_D), jnp.float32) * s, 'W_q_down': jax.random.normal(ks[5], (DIM, Q_RANK), jnp.float32) * s, 'W_q_nope': jax.random.normal(ks[6], (Q_RANK, H * NOPE_D), jnp.float32) * s, 'W_q_rope': jax.random.normal(ks[7], (Q_RANK, H * ROPE_D), jnp.float32) * s, 'W_o': jax.random.normal(ks[8], (H * V_D, DIM), jnp.float32) * s}
    _L1_attn_all = _L1_attn_setup()
    _L1_attn_in = {k: v for k, v in _L1_attn_all.items() if k in ('W_kv_down', 'W_k_nope', 'W_k_rope', 'W_v', 'W_q_down', 'W_q_nope', 'W_q_rope', 'W_o')}
    del _L1_attn_all

    def _L1_ffn_setup():
        import jax, jax.numpy as jnp
        import numpy as np
        B, S, H, F, E, R, K = (2, 128, 256, 896, 8, 32, 2)

        def _gather_slot(a_all, e):
            return jnp.take_along_axis(a_all, e[:, None, None], axis=1)[:, 0]
        key = jax.random.key(seed)
        ks = jax.random.split(key, 12)
        sc = 0.02
        n = lambda k, shape, s: jax.random.normal(k, shape, dtype=jnp.float32) * s
        return {'hidden_states': n(ks[0], (B, S, H), 1.0), 'Wg': n(ks[1], (E, H), sc), 'W1': n(ks[2], (F, H), sc), 'W2': n(ks[3], (H, F), sc), 'W3': n(ks[4], (F, H), sc), 'A1': n(ks[5], (E, R, H), sc), 'B1': n(ks[6], (E, F, R), sc), 'A2': n(ks[7], (E, R, F), sc), 'B2': n(ks[8], (E, H, R), sc), 'A3': n(ks[9], (E, R, H), sc), 'B3': n(ks[10], (E, F, R), sc)}
    _L1_ffn_all = _L1_ffn_setup()
    _L1_ffn_in = {k: v for k, v in _L1_ffn_all.items() if k in ('Wg', 'W1', 'W2', 'W3', 'A1', 'B1', 'A2', 'B2', 'A3', 'B3')}
    del _L1_ffn_all
    return {'x': x, 'ctx_512': ctx_512, 'L0_xattn_Wq': _L0_xattn_in['Wq'], 'L0_xattn_Wkv_expand': _L0_xattn_in['Wkv_expand'], 'L0_xattn_Wout': _L0_xattn_in['Wout'], 'L0_attn_W_qkvz': _L0_attn_in['W_qkvz'], 'L0_attn_W_ba': _L0_attn_in['W_ba'], 'L0_attn_conv_w': _L0_attn_in['conv_w'], 'L0_attn_dt_bias': _L0_attn_in['dt_bias'], 'L0_attn_A_log': _L0_attn_in['A_log'], 'L0_attn_norm_w': _L0_attn_in['norm_w'], 'L0_attn_W_out': _L0_attn_in['W_out'], 'L0_ffn_w1': _L0_ffn_in['w1'], 'L0_ffn_w2': _L0_ffn_in['w2'], 'L1_xattn_Wq': _L1_xattn_in['Wq'], 'L1_xattn_w_kc_q': _L1_xattn_in['w_kc_q'], 'L1_xattn_w_kc_kv': _L1_xattn_in['w_kc_kv'], 'L1_xattn_W_qr': _L1_xattn_in['W_qr'], 'L1_xattn_W_kr': _L1_xattn_in['W_kr'], 'L1_xattn_Wo': _L1_xattn_in['Wo'], 'L1_attn_W_kv_down': _L1_attn_in['W_kv_down'], 'L1_attn_W_k_nope': _L1_attn_in['W_k_nope'], 'L1_attn_W_k_rope': _L1_attn_in['W_k_rope'], 'L1_attn_W_v': _L1_attn_in['W_v'], 'L1_attn_W_q_down': _L1_attn_in['W_q_down'], 'L1_attn_W_q_nope': _L1_attn_in['W_q_nope'], 'L1_attn_W_q_rope': _L1_attn_in['W_q_rope'], 'L1_attn_W_o': _L1_attn_in['W_o'], 'L1_ffn_Wg': _L1_ffn_in['Wg'], 'L1_ffn_W1': _L1_ffn_in['W1'], 'L1_ffn_W2': _L1_ffn_in['W2'], 'L1_ffn_W3': _L1_ffn_in['W3'], 'L1_ffn_A1': _L1_ffn_in['A1'], 'L1_ffn_B1': _L1_ffn_in['B1'], 'L1_ffn_A2': _L1_ffn_in['A2'], 'L1_ffn_B2': _L1_ffn_in['B2'], 'L1_ffn_A3': _L1_ffn_in['A3'], 'L1_ffn_B3': _L1_ffn_in['B3']}

def reference(x, ctx_512, L0_xattn_Wq, L0_xattn_Wkv_expand, L0_xattn_Wout, L0_attn_W_qkvz, L0_attn_W_ba, L0_attn_conv_w, L0_attn_dt_bias, L0_attn_A_log, L0_attn_norm_w, L0_attn_W_out, L0_ffn_w1, L0_ffn_w2, L1_xattn_Wq, L1_xattn_w_kc_q, L1_xattn_w_kc_kv, L1_xattn_W_qr, L1_xattn_W_kr, L1_xattn_Wo, L1_attn_W_kv_down, L1_attn_W_k_nope, L1_attn_W_k_rope, L1_attn_W_v, L1_attn_W_q_down, L1_attn_W_q_nope, L1_attn_W_q_rope, L1_attn_W_o, L1_ffn_Wg, L1_ffn_W1, L1_ffn_W2, L1_ffn_W3, L1_ffn_A1, L1_ffn_B1, L1_ffn_A2, L1_ffn_B2, L1_ffn_A3, L1_ffn_B3):
    import jax
    import jax.numpy as jnp

    def _L0_xattn_ref(q, latent_kv, Wq, Wkv_expand, Wout):
        import jax, jax.numpy as jnp
        import numpy as np
        B, S, H, NH, L = (2, 256, 256, 16, 64)
        HD = H // NH
        b, sq, _ = q.shape
        sk = latent_kv.shape[1]
        qp = q @ Wq.T
        kv = latent_kv @ Wkv_expand.T
        k, v = jnp.split(kv, 2, axis=-1)
        qh = qp.reshape(b, sq, NH, HD).transpose(0, 2, 1, 3)
        kh = k.reshape(b, sk, NH, HD).transpose(0, 2, 1, 3)
        vh = v.reshape(b, sk, NH, HD).transpose(0, 2, 1, 3)
        inv_sqrt_d = 1.0 / jnp.sqrt(jnp.float32(HD))
        scores = jnp.einsum('bhqd,bhkd->bhqk', qh, kh) * inv_sqrt_d
        causal = jnp.tril(jnp.ones((sq, sk), dtype=bool))
        scores = jnp.where(causal, scores, jnp.finfo(scores.dtype).min)
        attn = jax.nn.softmax(scores, axis=-1)
        out = jnp.einsum('bhqk,bhkd->bhqd', attn, vh)
        out = out.transpose(0, 2, 1, 3).reshape(b, sq, H)
        return out @ Wout.T

    def _L0_attn_ref(x, W_qkvz, W_ba, conv_w, dt_bias, A_log, norm_w, W_out):
        import jax, jax.numpy as jnp
        import numpy as np
        B, S, D = (2, 256, 256)
        HQK, HV, HD = (16, 32, 128)
        K = 4
        CHUNK = 64
        EPS = 1e-06

        def _rmsnorm(x, eps=EPS):
            return x * jax.lax.rsqrt(jnp.mean(x * x, axis=-1, keepdims=True) + eps)

        def _chunk_gated_delta_rule(q, k, v, g, beta):
            inv = HD ** (-0.5)
            q = _rmsnorm(q) * inv
            k = _rmsnorm(k) * inv
            tr = lambda t: jnp.swapaxes(t, 1, 2).astype(jnp.float32)
            q, k, v = (tr(q), tr(k), tr(v))
            g, beta = (tr(g), tr(beta))
            Bq, H, S0 = (q.shape[0], q.shape[1], q.shape[2])
            pad = -S0 % CHUNK
            if pad:
                pz4 = [(0, 0), (0, 0), (0, pad), (0, 0)]
                q, k, v = (jnp.pad(q, pz4), jnp.pad(k, pz4), jnp.pad(v, pz4))
                pz3 = [(0, 0), (0, 0), (0, pad)]
                g, beta = (jnp.pad(g, pz3), jnp.pad(beta, pz3))
            Sp = S0 + pad
            NC = Sp // CHUNK
            q = q * HD ** (-0.5)
            v_beta = v * beta[..., None]
            k_beta = k * beta[..., None]
            rs = lambda t: t.reshape(Bq, H, NC, CHUNK, -1)
            q, k, v, k_beta, v_beta = (rs(q), rs(k), rs(v), rs(k_beta), rs(v_beta))
            g = jnp.cumsum(g.reshape(Bq, H, NC, CHUNK), axis=-1)
            tril = jnp.tril(jnp.ones((CHUNK, CHUNK), bool))
            stril = jnp.tril(jnp.ones((CHUNK, CHUNK), bool), -1)
            decay = jnp.where(tril, jnp.exp(g[..., :, None] - g[..., None, :]), 0.0)
            M = jnp.where(stril, jnp.einsum('bhncd,bhnmd->bhncm', k_beta, k) * decay, 0.0)
            eye = jnp.eye(CHUNK, dtype=q.dtype)
            T = jax.scipy.linalg.solve_triangular(eye + M, jnp.broadcast_to(eye, M.shape), lower=True)
            v_c = jnp.einsum('bhnij,bhnjd->bhnid', T, v_beta)
            k_cumdecay = jnp.einsum('bhnij,bhnjd->bhnid', T, k_beta * jnp.exp(g)[..., None])

            def step(state, inp):
                q_i, k_i, v_i, g_i, dec_i, kcd_i = inp
                attn = jnp.einsum('bhcd,bhed->bhce', q_i, k_i) * dec_i
                v_new = v_i - jnp.einsum('bhcd,bhde->bhce', kcd_i, state)
                out_i = jnp.einsum('bhcd,bhde->bhce', q_i * jnp.exp(g_i)[..., None], state) + jnp.einsum('bhce,bhed->bhcd', attn, v_new)
                g_last = g_i[..., -1]
                state = state * jnp.exp(g_last)[..., None, None] + jnp.einsum('bhcd,bhce->bhde', k_i * jnp.exp(g_last[..., None] - g_i)[..., None], v_new)
                return (state, out_i)
            mv = lambda t: jnp.moveaxis(t, 2, 0)
            init = jnp.zeros((Bq, H, HD, HD), q.dtype)
            _, out = jax.lax.scan(step, init, (mv(q), mv(k), mv(v_c), mv(g), mv(decay), mv(k_cumdecay)))
            out = jnp.moveaxis(out, 0, 2).reshape(Bq, H, Sp, HD)[:, :, :S0]
            return jnp.swapaxes(out, 1, 2)
        Bq, Sq, _ = x.shape
        ratio = HV // HQK
        mixed_qkvz = jnp.einsum('bsd,od->bso', x, W_qkvz)
        mixed_ba = jnp.einsum('bsd,od->bso', x, W_ba)
        qkvz = mixed_qkvz.reshape(Bq, Sq, HQK, 2 * HD + 2 * ratio * HD)
        ba = mixed_ba.reshape(Bq, Sq, HQK, 2 * ratio)
        q = qkvz[..., :HD]
        k = qkvz[..., HD:2 * HD]
        v = qkvz[..., 2 * HD:(2 + ratio) * HD].reshape(Bq, Sq, HV, HD)
        z = qkvz[..., (2 + ratio) * HD:].reshape(Bq, Sq, HV, HD)
        b = ba[..., :ratio].reshape(Bq, Sq, HV)
        a = ba[..., ratio:].reshape(Bq, Sq, HV)
        qkv = jnp.concatenate([q.reshape(Bq, Sq, -1), k.reshape(Bq, Sq, -1), v.reshape(Bq, Sq, -1)], axis=-1)
        conv_dim = qkv.shape[-1]
        xc = jnp.swapaxes(qkv, 1, 2)
        yc = jax.lax.conv_general_dilated(xc, conv_w[:, None, :], (1,), [(K - 1, 0)], feature_group_count=conv_dim)
        qkv = jax.nn.silu(jnp.swapaxes(yc, 1, 2))
        d_qk = HQK * HD
        q = qkv[..., :d_qk].reshape(Bq, Sq, HQK, HD)
        k = qkv[..., d_qk:2 * d_qk].reshape(Bq, Sq, HQK, HD)
        v = qkv[..., 2 * d_qk:].reshape(Bq, Sq, HV, HD)
        beta = jax.nn.sigmoid(b)
        g = -jnp.exp(A_log) * jax.nn.softplus(a + dt_bias)
        q = jnp.repeat(q, ratio, axis=2)
        k = jnp.repeat(k, ratio, axis=2)
        core = _chunk_gated_delta_rule(q, k, v, g, beta)
        h = core.astype(jnp.float32)
        h = h * jax.lax.rsqrt(jnp.mean(h * h, axis=-1, keepdims=True) + EPS)
        h = norm_w * h * jax.nn.silu(z.astype(jnp.float32))
        out = jnp.einsum('bsf,df->bsd', h.reshape(Bq, Sq, HV * HD), W_out)
        return out

    def _L0_ffn_ref(x, w1, w2):
        import jax, jax.numpy as jnp
        import numpy as np
        DIM = 256
        INNER = 4 * DIM
        EPS = 1e-05

        def simple_rms_norm(x):
            d = x.shape[-1]
            n = jnp.linalg.norm(x, axis=-1, keepdims=True)
            return x / jnp.maximum(n, 1e-12) * jnp.sqrt(jnp.asarray(d, x.dtype))

        def activation_quant(x):
            scale = 127.0 / jnp.clip(jnp.max(jnp.abs(x), axis=-1, keepdims=True), EPS)
            return jnp.clip(jnp.round(x * scale), -128, 127) / scale

        def weight_quant(w):
            scale = 1.0 / jnp.clip(jnp.mean(jnp.abs(w)), EPS)
            return jnp.clip(jnp.round(w * scale), -1, 1) / scale

        def ste(x, q):
            return x + jax.lax.stop_gradient(q - x)

        def bitlinear158(x, w):
            xn = simple_rms_norm(x)
            xq = ste(xn, activation_quant(xn))
            wq = ste(w, weight_quant(w))
            return jnp.einsum('bsi,oi->bso', xq, wq)
        h = jax.nn.gelu(bitlinear158(x, w1), approximate=False)
        h = jax.nn.gelu(h, approximate=False)
        return bitlinear158(h, w2)

    def _L1_xattn_ref(hidden_q, kv_c, Wq, w_kc_q, w_kc_kv, W_qr, W_kr, Wo):
        import jax, jax.numpy as jnp
        import numpy as np
        B, S, L = (2, 128, 128)
        DIM_Q, H, K, D_C, D_CQ, R = (256, 16, 128, 64, 192, 64)

        def _rope_tables(length, dim):
            inv = 1.0 / 10000.0 ** (jnp.arange(0, dim, 2, dtype=jnp.float32) / dim)
            f = jnp.arange(length, dtype=jnp.float32)[:, None] * inv[None, :]
            sin = jnp.repeat(jnp.sin(f), 2, axis=-1)
            cos = jnp.repeat(jnp.cos(f), 2, axis=-1)
            return (sin, cos)

        def _rotate_half(x):
            half = x.shape[-1] // 2
            return jnp.concatenate([-x[..., half:], x[..., :half]], axis=-1)

        def _apply_rope(x, sin, cos):
            return x * cos + _rotate_half(x) * sin
        Bv, Sv, _ = hidden_q.shape
        _, Lv, _ = kv_c.shape
        q_hk = (hidden_q @ Wq.T).reshape(Bv, Sv, H, K)
        q_big = jnp.einsum('bshk,hkq->bshq', q_hk, w_kc_q)
        sin_q, cos_q = _rope_tables(Sv, D_CQ)
        q_big = _apply_rope(q_big, sin_q[None, :, None, :], cos_q[None, :, None, :])
        sin_k, cos_k = _rope_tables(Lv, D_C)
        kv_r = _apply_rope(kv_c, sin_k[None], cos_k[None])
        q_r = jnp.einsum('bshq,hqr->bhsr', q_big, W_qr)
        k_r = jnp.einsum('bld,hdr->bhlr', kv_r, W_kr)
        scores = jnp.einsum('bhsr,bhlr->bhsl', q_r, k_r)
        attn = jax.nn.softmax(scores, axis=-1)
        ctx_c = jnp.einsum('bhsl,bld->bhsd', attn, kv_r)
        ctx_lat = jnp.einsum('bhsd,hkd->bhsk', ctx_c, w_kc_kv)
        ctx = ctx_lat.transpose(0, 2, 1, 3).reshape(Bv, Sv, H * K)
        return ctx @ Wo.T

    def _L1_attn_ref(x, W_kv_down, W_k_nope, W_k_rope, W_v, W_q_down, W_q_nope, W_q_rope, W_o):
        import jax, jax.numpy as jnp
        import numpy as np
        DIM = 256
        H = 16
        HKV = 4
        NREP = H // HKV
        ROPE_D = 64
        NOPE_D = 128
        V_D = 128
        QK_D = ROPE_D + NOPE_D
        KV_RANK = 64
        Q_RANK = 192
        B, T = (2, 256)

        def _rope_cache(seq_len, head_dim, dtype=jnp.float32):
            theta = 1.0 / 10000.0 ** (jnp.arange(0, head_dim, 2, dtype=dtype) / head_dim)
            pos = jnp.arange(seq_len, dtype=dtype)
            ang = jnp.outer(pos, theta)
            ang = jnp.concatenate([ang, ang], axis=-1)
            return (jnp.cos(ang), jnp.sin(ang))

        def _rotate_half(x):
            half = x.shape[-1] // 2
            return jnp.concatenate([-x[..., half:], x[..., :half]], axis=-1)

        def _apply_rope(x, cos, sin):
            return x * cos[None, :, None, :] + _rotate_half(x) * sin[None, :, None, :]
        Bx, Tx, _ = x.shape
        scale = 1.0 / np.sqrt(QK_D)
        kv_c = x @ W_kv_down
        k_nope = (kv_c @ W_k_nope).reshape(Bx, Tx, HKV, NOPE_D)
        k_rope = (kv_c @ W_k_rope).reshape(Bx, Tx, HKV, ROPE_D)
        v = (kv_c @ W_v).reshape(Bx, Tx, HKV, V_D)
        q_c = x @ W_q_down
        q_nope = (q_c @ W_q_nope).reshape(Bx, Tx, H, NOPE_D)
        q_rope = (q_c @ W_q_rope).reshape(Bx, Tx, H, ROPE_D)
        cos, sin = _rope_cache(Tx, ROPE_D, x.dtype)
        q_rope = _apply_rope(q_rope, cos, sin)
        k_rope = _apply_rope(k_rope, cos, sin)
        q = jnp.concatenate([q_nope, q_rope], axis=-1).transpose(0, 2, 1, 3)
        k = jnp.concatenate([k_nope, k_rope], axis=-1).transpose(0, 2, 1, 3)
        vh = v.transpose(0, 2, 1, 3)
        k = jnp.repeat(k, NREP, axis=1)
        vh = jnp.repeat(vh, NREP, axis=1)
        attn = jnp.einsum('bhqd,bhkd->bhqk', q, k) * scale
        causal = jnp.triu(jnp.ones((Tx, Tx), dtype=bool), k=1)
        attn = jnp.where(causal[None, None], -jnp.inf, attn)
        attn = jax.nn.softmax(attn, axis=-1)
        out = jnp.einsum('bhqk,bhkd->bhqd', attn, vh)
        out = out.transpose(0, 2, 1, 3).reshape(Bx, Tx, H * V_D)
        return out @ W_o

    def _L1_ffn_ref(hidden_states, Wg, W1, W2, W3, A1, B1, A2, B2, A3, B3):
        import jax, jax.numpy as jnp
        import numpy as np
        B, S, H, F, E, R, K = (2, 128, 256, 896, 8, 32, 2)

        def _gather_slot(a_all, e):
            return jnp.take_along_axis(a_all, e[:, None, None], axis=1)[:, 0]
        b, s, h = hidden_states.shape
        x = hidden_states.reshape(-1, h)
        nE = Wg.shape[0]
        logits = x @ Wg.T
        probs = jax.nn.softmax(logits.astype(jnp.float32), axis=-1)
        rw, sel = jax.lax.top_k(probs, K)
        rw = (rw / rw.sum(axis=-1, keepdims=True)).astype(x.dtype)
        base1 = x @ W1.T
        base3 = x @ W3.T
        a1_all = jnp.einsum('th,erh->ter', x, A1)
        a3_all = jnp.einsum('th,erh->ter', x, A3)
        out = jnp.zeros_like(x)
        for k in range(K):
            e = sel[:, k]
            mask = jax.nn.one_hot(e, nE, dtype=x.dtype)
            a1 = _gather_slot(a1_all, e)
            a3 = _gather_slot(a3_all, e)
            lora1 = jnp.einsum('ter,efr->tf', mask[:, :, None] * a1[:, None, :], B1)
            lora3 = jnp.einsum('ter,efr->tf', mask[:, :, None] * a3[:, None, :], B3)
            x1 = base1 + lora1
            x3 = base3 + lora3
            x2 = jax.nn.silu(x1) * x3
            down = x2 @ W2.T
            a2_all = jnp.einsum('tf,erf->ter', x2, A2)
            a2 = _gather_slot(a2_all, e)
            lora2 = jnp.einsum('ter,ehr->th', mask[:, :, None] * a2[:, None, :], B2)
            out = out + (down + lora2) * rw[:, k:k + 1]
        return out.reshape(b, s, h)
    x = x + _L0_xattn_ref(_layernorm(x, axis=-1), ctx_512, L0_xattn_Wq, L0_xattn_Wkv_expand, L0_xattn_Wout)
    x = x + _L0_attn_ref(_layernorm(x, axis=-1), L0_attn_W_qkvz, L0_attn_W_ba, L0_attn_conv_w, L0_attn_dt_bias, L0_attn_A_log, L0_attn_norm_w, L0_attn_W_out)
    x = x + _L0_ffn_ref(_layernorm(x, axis=-1), L0_ffn_w1, L0_ffn_w2)
    x = x + _L1_xattn_ref(_layernorm(x, axis=-1), ctx_512, L1_xattn_Wq, L1_xattn_w_kc_q, L1_xattn_w_kc_kv, L1_xattn_W_qr, L1_xattn_W_kr, L1_xattn_Wo)
    x = x + _L1_attn_ref(_layernorm(x, axis=-1), L1_attn_W_kv_down, L1_attn_W_k_nope, L1_attn_W_k_rope, L1_attn_W_v, L1_attn_W_q_down, L1_attn_W_q_nope, L1_attn_W_q_rope, L1_attn_W_o)
    x = x + _L1_ffn_ref(_layernorm(x, axis=-1), L1_ffn_Wg, L1_ffn_W1, L1_ffn_W2, L1_ffn_W3, L1_ffn_A1, L1_ffn_B1, L1_ffn_A2, L1_ffn_B2, L1_ffn_A3, L1_ffn_B3)
    return x

_drawn_inputs = setup_inputs


def setup_inputs(seed=0):
    import zlib

    import numpy as np

    out = dict(_drawn_inputs(seed))
    spreads = {'L0_attn_dt_bias': (1.0, 0.6), 'L0_attn_norm_w': (1.0, 0.6)}
    factors = {'L0_xattn_Wq': 8.0,
     'L0_attn_W_ba': 3.717,
     'L0_attn_A_log': 4.194,
     'L1_attn_W_kv_down': 4.787,
     'L1_attn_W_k_nope': 8.0,
     'L1_attn_W_k_rope': 8.0,
     'L1_attn_W_v': 4.551,
     'L1_attn_W_q_down': 8.0,
     'L1_attn_W_q_nope': 8.0,
     'L1_attn_W_q_rope': 8.0,
     'L1_attn_W_o': 4.663,
     'L1_ffn_Wg': 8.0,
     'L1_ffn_A1': 8.0,
     'L1_ffn_B1': 8.0,
     'L1_ffn_A2': 8.0,
     'L1_ffn_B2': 8.0,
     'L1_ffn_A3': 8.0,
     'L1_ffn_B3': 8.0}
    for name, (base, spread) in spreads.items():
        noise = np.random.default_rng([zlib.crc32(name.encode()), seed]).standard_normal(out[name].shape)
        drawn = base * np.exp(spread * noise) if base else spread * noise
        out[name] = jnp.asarray(drawn.astype(out[name].dtype))
    for name, factor in factors.items():
        out[name] = (out[name] * factor).astype(out[name].dtype)
    return out
```

```python
from contextlib import ExitStack

import concourse.bass as bass
from concourse import mybir

F32 = mybir.dt.float32
BF16 = mybir.dt.bfloat16
U32 = mybir.dt.uint32
ALU = mybir.AluOpType
ACT = mybir.ActivationFunctionType
AX = mybir.AxisListType.X

P = 128
B = 2
D = 256
DC = D // P
TOK = B * P
CTX = 2048
LAT = 64
MASKED = -1e30

A_H, A_HD, A_PAD = 16, 16, 32
G_QK, G_V, G_HD, TAPS = 16, 32, 128, 4
RATIO = G_V // G_QK
PAIRS = G_QK // 2
LEVELS = 7
SLAB = DC * 4 * P + 4 * TAPS
C_IN = 1024
ROUND = 12582912.0
X_H, X_K, X_CQ, X_R = 16, 128, 192, 64
XQ = X_CQ // 2
KT = CTX // P
E_H, E_KV, E_REP, E_NOPE, E_ROPE, E_V = 16, 4, 4, 128, 64, 128
E_QR = 192
M_F, M_E, M_R, M_K = 896, 8, 32, 2
FCH = M_F // P

C_ID = 0
C_UP = 128
C_LOW = 256
C_CAUSAL = 384
C_LV = 512
C_LVT = C_LV + LEVELS * P
C_CQ = C_LVT + LEVELS * P
C_SQ = C_CQ + 2 * TOK
C_CE = C_SQ + 2 * TOK
C_SE = C_CE + TOK
C_IOTA = C_SE + TOK
C_ALL = C_IOTA + M_E
BIG = 1024.0


class Chain:

    def __init__(self, eng, sem):
        self.eng, self.sem, self.n, self.at, self.per = eng, sem, 0, None, 0

    def __call__(self, ins):
        ins.then_inc(self.sem, 1)
        self.n += 1
        self.eng.wait_ge(self.sem, self.n if self.at is None else self.at * self.per + self.n)

    def enter(self, i, first, per):
        self.at, self.per, self.start = i, per, self.n
        self.n -= first * per
        self.shift = first * per

    def leave(self, turns):
        used = self.n + self.shift - self.start
        assert used == self.per, used
        self.n, self.at = self.start + self.per * turns, None


def build(nc, a, upto=6):
    ctx = ExitStack()

    def sem(name):
        return ctx.enter_context(nc.semaphore(name))

    def sb(name, shape, dt=F32):
        return ctx.enter_context(nc.sbuf_tensor(name, shape, dt))

    with ctx:
        bk = [ctx.enter_context(nc.psum_tensor(f"bank{i}", [P, 512], F32))[:] for i in range(4)]
        scores = ctx.enter_context(nc.psum_tensor("scores", [P, 4, 512], F32))
        bk += [scores[:, i, :] for i in range(4)]
        X = sb("X", [P, B, D])
        cst = sb("cst", [P, C_ALL])
        xn = sb("xn", [P, B, D])
        xnT = sb("xnT", [P, DC, TOK])
        stats = sb("stats", [P, B, 6])
        mv = sb("mv", [P, B, 2])
        veps = sb("veps", [P, B])
        rstd = sb("rstd", [P, B])
        mhalf = sb("mhalf", [P, 8])
        ones = sb("ones", [P, P])
        ident = cst[:, C_ID:C_ID + P]

        env = dict(locals())
        s = dict(
            x_in=sem("x_in"), cst_in=sem("cst_in"), ones_set=sem("ones_set"),
            ln_var=sem("ln_var"), ln_rstd=sem("ln_rstd"), ln_xn=sem("ln_xn"),
            ln_tr=sem("ln_tr"), ln_xT=sem("ln_xT"), dve_chain=sem("dve_chain"), act_chain=sem("act_chain"), pool_chain=sem("pool_chain"),
            out_done=sem("out_done"),
        )
        env["s"] = s
        env["dve_link"] = Chain(nc.vector, s["dve_chain"])
        env["act_link"] = Chain(nc.scalar, s["act_chain"])
        env["pool_link"] = Chain(nc.gpsimd, s["pool_chain"])

        def turned(n):
            return n + 1 - (n > 2)

        def ln_vector(n):
            link = env["dve_link"]
            for b in range(B):
                link(nc.vector.bn_stats(stats[:, b, :], X[:, b, :]))
            for b in range(B):
                link(nc.vector.bn_aggr(mv[:, b, :], stats[:, b, :]))
            nc.vector.tensor_scalar(veps[:], mv[:, :, 1], 1e-5, None, ALU.add).then_inc(s["ln_var"], 1)
            nc.vector.wait_ge(s["ln_rstd"], n + 1)
            for b in range(B):
                nc.vector.tensor_scalar(xn[:, b, :], X[:, b, :], mv[:, b, 0:1], rstd[:, b:b + 1],
                                        ALU.subtract, ALU.mult).then_inc(s["ln_xn"], 1)

        def ln_gpsimd(n):
            nc.gpsimd.wait_ge(s["ln_var"], n + 1)
            nc.gpsimd.tensor_tensor(rstd[:], veps[:], mhalf[:, 0:B], ALU.pow).then_inc(s["ln_rstd"], 1)

        def ln_tensor(n):
            nc.tensor.wait_ge(s["ln_xn"], B * (n + 1))
            for c in range(DC):
                for b in range(B):
                    last = nc.tensor.transpose(bk[7][:, c * TOK + b * P:c * TOK + (b + 1) * P],
                                               xn[:, b, c * P:(c + 1) * P], ident)
            last.then_inc(s["ln_tr"], 1)

        def ln_scalar(n):
            nc.scalar.wait_ge(s["ln_tr"], turned(n))
            nc.scalar.copy(xnT[:].rearrange("p c t -> p (c t)"), bk[7]).then_inc(s["ln_xT"], 1)

        env.update(ln_vector=ln_vector, ln_gpsimd=ln_gpsimd, ln_tensor=ln_tensor, ln_scalar=ln_scalar, turned=turned)

        with nc.Block() as block:
            @block.sync
            def _(sp):
                sp.dma_start(X[:], a["x"].rearrange("b t d -> t b d")).then_inc(s["x_in"], 16)
                sp.dma_start(cst[:], a["cst"]).then_inc(s["cst_in"], 16)
                sp.wait_ge(s["x_in"], 16)
                sp.wait_ge(s["cst_in"], 16)

            @block.vector
            def _(dve):
                dve.memset(ones[:], 1.0)
                dve.memset(mhalf[:], -0.5)

        stages = [stage_a, stage_b, stage_c, stage_d, stage_e, stage_f][:upto]
        for st in stages:
            with ExitStack() as own:
                env["used"] = []
                st(nc, a, env, own)
                with nc.Block() as block:
                    @block.vector
                    def _(dve):
                        for used in env["used"]:
                            dve.sem_clear(used)

        with nc.Block() as block:
            @block.sync
            def _(sp):
                sp.dma_start(a["out"].rearrange("b t d -> t b d"), X[:]).then_inc(s["out_done"], 16)
                sp.wait_ge(s["out_done"], 16)


def stage_a(nc, a, env, own):
    X, xnT, bk, ident, cst, s = (env[k] for k in ("X", "xnT", "bk", "ident", "cst", "s"))
    link = env["dve_link"]

    def sb(name, shape, dt=F32):
        return own.enter_context(nc.sbuf_tensor("a_" + name, shape, dt))

    def sem(name):
        env["used"].append(own.enter_context(nc.semaphore("a_" + name)))
        return env["used"][-1]

    HG = A_H // 4
    ctxT = sb("ctxT", [LAT, B, P])
    wq = sb("wq", [P, DC, D])
    wkv = sb("wkv", [LAT, 2 * D])
    wo = sb("wo", [P, DC, D])
    wq_pad = sb("wq_pad", [P, DC, A_H, A_PAD])
    wk_pad = sb("wk_pad", [LAT, A_H, A_PAD])
    qT = sb("qT", [P, HG, TOK])
    kT = sb("kT", [P, HG, TOK])
    v = sb("v", [P, B, D])
    S = sb("S", [P, B, 4, 4, P])
    nmax = sb("nmax", [P, B, 4, 4])
    sums = sb("sums", [P, B, 4, 4])
    rec = sb("rec", [P, B, 4, 4])
    PT = sb("PT", [P, B, 4, 4, P])
    o = sb("o", [P, B, D])
    oT = sb("oT", [P, DC, TOK])
    loads, padded, kq_mm, kq_cp, v_mm, v_cp = (sem(n) for n in "loads padded kq_mm kq_cp v_mm v_cp".split())
    sc_mm, sc_masked, nmax_done, exp_done, tr_mm, tr_cp = (sem(n) for n in "sc_mm sc_masked nmax_done exp_done tr_mm tr_cp".split())
    rec_done, pv_mm, o_cp, ot_mm, ot_cp, y_mm = (sem(n) for n in "rec_done pv_mm o_cp ot_mm ot_cp y_mm".split())

    with nc.Block() as block:
        @block.sync
        def _(sp):
            for t, d in ((ctxT, "a_ctxT"), (wq, "a_wq"), (wkv, "a_wkv"), (wo, "a_wo")):
                sp.dma_start(t[:], a[d]).then_inc(loads, 16)

        @block.gpsimd
        def _(pool):
            pool.memset(wq_pad[:], 0.0).then_inc(padded, 1)
            pool.memset(wk_pad[:], 0.0).then_inc(padded, 1)
            env["ln_gpsimd"](0)
            pool.wait_ge(padded, 2)
            pool.wait_ge(loads, 64)
            pool.tensor_copy(wk_pad[:, :, 0:A_HD], wkv[:, 0:D].rearrange("p (h e) -> p h e", h=A_H)).then_inc(padded, 1)
            for c in range(DC):
                pool.tensor_copy(wq_pad[:, c, :, 0:A_HD],
                                 wq[:, c, :].rearrange("p (h e) -> p h e", h=A_H)).then_inc(padded, 1)

        @block.tensor
        def _(pe):
            env["ln_tensor"](0)
            pe.wait_ge(loads, 64)
            for b in range(B):
                last = pe.matmul(bk[0][:, b * D:(b + 1) * D], ctxT[:, b, :], wkv[:, D:2 * D], start=True, stop=True)
            last.then_inc(v_mm, 1)
            pe.wait_ge(padded, 5)
            for m in range(HG):
                last = pe.matmul(bk[1 + m // 2][:, (m % 2) * TOK:(m % 2 + 1) * TOK],
                                 wk_pad[:, 4 * m:4 * m + 4, :].rearrange("p h e -> p (h e)"),
                                 ctxT[:].rearrange("p b t -> p (b t)"), start=True, stop=True)
                if m % 2:
                    last.then_inc(kq_mm, 1)
            pe.wait_ge(s["ln_xT"], env["turned"](0))
            for m in range(HG):
                for c in range(DC):
                    last = pe.matmul(bk[3 + m // 2][:, (m % 2) * TOK:(m % 2 + 1) * TOK],
                                     wq_pad[:, c, 4 * m:4 * m + 4, :].rearrange("p h e -> p (h e)"),
                                     xnT[:, c, :], start=(c == 0), stop=(c == DC - 1))
                if m % 2:
                    last.then_inc(kq_mm, 1)
            pe.wait_ge(kq_cp, 4)
            pe.wait_ge(v_cp, 1)
            for b in range(B):
                for j in range(4):
                    rows = slice(32 * j, 32 * j + 32)
                    for m in range(HG):
                        last = pe.matmul(bk[4 * b + j][:, m * P:(m + 1) * P], qT[rows, m, b * P:(b + 1) * P],
                                         kT[rows, m, b * P:(b + 1) * P], start=True, stop=True)
                    last.then_inc(sc_mm, 1)
            for b in range(B):
                for j in range(4):
                    n = 4 * b + j
                    pe.wait_ge(exp_done, n + 1)
                    for m in range(HG):
                        last = pe.transpose(bk[n][:, m * P:(m + 1) * P], S[:, b, j, m, :], ident)
                    last.then_inc(tr_mm, 1)
            for b in range(B):
                pe.wait_ge(tr_cp, 4 * b + 4)
                for h in range(A_H):
                    j, m = h % 4, h // 4
                    last = pe.matmul(bk[4 * b][:, h * A_HD:(h + 1) * A_HD], PT[:, b, j, m, :],
                                     v[:, b, h * A_HD:(h + 1) * A_HD], start=True, stop=True)
                last.then_inc(pv_mm, 1)
            pe.wait_ge(o_cp, 2)
            for c in range(DC):
                for b in range(B):
                    last = pe.transpose(bk[1][:, c * TOK + b * P:c * TOK + (b + 1) * P], o[:, b, c * P:(c + 1) * P], ident)
            last.then_inc(ot_mm, 1)
            pe.wait_ge(ot_cp, 1)
            for b in range(B):
                for c in range(DC):
                    last = pe.matmul(bk[2][:, b * D:(b + 1) * D], oT[:, c, b * P:(b + 1) * P], wo[:, c, :],
                                     start=(c == 0), stop=(c == DC - 1))
            last.then_inc(y_mm, 1)

        @block.scalar
        def _(act):
            env["ln_scalar"](0)
            for n in range(4):
                act.wait_ge(kq_mm, n + 1)
                dst = (kT if n < 2 else qT)[:, 2 * (n % 2):2 * (n % 2) + 2, :].rearrange("p m t -> p (m t)")
                act.copy(dst, bk[1 + n]).then_inc(kq_cp, 1)
            for b in range(B):
                for j in range(4):
                    act.wait_ge(nmax_done, 4 * b + j + 1)
                    for m in range(HG):
                        last = act.activation(S[:, b, j, m, :], S[:, b, j, m, :], ACT.Exp,
                                              bias=nmax[:, b, j, m:m + 1], accum_out=sums[:, b, j, m:m + 1])
                    last.then_inc(exp_done, 1)
            act.wait_ge(ot_mm, 1)
            act.copy(oT[:].rearrange("p c t -> p (c t)"), bk[1]).then_inc(ot_cp, 1)

        @block.vector
        def _(dve):
            env["ln_vector"](0)
            dve.wait_ge(v_mm, 1)
            dve.tensor_copy(v[:].rearrange("p b d -> p (b d)"), bk[0]).then_inc(v_cp, 1)
            causal = cst[:, C_CAUSAL:C_CAUSAL + P].unsqueeze(1).to_broadcast([P, 4, P])
            for b in range(B):
                for j in range(4):
                    n = 4 * b + j
                    dve.wait_ge(sc_mm, n + 1)
                    dve.scalar_tensor_tensor(S[:, b, j], bk[n].rearrange("p (m k) -> p m k", m=4), A_HD ** -0.5, causal,
                                             ALU.mult, ALU.add).then_inc(sc_masked, 1)
                    dve.wait_ge(sc_masked, n + 1)
                    dve.tensor_reduce(nmax[:, b, j, :], S[:, b, j], AX, ALU.max, negate=True).then_inc(nmax_done, 1)
            for b in range(B):
                for j in range(4):
                    n = 4 * b + j
                    dve.wait_ge(tr_mm, n + 1)
                    dve.tensor_copy(PT[:, b, j].rearrange("p m q -> p (m q)"), bk[n]).then_inc(tr_cp, 1)
                dve.reciprocal(rec[:, b], sums[:, b]).then_inc(rec_done, 1)
                dve.wait_ge(rec_done, b + 1)
                dve.wait_ge(pv_mm, b + 1)
                dve.tensor_tensor(o[:, b, :].rearrange("p (m j e) -> p m j e", m=4, j=4),
                                  bk[4 * b][:, 0:D].rearrange("p (m j e) -> p m j e", m=4, j=4),
                                  rec[:, b].rearrange("p j m -> p m j").unsqueeze(3).to_broadcast([P, 4, 4, A_HD]),
                                  ALU.mult).then_inc(o_cp, 1)
            dve.wait_ge(y_mm, 1)
            link(dve.tensor_tensor(X[:].rearrange("p b d -> p (b d)"), X[:].rearrange("p b d -> p (b d)"), bk[2], ALU.add))


def stage_b(nc, a, env, own):
    X, xnT, bk, ident, cst, s, mhalf, ones = (env[k] for k in ("X", "xnT", "bk", "ident", "cst", "s", "mhalf", "ones"))
    vlink, plink, alink = env["dve_link"], env["pool_link"], env["act_link"]
    INV = G_HD ** -0.5
    EPS = 1e-6
    HB = 2 * G_V
    LAST = LEVELS - 1

    def sb(name, shape, dt=F32):
        return own.enter_context(nc.sbuf_tensor("b_" + name, shape, dt))

    def two(name, shape):
        return [sb(f"{name}{x}", shape) for x in range(2)]

    def sem(name):
        env["used"].append(own.enter_context(nc.semaphore("b_" + name)))
        return env["used"][-1]

    slab, wz, wo = two("slab", [P, SLAB]), two("wz", [P, DC, 2 * P]), two("wo", [P, RATIO, D])
    wba = sb("wba", [P, DC, HB])
    dtb, alog, normw = sb("dtb", [P, G_V]), sb("alog", [P, G_V]), sb("normw", [P, 1])
    DT = sb("DT", [P, G_QK, 4 * P])
    beta = sb("beta", [P, G_QK, B, RATIO])
    gl = sb("gl", [P, G_QK, B, RATIO])
    t1, t2, t3 = sb("t1", [P, B, G_V]), sb("t2", [P, B, G_V]), sb("t3", [P, B, G_V])
    Gm = two("Gm", [P, 4, P])
    cpad = two("cpad", [P, 4, B, TAPS - 1 + P])
    yc, qkv = two("yc", [P, 4, B, P]), two("qkv", [P, 4, B, P])
    sq = two("sq", [P, 2, B, P])
    Np, At, T, TT, Ys = two("Np", [P, 4, P]), two("At", [P, 4, P]), two("T", [P, 4, P]), two("TT", [P, 4, P]), two("Ys", [P, 4, P])
    Vh, vn, sz, hs = two("Vh", [P, 4, P]), two("vn", [P, 4, P]), two("sz", [P, 4, P]), two("hs", [P, 4, P])
    hT = two("hT", [P, 4, P])
    I4 = sb("I4", [P, 4, P])
    carrier = sb("carrier", [P, 2 * 2 * LEVELS])
    m8, r8 = sb("m8", [P, 2, 2, B]), sb("r8", [P, 2, 2, B])
    r2, vi = sb("r2", [P, 2, B]), sb("vi", [P, 2, B])
    rqs, rq2 = sb("rqs", [P, 2, B]), sb("rq2", [P, 2, B])
    nb = sb("nb", [P, 2, B, RATIO])
    so, hv, hr, hsc = two("so", [P, 4]), two("hv", [P, 4]), two("hr", [P, 4]), two("hsc", [P, 4])

    w_in, small_in = sem("w_in"), sem("small_in")
    slab_in, wz_in, wo_in = [sem(f"slab_in{x}") for x in range(2)], [sem(f"wz_in{x}") for x in range(2)], [sem(f"wo_in{x}") for x in range(2)]
    (i4_set, ba_mm, ba_act, ba_dve, gl_done, gm_done, dec_mm, dec_exp, dec_done, proj_mm, pads_set, pads_cp, conv_step,
     silu_done, sq_done, kk_mm, vt_mm, z_mm, ssq_mm, sz_done, vh_done, norm_var, norm_pow, norm_done, np_done, at_done,
     mt_mm, t_reset, t_upd, tt_upd, y_mm, y_cp, zz_mm, zt_mm, tv_mm, vn_done, o_mm, so_done, h_var, h_pow, h_done,
     ht_mm, ht_cp, yp_mm, x_acc) = (sem(n) for n in (
        "i4_set ba_mm ba_act ba_dve gl_done gm_done dec_mm dec_exp dec_done proj_mm pads_set pads_cp conv_step "
        "silu_done sq_done kk_mm vt_mm z_mm ssq_mm sz_done vh_done norm_var norm_pow norm_done np_done at_done "
        "mt_mm t_reset t_upd tt_upd y_mm y_cp zz_mm zt_mm tv_mm vn_done o_mm so_done h_var h_pow h_done "
        "ht_mm ht_cp yp_mm x_acc").split())

    PJ, PZ, PY, YZ, ZT = [bk[0], bk[1]], bk[2], bk[3], [bk[4], bk[6]], [bk[5], bk[7]]
    UP4 = cst[:, C_UP:C_UP + P].unsqueeze(1).to_broadcast([P, 4, P])

    def quad(ap):
        return ap.rearrange("p (u k) -> p u k", u=4)

    def mask(base, level):
        m = cst[:, base + level * P:base + (level + 1) * P].bitcast(U32)
        return m.unsqueeze(1).to_broadcast([P, 4, P])

    def loop(eng, body):
        body(0, True)
        with eng.Fori(1, PAIRS - 1) as i:
            body(i, True)
        body(PAIRS - 1, False)

    with nc.Block() as block:
        @block.sync
        def _(sp):
            sp.dma_start(wba[:], a["b_wba"]).then_inc(w_in, 16)
            sp.dma_start(dtb[:], a["b_dt"].to_broadcast([P, G_V])).then_inc(small_in, 16)
            sp.dma_start(alog[:], a["b_alog"].to_broadcast([P, G_V])).then_inc(small_in, 16)
            sp.dma_start(normw[:], a["b_norm"]).then_inc(small_in, 16)
            for x in range(2):
                sp.dma_start(slab[x][:], a["b_slab"][x]).then_inc(slab_in[x], 16)
                sp.dma_start(wz[x][:].rearrange("p c n -> p (c n)"), a["b_wz"][x]).then_inc(wz_in[x], 16)
                sp.dma_start(wo[x][:].rearrange("p r n -> p (r n)"), a["b_wo"][x]).then_inc(wo_in[x], 16)

            with sp.Fori(0, PAIRS - 1) as i:
                for x in range(2):
                    sp.wait_ge(conv_step, 32 * i + 16 * x + 16)
                    sp.dma_start(slab[x][:], a["b_slab"][bass.ds(2 * i + 2 + x, 1)].rearrange("g p n -> (g p) n")).then_inc(slab_in[x], 16)
                for x in range(2):
                    sp.wait_ge(z_mm, 2 * i + x + 1)
                    sp.dma_start(wz[x][:].rearrange("p c n -> p (c n)"),
                                 a["b_wz"][bass.ds(2 * i + 2 + x, 1)].rearrange("g p n -> (g p) n")).then_inc(wz_in[x], 16)
                for x in range(2):
                    sp.wait_ge(yp_mm, i + 1)
                    sp.dma_start(wo[x][:].rearrange("p r n -> p (r n)"),
                                 a["b_wo"][bass.ds(2 * i + 2 + x, 1)].rearrange("g p n -> (g p) n")).then_inc(wo_in[x], 16)

        @block.gpsimd
        def _(pool):
            for x in range(2):
                pool.memset(cpad[x][:], 0.0).then_inc(pads_set, 1)
            pool.wait_ge(s["cst_in"], 16)
            for u in range(4):
                pool.tensor_copy(I4[:, u, :], ident).then_inc(i4_set, 1)
            env["ln_gpsimd"](1)
            pool.wait_ge(i4_set, 4)
            for x in range(2):
                pool.tensor_copy(T[x][:], I4[:])
                pool.tensor_copy(TT[x][:], I4[:]).then_inc(t_reset, 1)

            def body(i, more):
                pool.wait_ge(norm_var, i + 1)
                pool.tensor_tensor(r8[:].rearrange("p x q b -> p (x q b)"), m8[:].rearrange("p x q b -> p (x q b)"),
                                   mhalf[:, 0:8], ALU.pow).then_inc(norm_pow, 1)
                for x in range(2):
                    pool.wait_ge(h_var, 2 * i + x + 1)
                    pool.tensor_tensor(hr[x][:], hv[x][:], mhalf[:, 0:4], ALU.pow).then_inc(h_pow, 1)
                    if more:
                        turn = pool.snap(2 * i + x + 1)
                        pool.wait_ge(i4_set, 4)
                        pool.wait_ge(tv_mm, turn)
                        pool.tensor_copy(T[x][:], I4[:])
                        pool.tensor_copy(TT[x][:], I4[:]).then_inc(t_reset, 1)

            loop(pool, body)

        @block.tensor
        def _(pe):
            env["ln_tensor"](1)
            pe.wait_ge(w_in, 16)
            pe.wait_ge(s["ln_xT"], env["turned"](1))
            for b in range(B):
                for c in range(DC):
                    last = pe.matmul(bk[0][:, b * HB:(b + 1) * HB], xnT[:, c, b * P:(b + 1) * P], wba[:, c, :],
                                     start=(c == 0), stop=(c == DC - 1))
            last.then_inc(ba_mm, 1)
            def decays(i, x):
                pe.wait_ge(gm_done, 2 * i + x + 1)
                if not isinstance(i, int):
                    pe.wait_ge(dec_exp, 2 * i)
                pe.matmul(bk[4 + x], cst[:, C_LOW:C_LOW + P], Gm[x][:].rearrange("p u k -> p (u k)"),
                          start=True, stop=True).then_inc(dec_mm, 1)

            for x in range(2):
                decays(0, x)
            with pe.Fori(1, PAIRS) as i:
                for x in range(2):
                    decays(i, x)

            def project(i, x):
                pe.wait_ge(slab_in[x], 16 * i + 16)
                if x or not isinstance(i, int) or i > 0:
                    pe.wait_ge(pads_cp, 2 * i + x)
                for ch in range(4):
                    for c in range(DC):
                        last = pe.matmul(PJ[ch // 2][:, ch % 2 * TOK:(ch % 2 + 1) * TOK],
                                         slab[x][:, (c * 4 + ch) * P:(c * 4 + ch + 1) * P], xnT[:, c, :],
                                         start=(c == 0), stop=(c == DC - 1))
                last.then_inc(proj_mm, 1)

            pe.wait_ge(ba_dve, 1)
            project(0, 0)
            project(0, 1)

            def body(i, more):
                again = not isinstance(i, int) or i > 0
                pe.wait_ge(sq_done, 2 * i + 2)
                if again:
                    pe.wait_ge(x_acc, i)
                for x in range(2):
                    for q in range(2):
                        for b in range(B):
                            col = x * 4 + q * 2 + b
                            last = pe.matmul(PY[:, col:col + 1], sq[x][:, q, b, :], ones[:, 0:1], start=True, stop=True)
                last.then_inc(ssq_mm, 1)
                for x in range(2):
                    for b in range(B):
                        last = pe.matmul(PJ[x][:, b * 2 * P:(b + 1) * 2 * P].rearrange("p (q k) -> p q k", q=2),
                                         qkv[x][:, 1, b, :], qkv[x][:, 0:2, b, :], start=True, stop=True)
                    last.then_inc(kk_mm, 1)
                    if x == 0 and again:
                        pe.wait_ge(h_done, 2 * i)
                    for b in range(B):
                        for r in range(RATIO):
                            u = b * RATIO + r
                            last = pe.transpose(ZT[x][:, u * P:(u + 1) * P], qkv[x][:, 2 + r, b, :], ident)
                    last.then_inc(vt_mm, 1)
                for x in range(2):
                    pe.wait_ge(wz_in[x], 16 * i + 16)
                    if x or again:
                        pe.wait_ge(sz_done, 2 * i + x)
                    for b in range(B):
                        for c in range(DC):
                            last = pe.matmul(PZ[:, b * 2 * P:(b + 1) * 2 * P], xnT[:, c, b * P:(b + 1) * P], wz[x][:, c, :],
                                             start=(c == 0), stop=(c == DC - 1))
                    last.then_inc(z_mm, 1)
                if again:
                    pe.wait_ge(ht_cp, 2 * i)
                for x in range(2):
                    pe.wait_ge(np_done, 2 * i + x + 1)
                    for u in range(4):
                        last = pe.transpose(YZ[x][:, u * P:(u + 1) * P], Np[x][:, u, :], ident)
                    last.then_inc(mt_mm, 1)
                for lv in range(1, LEVELS):
                    for x in range(2):
                        pe.wait_ge(t_upd, 12 * i + 2 * (lv - 1) + x + 1)
                        for u in range(4):
                            last = pe.matmul(YZ[x][:, u * P:(u + 1) * P], Np[x][:, u, :], T[x][:, u, :], start=True, stop=True)
                        last.then_inc(y_mm, 1)
                    if more and lv in (2, 3):
                        if lv == 2:
                            pe.wait_ge(at_done, 2 * i + 2)
                        project(i + 1, lv - 2)
                    for x in range(2):
                        pe.wait_ge(y_cp, 12 * i + 2 * (lv - 1) + x + 1)
                        pe.wait_ge(tt_upd, 14 * i + 2 * (lv - 1) + x + 1)
                        if lv == 1:
                            pe.wait_ge(vh_done, 2 * i + x + 1)
                        if lv < LAST:
                            for u in range(4):
                                last = pe.matmul(YZ[x][:, u * P:(u + 1) * P], TT[x][:, u, :], Ys[x][:, u, :], start=True, stop=True)
                            last.then_inc(zz_mm, 1)
                        for u in range(4):
                            last = pe.matmul(ZT[x][:, u * P:(u + 1) * P], Ys[x][:, u, :], TT[x][:, u, :], start=True, stop=True)
                        last.then_inc(zt_mm, 1)
                for x in range(2):
                    pe.wait_ge(tt_upd, 14 * i + 2 * LAST + x + 1)
                    for u in range(4):
                        last = pe.matmul(YZ[x][:, u * P:(u + 1) * P], TT[x][:, u, :], Vh[x][:, u, :], start=True, stop=True)
                    last.then_inc(tv_mm, 1)
                for x in range(2):
                    pe.wait_ge(vn_done, 2 * i + x + 1)
                    for u in range(4):
                        last = pe.matmul(ZT[x][:, u * P:(u + 1) * P], At[x][:, u, :], vn[x][:, u, :], start=True, stop=True)
                    last.then_inc(o_mm, 1)
                for x in range(2):
                    pe.wait_ge(h_done, 2 * i + x + 1)
                    for u in range(4):
                        last = pe.transpose(YZ[x][:, u * P:(u + 1) * P], hs[x][:, u, :], ident)
                    last.then_inc(ht_mm, 1)
                pe.wait_ge(ht_cp, 2 * i + 2)
                for x in range(2):
                    pe.wait_ge(wo_in[x], 16 * i + 16)
                for b in range(B):
                    for x in range(2):
                        for r in range(RATIO):
                            last = pe.matmul(PY[:, b * D:(b + 1) * D], hT[x][:, b * RATIO + r, :], wo[x][:, r, :],
                                             start=(x + r == 0), stop=(x + r == 2))
                last.then_inc(yp_mm, 1)

            loop(pe, body)

        @block.scalar
        def _(act):
            env["ln_scalar"](1)
            act.wait_ge(small_in, 48)
            act.activation(alog[:], alog[:], ACT.Exp).then_inc(ba_act, 1)
            act.wait_ge(ba_mm, 1)
            act.activation(t1[:], bk[0][:, 0:B * HB].rearrange("p (b n) -> p b n", b=B)[:, :, 0:G_V], ACT.Exp, scale=-1.0).then_inc(ba_act, 1)
            act.wait_ge(ba_dve, 1)
            alink(act.activation(t3[:], t2[:], ACT.Abs))
            alink(act.activation(t3[:], t3[:], ACT.Exp, scale=-1.0))
            act.activation(t3[:], t3[:], ACT.Ln, bias=1.0).then_inc(ba_act, 1)
            with act.Fori(0, PAIRS) as i:
                for x in range(2):
                    act.wait_ge(dec_mm, 2 * i + x + 1)
                    act.activation(DT[:, bass.ds(2 * i + x, 1), :].rearrange("p g k -> p (g k)"), bk[4 + x], ACT.Exp).then_inc(dec_exp, 1)

            def pads(i, x):
                act.wait_ge(proj_mm, 2 * i + x + 1)
                for k in range(2):
                    last = act.copy(cpad[x][:, 2 * k:2 * k + 2, :, TAPS - 1:].rearrange("p c b t -> p (c b) t"),
                                    PJ[k].rearrange("p (c t) -> p c t", t=P))
                last.then_inc(pads_cp, 1)

            def silu(i, x):
                act.wait_ge(conv_step, 32 * i + 16 * x + 16)
                act.activation(qkv[x][:].rearrange("p c b t -> p (c b t)"), yc[x][:].rearrange("p c b t -> p (c b t)"),
                               ACT.Silu).then_inc(silu_done, 1)
                act.wait_ge(silu_done, 2 * i + x + 1)
                act.activation(sq[x][:].rearrange("p c b t -> p (c b t)"), qkv[x][:, 0:2].rearrange("p c b t -> p (c b t)"),
                               ACT.Square).then_inc(sq_done, 1)

            act.wait_ge(pads_set, 2)
            pads(0, 0)
            pads(0, 1)
            silu(0, 0)
            silu(0, 1)

            def body(i, more):
                for x in range(2):
                    act.wait_ge(z_mm, 2 * i + x + 1)
                    act.activation(sz[x][:].rearrange("p u k -> p (u k)"), PZ, ACT.Silu).then_inc(sz_done, 1)
                act.wait_ge(norm_done, i + 1)
                for x in range(2):
                    act.wait_ge(vt_mm, 2 * i + x + 1)
                    for b in range(B):
                        last = act.activation(Vh[x][:, b * RATIO:(b + 1) * RATIO, :],
                                              quad(ZT[x])[:, b * RATIO:(b + 1) * RATIO, :], ACT.Copy, scale=vi[:, x, b:b + 1])
                    last.then_inc(vh_done, 1)
                for lv in range(1, LEVELS):
                    for x in range(2):
                        act.wait_ge(y_mm, 12 * i + 2 * (lv - 1) + x + 1)
                        act.copy(Ys[x][:], quad(YZ[x])).then_inc(y_cp, 1)
                    if more and lv in (2, 3):
                        pads(i + 1, lv - 2)
                    if more and lv in (4, 6):
                        silu(i + 1, lv // 2 - 2)
                for x in range(2):
                    act.wait_ge(o_mm, 2 * i + x + 1)
                    for u in range(4):
                        last = act.activation(Ys[x][:, u, :], quad(ZT[x])[:, u, :], ACT.Square, accum_out=so[x][:, u:u + 1])
                    last.then_inc(so_done, 1)
                for x in range(2):
                    act.wait_ge(ht_mm, 2 * i + x + 1)
                    act.activation(hT[x][:], quad(YZ[x]), ACT.Copy, scale=normw[:, 0:1]).then_inc(ht_cp, 1)

            loop(act, body)

        @block.vector
        def _(dve):
            env["ln_vector"](1)
            dve.wait_ge(ba_act, 1)
            vlink(dve.tensor_scalar(alog[:], alog[:], -1.0, None, ALU.mult))
            dve.wait_ge(ba_act, 2)
            ba = bk[0][:, 0:B * HB].rearrange("p (b n) -> p b n", b=B)
            dve.tensor_tensor(t2[:], ba[:, :, G_V:HB], dtb[:].unsqueeze(1).to_broadcast([P, B, G_V]), ALU.add).then_inc(ba_dve, 1)
            vlink(dve.tensor_scalar(t1[:], t1[:], 1.0, None, ALU.add))
            vlink(dve.reciprocal(t1[:], t1[:]))
            for b in range(B):
                vlink(dve.tensor_scalar(beta[:, :, b, :], t1[:, b, :].rearrange("p (g r) -> p g r", r=RATIO), -INV * INV, None, ALU.mult))
            dve.wait_ge(ba_act, 3)
            vlink(dve.scalar_tensor_tensor(t3[:], t2[:], 0.0, t3[:], ALU.max, ALU.add))
            for b in range(B):
                dve.tensor_tensor(gl[:, :, b, :], t3[:, b, :].rearrange("p (g r) -> p g r", r=RATIO),
                                  alog[:].rearrange("p (g r) -> p g r", r=RATIO), ALU.mult).then_inc(gl_done, 1)
            dve.wait_ge(gl_done, 2)
            flat = gl[:].rearrange("p g b r -> p (g b r)")

            def decays(i):
                for x in range(2):
                    if not isinstance(i, int):
                        dve.wait_ge(dec_mm, 2 * i)
                    dve.tensor_tensor(Gm[x][:], UP4, flat[:, bass.ds(8 * i + 4 * x, 4)].unsqueeze(2).to_broadcast([P, 4, P]),
                                      ALU.mult).then_inc(gm_done, 1)
                for x in range(2):
                    dve.wait_ge(dec_exp, 2 * i + x + 1)
                    t = DT[:, bass.ds(2 * i + x, 1), :].rearrange("p g (u k) -> p (g u) k", u=4)
                    dve.tensor_tensor(t, t, UP4, ALU.mult).then_inc(dec_done, 1)

            decays(0)
            with dve.Fori(1, PAIRS) as i:
                decays(i)
            dve.wait_ge(dec_done, 2 * PAIRS)

            def conv(i, x, taps=range(TAPS)):
                if 0 in taps:
                    dve.wait_ge(pads_cp, 2 * i + x + 1)
                for n in taps:
                    for ch in range(4):
                        w = slab[x][:, DC * 4 * P + ch * TAPS + n:DC * 4 * P + ch * TAPS + n + 1]
                        src = cpad[x][:, ch, :, n:n + P]
                        if n == 0:
                            last = dve.tensor_scalar(yc[x][:, ch], src, w, None, ALU.mult)
                        else:
                            dve.wait_ge(conv_step, 32 * i + 16 * x + 4 * n + ch - 3)
                            last = dve.scalar_tensor_tensor(yc[x][:, ch], src, w, yc[x][:, ch], ALU.mult, ALU.add)
                        last.then_inc(conv_step, 1)

            conv(0, 0)
            conv(0, 1)

            def wait_masks(signal, count, cell):
                dve.wait_ge(signal, count)
                dve.memset(carrier[:, cell:cell + 1], 0.0)

            def body(i, more):
                dve.wait_ge(ssq_mm, i + 1)
                dve.tensor_scalar(m8[:].rearrange("p x q b -> p (x q b)"), PY[:, 0:8], 1.0 / G_HD, EPS, ALU.mult, ALU.add).then_inc(norm_var, 1)
                dve.wait_ge(norm_pow, i + 1)
                vlink(dve.tensor_tensor(r2[:], r8[:, :, 1, :], r8[:, :, 1, :], ALU.mult))
                vlink(dve.tensor_tensor(nb[:].rearrange("p x b r -> p (x b) r"), beta[:, bass.ds(2 * i, 2)].rearrange("p x b r -> p (x b) r"),
                                        r2[:].rearrange("p x b -> p (x b)").unsqueeze(2).to_broadcast([P, 2 * B, RATIO]), ALU.mult))
                dve.scalar_tensor_tensor(vi[:], m8[:, :, 1, :], -1.0 / INV, r8[:, :, 1, :], ALU.mult, ALU.mult)
                vlink(dve.tensor_scalar(rqs[:], r8[:, :, 0, :], INV * INV, None, ALU.mult))
                dve.scalar_tensor_tensor(rq2[:], rqs[:], 1.0 / G_HD, rqs[:], ALU.mult, ALU.mult).then_inc(norm_done, 1)
                for x in range(2):
                    dve.wait_ge(kk_mm, 2 * i + x + 1)
                    dt = DT[:, bass.ds(2 * i + x, 1), :].rearrange("p g k -> p (g k)")
                    for b in range(B):
                        for r in range(RATIO):
                            u = b * RATIO + r
                            last = dve.scalar_tensor_tensor(Np[x][:, u, :], PJ[x][:, (2 * b + 1) * P:(2 * b + 2) * P], nb[:, x, b, r:r + 1],
                                                            dt[:, u * P:(u + 1) * P], ALU.mult, ALU.mult)
                    last.then_inc(np_done, 1)
                for x in range(2):
                    dt = DT[:, bass.ds(2 * i + x, 1), :].rearrange("p g (u k) -> p (g u) k", u=4)
                    for b in range(B):
                        last = dve.tensor_tensor(At[x][:, b * RATIO:(b + 1) * RATIO, :],
                                                 PJ[x][:, 2 * b * P:(2 * b + 1) * P].unsqueeze(1).to_broadcast([P, RATIO, P]),
                                                 dt[:, b * RATIO:(b + 1) * RATIO, :], ALU.mult)
                    last.then_inc(at_done, 1)
                for x in range(2):
                    dve.wait_ge(t_reset, 2 * i + x + 1)
                    wait_masks(mt_mm, 2 * i + x + 1, x)
                    dve.copy_predicated(T[x][:], mask(C_LV, 0), quad(YZ[x])).then_inc(t_upd, 1)
                    dve.copy_predicated(TT[x][:], mask(C_LVT, 0), Np[x][:]).then_inc(tt_upd, 1)
                for lv in range(1, LEVELS):
                    for x in range(2):
                        if lv < LAST:
                            wait_masks(zz_mm, 10 * i + 2 * (lv - 1) + x + 1, 4 * lv + x)
                            dve.copy_predicated(T[x][:], mask(C_LV, lv), quad(YZ[x])).then_inc(t_upd, 1)
                        wait_masks(zt_mm, 12 * i + 2 * (lv - 1) + x + 1, 4 * lv + 2 + x)
                        dve.copy_predicated(TT[x][:], mask(C_LVT, lv), quad(ZT[x])).then_inc(tt_upd, 1)
                    if more and lv in (3, 4, 5, 6):
                        conv(i + 1, (lv - 3) // 2, range(0, 2) if lv % 2 else range(2, 4))
                for x in range(2):
                    dve.wait_ge(tv_mm, 2 * i + x + 1)
                    dve.tensor_tensor(vn[x][:], quad(YZ[x]), nb[:, x].rearrange("p b r -> p (b r)").unsqueeze(2).to_broadcast([P, 4, P]),
                                      ALU.mult).then_inc(vn_done, 1)
                for x in range(2):
                    dve.wait_ge(so_done, 2 * i + x + 1)
                    vlink(dve.tensor_tensor(hv[x][:].rearrange("p (b r) -> p b r", b=B), so[x][:].rearrange("p (b r) -> p b r", b=B),
                                            rq2[:, x, :].unsqueeze(2).to_broadcast([P, B, RATIO]), ALU.mult))
                    dve.tensor_scalar(hv[x][:], hv[x][:], EPS, None, ALU.add).then_inc(h_var, 1)
                for x in range(2):
                    dve.wait_ge(h_pow, 2 * i + x + 1)
                    vlink(dve.tensor_tensor(hsc[x][:].rearrange("p (b r) -> p b r", b=B), hr[x][:].rearrange("p (b r) -> p b r", b=B),
                                            rqs[:, x, :].unsqueeze(2).to_broadcast([P, B, RATIO]), ALU.mult))
                    for u in range(4):
                        last = dve.scalar_tensor_tensor(hs[x][:, u, :], quad(ZT[x])[:, u, :], hsc[x][:, u:u + 1], sz[x][:, u, :],
                                                        ALU.mult, ALU.mult)
                    last.then_inc(h_done, 1)
                dve.wait_ge(yp_mm, i + 1)
                dve.tensor_tensor(X[:].rearrange("p b d -> p (b d)"), X[:].rearrange("p b d -> p (b d)"), PY, ALU.add).then_inc(x_acc, 1)

            PER = 7
            body(0, True)
            with dve.Fori(1, PAIRS - 1) as i:
                vlink.enter(i, 1, PER)
                body(i, True)
                vlink.leave(PAIRS - 2)
            body(PAIRS - 1, False)


def stage_c(nc, a, env, own):
    X, bk, cst, s, xn, mhalf, ones = (env[k] for k in ("X", "bk", "cst", "s", "xn", "mhalf", "ones"))
    link, alink, plink = env["dve_link"], env["act_link"], env["pool_link"]
    FC = C_IN // P

    def sb(name, shape, dt=F32):
        return own.enter_context(nc.sbuf_tensor("c_" + name, shape, dt))

    def sem(name):
        env["used"].append(own.enter_context(nc.semaphore("c_" + name)))
        return env["used"][-1]

    w = [sb("w1", [P, DC * C_IN]), sb("w2", [P, FC * D])]
    wr = [sb("w1r", [P, DC * C_IN]), sb("w2r", [P, FC * D])]
    wq = [sb("w1q", [P, DC * C_IN], BF16), sb("w2q", [P, FC * D], BF16)]
    wsum, wmean, wscale = sb("wsum", [P, 2]), sb("wmean", [P, 2]), sb("wscale", [P, 2])
    identb = sb("identb", [P, P], BF16)
    H, xs, xr = sb("H", [P, B, C_IN]), sb("xs", [P, B, C_IN]), sb("xr", [P, B, C_IN])
    xq = sb("xq", [P, B, C_IN], BF16)
    xqT = sb("xqT", [P, FC, TOK], BF16)
    ss, ssg, rn, am, sc, f = (sb(n, [P, 2, B]) for n in "ss ssg rn am sc f".split())
    w_in, wsum_done, tot_mm, wq_done, sq_done, ss_done, rn_done = (sem(n) for n in "w_in wsum_done tot_mm wq_done sq_done ss_done rn_done".split())
    xq_done, tr_mm, tr_cp, h_mm, h_done, f_done, y_mm, idb = (sem(n) for n in "xq_done tr_mm tr_cp h_mm h_done f_done y_mm idb".split())

    with nc.Block() as block:
        @block.sync
        def _(sp):
            sp.dma_start(w[0][:], a["c_w1"].rearrange("p c n -> p (c n)")).then_inc(w_in, 16)
            sp.dma_start(w[1][:], a["c_w2"].rearrange("p c n -> p (c n)")).then_inc(w_in, 16)

        @block.gpsimd
        def _(pool):
            env["ln_gpsimd"](2)
            for k in range(2):
                pool.wait_ge(ss_done, k + 1)
                pool.tensor_tensor(rn[:, k, :], ssg[:, k, :], mhalf[:, 0:B], ALU.pow).then_inc(rn_done, 1)

        @block.scalar
        def _(act):
            act.wait_ge(w_in, 32)
            for k in range(2):
                act.activation(wr[k][:], w[k][:], ACT.Abs, accum_out=wsum[:, k:k + 1]).then_inc(wsum_done, 1)
            act.wait_ge(s["ln_xn"], B * 3)
            for b in range(B):
                act.activation(xs[:, b, 0:D], xn[:, b, :], ACT.Square, accum_out=ss[:, 0, b:b + 1]).then_inc(sq_done, 1)
            act.wait_ge(tr_mm, 1)
            act.copy(xqT[:, 0:DC, :].rearrange("p c t -> p (c t)"), bk[0].bitcast(BF16)[:, 0:DC * TOK]).then_inc(tr_cp, 1)
            act.wait_ge(f_done, 1)
            for b in range(B):
                act.wait_ge(h_mm, b + 1)
                for n in range(2):
                    alink(act.activation(H[:, b, n * 512:(n + 1) * 512], bk[2 + 2 * b + n], ACT.Gelu, scale=f[:, 0, b:b + 1]))
                act.activation(H[:, b, :], H[:, b, :], ACT.Gelu).then_inc(h_done, 1)
                act.wait_ge(h_done, b + 1)
                act.activation(xs[:, b, :], H[:, b, :], ACT.Square, accum_out=ss[:, 1, b:b + 1]).then_inc(sq_done, 1)
            for n in range(2):
                act.wait_ge(tr_mm, 2 + n)
                act.copy(xqT[:, 4 * n:4 * n + 4, :].rearrange("p c t -> p (c t)"), bk[n].bitcast(BF16)).then_inc(tr_cp, 1)

        @block.tensor
        def _(pe):
            pe.wait_ge(wsum_done, 2)
            pe.matmul(bk[1][:, 0:2], ones[:], wsum[:], start=True, stop=True).then_inc(tot_mm, 1)
            pe.wait_ge(idb, 1)
            pe.wait_ge(xq_done, B)
            for c in range(DC):
                for b in range(B):
                    last = pe.transpose(bk[0].bitcast(BF16)[:, c * TOK + b * P:c * TOK + (b + 1) * P],
                                        xq[:, b, c * P:(c + 1) * P], identb[:])
            last.then_inc(tr_mm, 1)
            pe.wait_ge(tr_cp, 1)
            pe.wait_ge(wq_done, 1)
            for b in range(B):
                for n in range(2):
                    for c in range(DC):
                        last = pe.matmul(bk[2 + 2 * b + n], xqT[:, c, b * P:(b + 1) * P],
                                         wq[0][:, c * C_IN + n * 512:c * C_IN + (n + 1) * 512], start=(c == 0), stop=(c == DC - 1))
                last.then_inc(h_mm, 1)
            pe.wait_ge(xq_done, 2 * B)
            for n in range(2):
                for c in range(4):
                    for b in range(B):
                        last = pe.transpose(bk[n].bitcast(BF16)[:, c * TOK + b * P:c * TOK + (b + 1) * P],
                                            xq[:, b, (4 * n + c) * P:(4 * n + c + 1) * P], identb[:])
                last.then_inc(tr_mm, 1)
            pe.wait_ge(tr_cp, 3)
            pe.wait_ge(wq_done, 2)
            for b in range(B):
                for c in range(FC):
                    last = pe.matmul(bk[6][:, b * D:(b + 1) * D], xqT[:, c, b * P:(b + 1) * P], wq[1][:, c * D:(c + 1) * D],
                                     start=(c == 0), stop=(c == FC - 1))
            last.then_inc(y_mm, 1)

        @block.vector
        def _(dve):
            dve.tensor_copy(identb[:], cst[:, C_ID:C_ID + P]).then_inc(idb, 1)
            env["ln_vector"](2)

            def quantise(k, src, n):
                dve.wait_ge(sq_done, B * (k + 1))
                dve.tensor_scalar(ssg[:, k, :], ss[:, k, :], 1e-24, None, ALU.max).then_inc(ss_done, 1)
                dve.wait_ge(rn_done, k + 1)
                for b in range(B):
                    link(dve.tensor_scalar(xs[:, b, 0:n], src[:, b, :], rn[:, k, b:b + 1], float(n) ** 0.5, ALU.mult, ALU.mult))
                link(dve.tensor_reduce(am[:, k, :], xs[:, :, 0:n], AX, ALU.max, apply_absolute_value=True))
                link(dve.tensor_scalar(am[:, k, :], am[:, k, :], 1e-5, None, ALU.max))
                link(dve.reciprocal(sc[:, k, :], am[:, k, :]))
                link(dve.tensor_scalar(sc[:, k, :], sc[:, k, :], 127.0, None, ALU.mult))
                for b in range(B):
                    link(dve.tensor_scalar(xr[:, b, 0:n], xs[:, b, 0:n], sc[:, k, b:b + 1], ROUND, ALU.mult, ALU.add))
                    link(dve.tensor_scalar(xr[:, b, 0:n], xr[:, b, 0:n], -ROUND, 127.0, ALU.add, ALU.min))
                    dve.tensor_scalar(xq[:, b, 0:n], xr[:, b, 0:n], -128.0, None, ALU.max).then_inc(xq_done, 1)
                dve.tensor_scalar(f[:, k, :], am[:, k, :], wmean[:, k:k + 1], 1.0 / 127.0, ALU.mult, ALU.mult).then_inc(f_done, 1)

            dve.wait_ge(tot_mm, 1)
            link(dve.tensor_scalar(wmean[:], bk[1][:, 0:2], 1.0 / (C_IN * D), 1e-5, ALU.mult, ALU.max))
            link(dve.reciprocal(wscale[:], wmean[:]))
            quantise(0, xn, D)
            for k in range(2):
                link(dve.tensor_scalar(wr[k][:], w[k][:], wscale[:, k:k + 1], ROUND, ALU.mult, ALU.add))
                link(dve.tensor_scalar(wr[k][:], wr[k][:], -ROUND, 1.0, ALU.add, ALU.min))
                dve.tensor_scalar(wq[k][:], wr[k][:], -1.0, None, ALU.max).then_inc(wq_done, 1)
            quantise(1, H, C_IN)
            dve.wait_ge(f_done, 2)
            dve.wait_ge(y_mm, 1)
            for b in range(B):
                link(dve.scalar_tensor_tensor(X[:, b, :], bk[6][:, b * D:(b + 1) * D], f[:, 1, b:b + 1], X[:, b, :], ALU.mult, ALU.add))


def stage_d(nc, a, env, own):
    X, xnT, bk, ident, cst, s, scores = (env[k] for k in ("X", "xnT", "bk", "ident", "cst", "s", "scores"))
    link, alink = env["dve_link"], env["act_link"]
    HP = X_H // 2
    KG = KT // 4

    def sb(name, shape, dt=F32):
        return own.enter_context(nc.sbuf_tensor("d_" + name, shape, dt))

    def two(name, shape):
        return [sb(f"{name}{x}", shape) for x in range(2)]

    def sem(name):
        env["used"].append(own.enter_context(nc.semaphore("d_" + name)))
        return env["used"][-1]

    raw, KV, tmp = sb("raw", [P, KT, B, LAT]), sb("KV", [P, KT, B, LAT]), sb("tmp", [P, KT, B, LAT])
    rope = sb("rope", [P, 2, KT, LAT])
    KVT = sb("KVT", [P, CTX])
    w128, w64 = two("w128", [P, DC * X_K + X_CQ]), two("w64", [X_R, X_CQ + LAT])
    qh, wc = sb("qh", [P, TOK]), sb("wc", [XQ, 2, P])
    r1, r2, qr = sb("r1", [XQ, 2, TOK]), sb("r2", [XQ, 2, TOK]), sb("qr", [XQ, 2, TOK])
    qp = two("qp", [P, P])
    Pr = two("Pr", [P, CTX])
    Pt = [sb(f"Pt{g}", [P, 4, P]) for g in range(KG)]
    nm2, negm, sums, rc = sb("nm2", [P, B, 2]), sb("negm", [P, B]), sb("sums", [P, B]), sb("rc", [P, B])
    ctxc = sb("ctxc", [P, B, X_H * LAT])
    wkv, wo = sb("wkv", [P, HP, 2, X_K]), sb("wo", [P, X_H, D])
    ccT, cl = two("ccT", [P, TOK]), two("cl", [P, 2, TOK])

    raw_in, rope_in, w_in = sem("raw_in"), sem("rope_in"), [sem(f"w_in{x}") for x in range(2)]
    tail_in = sem("tail_in")
    (kv_done, kvt_mm, kvt_cp, f1_mm, f1_cp, f2_mm, rope_done, f3_mm, q_done, sc_mm, max_done, exp_done, rc_done, tr_mm,
     tr_cp, pv_mm, ev_done, wkv_zero) = (sem(n) for n in (
         "kv_done kvt_mm kvt_cp f1_mm f1_cp f2_mm rope_done f3_mm q_done sc_mm max_done exp_done rc_done tr_mm "
         "tr_cp pv_mm ev_done wkv_zero").split())
    TP, CT, FB = [bk[0], bk[1]], bk[2], bk[3]

    def pairs(eng, body):
        body(0, True, False)
        with eng.Fori(1, HP - 1) as p:
            body(p, False, False)
        body(HP - 1, False, True)

    with nc.Block() as block:
        @block.sync
        def _(sp):
            sp.dma_start(raw[:], a["d_ctx"]).then_inc(raw_in, 16)
            sp.dma_start(rope[:], a["rope"]).then_inc(rope_in, 16)
            for x in range(2):
                sp.dma_start(w128[x][:], a["d_w128"][x]).then_inc(w_in[x], 16)
                sp.dma_start(w64[x][:], a["d_w64"][x]).then_inc(w_in[x], 16)
            sp.dma_start(wo[:], a["d_wo"]).then_inc(tail_in, 16)
            sp.wait_ge(wkv_zero, 1)
            for hh in range(2):
                sp.dma_start(wkv[64 * hh:64 * hh + 64, :, hh, :], a["d_wkv"][hh]).then_inc(tail_in, 16)
            with sp.Fori(0, HP - 1) as p:
                for x in range(2):
                    sp.wait_ge(f2_mm, 2 * p + x + 1)
                    sp.dma_start(w128[x][:], a["d_w128"][bass.ds(2 * p + 2 + x, 1)].rearrange("h p n -> (h p) n")).then_inc(w_in[x], 16)
                    sp.dma_start(w64[x][:], a["d_w64"][bass.ds(2 * p + 2 + x, 1)].rearrange("h p n -> (h p) n")).then_inc(w_in[x], 16)

        @block.gpsimd
        def _(pool):
            pool.memset(wkv[:], 0.0).then_inc(wkv_zero, 1)
            env["ln_gpsimd"](3)

        @block.tensor
        def _(pe):
            pe.wait_ge(kv_done, 1)
            for g in range(KG):
                for j in range(4):
                    last = pe.transpose(scores[:, g, j * P:(j + 1) * P], KV[:, 4 * g + j].rearrange("p b d -> p (b d)"), ident)
                last.then_inc(kvt_mm, 1)
            pe.wait_ge(kvt_cp, KG)
            env["ln_tensor"](3)
            pe.wait_ge(s["ln_xT"], env["turned"](3))

            def front1(p, x):
                h = 2 * p + x
                pe.wait_ge(w_in[x], 32 * p + 32)
                pe.wait_ge(q_done, h)
                for c in range(DC):
                    pe.matmul(FB[:, 0:TOK], w128[x][:, c * X_K:(c + 1) * X_K], xnT[:, c, :], start=(c == 0), stop=(c == DC - 1))
                for half in range(2):
                    last = pe.matmul(FB[0:XQ, TOK + half * P:TOK + (half + 1) * P].rearrange("p (b d) -> p b d", b=B),
                                     w64[x][:, half * XQ:(half + 1) * XQ],
                                     w64[x][:, X_CQ:].unsqueeze(1).to_broadcast([X_R, B, LAT]), start=True, stop=True)
                last.then_inc(f1_mm, 1)

            def front2(p, x):
                pe.wait_ge(f1_cp, 2 * p + x + 1)
                for half in range(2):
                    last = pe.matmul(FB[0:XQ, half * TOK:(half + 1) * TOK], w128[x][:, DC * X_K + half * XQ:DC * X_K + (half + 1) * XQ],
                                     qh[:], start=True, stop=True)
                last.then_inc(f2_mm, 1)

            def front3(p, x):
                pe.wait_ge(rope_done, 2 * p + x + 1)
                for half in range(2):
                    last = pe.matmul(FB[:, 0:TOK], wc[:, half, :], qr[:, half, :], start=(half == 0), stop=(half == 1))
                last.then_inc(f3_mm, 1)

            def weigh(m, b):
                for g in range(KG + 1):
                    if g < KG:
                        if g == 0:
                            pe.wait_ge(exp_done, m + 1)
                        if not (isinstance(m, int) and 4 * m + g < 2):
                            pe.wait_ge(tr_cp, 4 * m + g - 1)
                        for j in range(4):
                            t = 4 * g + j
                            last = pe.transpose(TP[g % 2][:, j * P:(j + 1) * P], Pr[b][:, t * P:(t + 1) * P], ident)
                        last.then_inc(tr_mm, 1)
                    if g >= 1:
                        if g == 1:
                            pe.wait_ge(ev_done, m)
                        pe.wait_ge(tr_cp, 4 * m + g)
                        for j in range(4):
                            t = 4 * (g - 1) + j
                            last = pe.matmul(CT[:, 0:LAT], Pt[g - 1][:, j, :], KV[:, t, b, :], start=(t == 0), stop=(t == KT - 1))
                last.then_inc(pv_mm, 1)

            front1(0, 0)
            front2(0, 0)
            front3(0, 0)

            def body(p, first, last_pair):
                for x in range(2):
                    for b in range(B):
                        n = 4 * p + 2 * x + b
                        nxt = (p, 1) if x == 0 else (p + 1, 0)
                        more = not (last_pair and x == 1)
                        pe.wait_ge(q_done, 2 * p + x + 1)
                        pe.wait_ge(exp_done, n)
                        rows = slice(LAT * b, LAT * (b + 1))
                        for g in range(KG):
                            pe.matmul(scores[:, g, :], qp[x][rows, :], KVT[rows, g * 512:(g + 1) * 512],
                                      start=True, stop=True).then_inc(sc_mm, 1)
                        if more and b == 0:
                            front1(*nxt)
                        if more and b == 1:
                            front3(*nxt)
                        if not (first and x == 0 and b == 0):
                            weigh(n - 1, (b + 1) % 2)
                        if more and b == 0:
                            front2(*nxt)

            pairs(pe, body)
            weigh(4 * HP - 1, 1)

        @block.scalar
        def _(act):
            for g in range(KG):
                act.wait_ge(kvt_mm, g + 1)
                act.copy(KVT[:, g * 512:(g + 1) * 512], scores[:, g, :]).then_inc(kvt_cp, 1)
            env["ln_scalar"](3)

            def front1(p, x):
                act.wait_ge(f1_mm, 2 * p + x + 1)
                act.copy(qh[:], FB[:, 0:TOK])
                act.copy(wc[:].rearrange("p f d -> p (f d)"), FB[0:XQ, TOK:2 * TOK]).then_inc(f1_cp, 1)

            def front3(p, x):
                act.wait_ge(f3_mm, 2 * p + x + 1)
                act.copy(qp[x][0:LAT, :], FB[0:LAT, 0:P])
                act.copy(qp[x][LAT:P, :], FB[LAT:P, P:TOK]).then_inc(q_done, 1)

            def keep(m, h, b):
                act.wait_ge(rc_done, m + 1)
                act.wait_ge(pv_mm, m + 1)
                at = slice(h * LAT, (h + 1) * LAT) if isinstance(h, int) else bass.ds(h * LAT, LAT)
                act.activation(ctxc[:, b, at], CT[:, 0:LAT], ACT.Copy, scale=rc[:, b:b + 1]).then_inc(ev_done, 1)

            front1(0, 0)
            front3(0, 0)

            def body(p, first, last_pair):
                for x in range(2):
                    for b in range(B):
                        n = 4 * p + 2 * x + b
                        nxt = (p, 1) if x == 0 else (p + 1, 0)
                        more = not (last_pair and x == 1)
                        if more:
                            (front1 if b == 0 else front3)(*nxt)
                        act.wait_ge(max_done, n + 1)
                        act.activation(Pr[b][:], scores[:].rearrange("p g k -> p (g k)"), ACT.Exp, bias=negm[:, b:b + 1],
                                       accum_out=sums[:, b:b + 1]).then_inc(exp_done, 1)
                        if not (first and x == 0 and b == 0):
                            keep(n - 1, 2 * p + x - (b == 0), 1 - b)

            pairs(act, body)
            keep(4 * HP - 1, X_H - 1, 1)

        @block.vector
        def _(dve):
            dve.wait_ge(raw_in, 16)
            dve.wait_ge(rope_in, 16)
            HL = LAT // 2
            cos, sin = rope[:, 0].unsqueeze(2).to_broadcast([P, KT, B, LAT]), rope[:, 1].unsqueeze(2).to_broadcast([P, KT, B, LAT])
            dve.tensor_tensor(tmp[:, :, :, 0:HL], raw[:, :, :, HL:LAT], sin[:, :, :, 0:HL], ALU.mult)
            link(dve.tensor_tensor(tmp[:, :, :, HL:LAT], raw[:, :, :, 0:HL], sin[:, :, :, HL:LAT], ALU.mult))
            link(dve.tensor_tensor(KV[:], raw[:], cos, ALU.mult))
            dve.tensor_tensor(KV[:], KV[:], tmp[:], ALU.add).then_inc(kv_done, 1)
            env["ln_vector"](3)

            def rotate(p, x):
                dve.wait_ge(f2_mm, 2 * p + x + 1)
                q = FB[0:XQ].rearrange("p (f t) -> p f t", f=2)
                cq = cst[0:XQ, C_CQ:C_CQ + 2 * TOK].rearrange("p (f t) -> p f t", f=2)
                sq = cst[0:XQ, C_SQ:C_SQ + 2 * TOK].rearrange("p (f t) -> p f t", f=2)
                dve.tensor_tensor(r1[:], q, cq, ALU.mult)
                for half in range(2):
                    last = dve.tensor_tensor(r2[:, half, :], q[:, 1 - half, :], sq[:, half, :], ALU.mult)
                link(last)
                dve.tensor_tensor(qr[:], r1[:], r2[:], ALU.add).then_inc(rope_done, 1)

            def turn(m):
                for g in range(KG):
                    dve.wait_ge(tr_mm, 4 * m + g + 1)
                    dve.tensor_copy(Pt[g][:].rearrange("p j q -> p (j q)"), TP[g % 2]).then_inc(tr_cp, 1)

            rotate(0, 0)

            def body(p, first, last_pair):
                for x in range(2):
                    for b in range(B):
                        n = 4 * p + 2 * x + b
                        nxt = (p, 1) if x == 0 else (p + 1, 0)
                        if b == 1 and not (last_pair and x == 1):
                            rotate(*nxt)
                        for k in range(2):
                            dve.wait_ge(sc_mm, 4 * n + 2 * k + 2)
                            last = dve.tensor_reduce(nm2[:, b, k:k + 1], scores[:, 2 * k:2 * k + 2, :].rearrange("p g k -> p (g k)"),
                                                     AX, ALU.max, negate=True)
                        link(last)
                        dve.tensor_tensor(negm[:, b:b + 1], nm2[:, b, 0:1], nm2[:, b, 1:2], ALU.min).then_inc(max_done, 1)
                        if not (first and x == 0 and b == 0):
                            dve.wait_ge(exp_done, n)
                            dve.reciprocal(rc[:, 1 - b:2 - b], sums[:, 1 - b:2 - b]).then_inc(rc_done, 1)
                            turn(n - 1)

            body(0, True, False)
            per = 6
            with dve.Fori(1, HP - 1) as p:
                link.enter(p, 1, per)
                body(p, False, False)
                link.leave(HP - 2)
            body(HP - 1, False, True)
            dve.wait_ge(exp_done, 4 * HP)
            dve.reciprocal(rc[:, 1:2], sums[:, 1:2]).then_inc(rc_done, 1)
            turn(4 * HP - 1)

    ct_mm, ct_cp, cl_mm, cl_cp, y_mm = (sem(n) for n in "ct_mm ct_cp cl_mm cl_cp y_mm".split())
    with nc.Block() as block:
        @block.tensor
        def _(pe):
            pe.wait_ge(tail_in, 48)
            for q in range(HP + 2):
                if q < HP:
                    if q >= 2:
                        pe.wait_ge(ct_cp, q - 1)
                    for b in range(B):
                        last = pe.transpose(bk[q % 2][:, b * P:(b + 1) * P], ctxc[:, b, q * P:(q + 1) * P], ident)
                    last.then_inc(ct_mm, 1)
                if 1 <= q <= HP:
                    k = q - 1
                    pe.wait_ge(ct_cp, k + 1)
                    if k >= 2:
                        pe.wait_ge(cl_cp, k - 1)
                    for hh in range(2):
                        last = pe.matmul(bk[2 + k % 2][:, hh * TOK:(hh + 1) * TOK], wkv[:, k, hh, :], ccT[k % 2][:], start=True, stop=True)
                    last.then_inc(cl_mm, 1)
                if q >= 2:
                    k = q - 2
                    pe.wait_ge(cl_cp, k + 1)
                    for hh in range(2):
                        for b in range(B):
                            last = pe.matmul(bk[4 + b][:, 0:D], cl[k % 2][:, hh, b * P:(b + 1) * P], wo[:, 2 * k + hh, :],
                                             start=(k + hh == 0), stop=(k == HP - 1 and hh == 1))
                    last.then_inc(y_mm, 1)

        @block.scalar
        def _(act):
            for k in range(HP):
                act.wait_ge(ct_mm, k + 1)
                if k >= 2:
                    act.wait_ge(cl_mm, k - 1)
                act.copy(ccT[k % 2][:], bk[k % 2][:, 0:TOK]).then_inc(ct_cp, 1)

        @block.vector
        def _(dve):
            for k in range(HP):
                dve.wait_ge(cl_mm, k + 1)
                if k >= 2:
                    dve.wait_ge(y_mm, k - 1)
                dve.tensor_copy(cl[k % 2][:].rearrange("p h t -> p (h t)"), bk[2 + k % 2]).then_inc(cl_cp, 1)
            dve.wait_ge(y_mm, HP)
            for b in range(B):
                link(dve.tensor_tensor(X[:, b, :], X[:, b, :], bk[4 + b][:, 0:D], ALU.add))


def stage_e(nc, a, env, own):
    X, xnT, bk, ident, cst, s = (env[k] for k in ("X", "xnT", "bk", "ident", "cst", "s"))
    link = env["dve_link"]
    QH, RH = E_QR // 2, E_ROPE // 2
    NP = E_REP // 2

    def sb(name, shape, dt=F32):
        return own.enter_context(nc.sbuf_tensor("e_" + name, shape, dt))

    def two(name, shape):
        return [sb(f"{name}{x}", shape) for x in range(2)]

    def sem(name):
        env["used"].append(own.enter_context(nc.semaphore("e_" + name)))
        return env["used"][-1]

    wkvd, wqd = sb("wkvd", [P, DC, LAT]), sb("wqd", [P, DC, E_QR])
    wkn, wv = sb("wkn", [LAT, E_KV * E_NOPE]), sb("wv", [LAT, E_KV * E_V])
    wkr = sb("wkr", [LAT, E_KV, 2, 2, E_ROPE])
    wqn = sb("wqn", [QH, 2, E_H * E_NOPE])
    wqr = sb("wqr", [QH, 2, 2, E_H, E_ROPE])
    wo = sb("wo", [P, E_H, D])
    kvcT, qcT = sb("kvcT", [LAT, TOK]), sb("qcT", [QH, 2, TOK])
    v = sb("v", [P, B, E_KV * E_V])
    knT = two("knT", [P, TOK])
    krT = [two(f"krT{x}", [P, TOK]) for x in range(2)]
    qnT, qrT = two("qnT", [P, E_REP, TOK]), two("qrT", [P, NP, TOK])
    r1, r2 = sb("r1", [P, TOK]), sb("r2", [P, TOK])
    S, PT, oT = (two(n, [P, E_REP, P]) for n in ("S", "PT", "oT"))
    nmax, sums, rec = (two(n, [P, E_REP]) for n in ("nmax", "sums", "rec"))
    w_in = sem("w_in")
    (kz, c_mm, c_cp, v_mm, v_cp, kn_mm, kr_mm, qn_mm, qr_mm, kn_cp, kr_cp, qn_cp, qr_cp, sc_mm, masked, nmax_done, exp_done,
     rec_done, norm_done, tr_mm, tr_cp, pv_mm, pv_cp, y_mm, x_acc) = (sem(n) for n in (
         "kz c_mm c_cp v_mm v_cp kn_mm kr_mm qn_mm qr_mm kn_cp kr_cp qn_cp qr_cp sc_mm masked nmax_done exp_done "
         "rec_done norm_done tr_mm tr_cp pv_mm pv_cp y_mm x_acc").split())
    KN, KR, QN, QR, SC = bk[0], bk[1], [bk[2], bk[3]], [bk[4], bk[5]], [bk[6], bk[7]]
    LOADS = 5 + 2 * 3 + 2 * 3 + 1
    scale = (E_NOPE + E_ROPE) ** -0.5

    with nc.Block() as block:
        @block.sync
        def _(sp):
            for t, d in ((wkvd, "e_wkvd"), (wqd, "e_wqd"), (wkn, "e_wkn"), (wv, "e_wv"), (wqn, "e_wqn")):
                sp.dma_start(t[:], a[d]).then_inc(w_in, 16)
            kr = a["e_wkr"].rearrange("l (n e) -> l n e", n=E_KV)
            for twice in range(2):
                sp.dma_start(wkr[:, :, 0, twice, :], kr).then_inc(w_in, 16)
                for half in range(2):
                    sp.dma_start(wkr[:, :, 1, twice, half * RH:(half + 1) * RH], kr[:, :, (1 - half) * RH:(2 - half) * RH]).then_inc(w_in, 16)
            for c in range(2):
                qr = a["e_wqr"][:, c, :].rearrange("p (h e) -> p h e", h=E_H)
                sp.dma_start(wqr[:, c, 0], qr).then_inc(w_in, 16)
                for half in range(2):
                    sp.dma_start(wqr[:, c, 1, :, half * RH:(half + 1) * RH], qr[:, :, (1 - half) * RH:(2 - half) * RH]).then_inc(w_in, 16)
            sp.dma_start(wo[:], a["e_wo"]).then_inc(w_in, 16)

        @block.gpsimd
        def _(pool):
            env["ln_gpsimd"](4)
            for x in range(2):
                for hh in range(2):
                    pool.memset(krT[hh][x][:], 0.0).then_inc(kz, 1)

        @block.tensor
        def _(pe):
            env["ln_tensor"](4)
            pe.wait_ge(w_in, 16 * LOADS)
            pe.wait_ge(s["ln_xT"], env["turned"](4))
            for c in range(DC):
                pe.matmul(KN[0:LAT, 0:TOK], wkvd[:, c, :], xnT[:, c, :], start=(c == 0), stop=(c == DC - 1))
            for half in range(2):
                for c in range(DC):
                    last = pe.matmul(KR[0:QH, half * TOK:(half + 1) * TOK], wqd[:, c, half * QH:(half + 1) * QH], xnT[:, c, :],
                                     start=(c == 0), stop=(c == DC - 1))
            last.then_inc(c_mm, 1)
            pe.wait_ge(c_cp, 2)
            for b in range(B):
                pe.matmul(SC[b], kvcT[:, b * P:(b + 1) * P], wv[:], start=True, stop=True).then_inc(v_mm, 1)

            def project(n):
                if n:
                    pe.wait_ge(kn_cp, n)
                pe.matmul(KN[:, 0:TOK], wkn[:, n * E_NOPE:(n + 1) * E_NOPE], kvcT[:], start=True, stop=True).then_inc(kn_mm, 1)
                if n:
                    pe.wait_ge(kr_cp, n)
                for sw in range(2):
                    last = pe.matmul(KR[:, sw * TOK:(sw + 1) * TOK], wkr[:, n, sw].rearrange("l t e -> l (t e)"), kvcT[:],
                                     start=True, stop=True)
                last.then_inc(kr_mm, 1)
                for k in range(NP):
                    if n:
                        pe.wait_ge(qn_cp, NP * (n - 1) + k + 1)
                    for hh in range(2):
                        h = n * E_REP + 2 * k + hh
                        for c in range(2):
                            last = pe.matmul(QN[k][:, hh * TOK:(hh + 1) * TOK], wqn[:, c, h * E_NOPE:(h + 1) * E_NOPE], qcT[:, c, :],
                                             start=(c == 0), stop=(c == 1))
                    last.then_inc(qn_mm, 1)
                for k in range(NP):
                    if n:
                        pe.wait_ge(qr_cp, NP * (n - 1) + k + 1)
                        pe.wait_ge(x_acc, n - 1)
                    h = n * E_REP + 2 * k
                    for sw in range(2):
                        for c in range(2):
                            last = pe.matmul(QR[k][:, sw * TOK:(sw + 1) * TOK], wqr[:, c, sw, h:h + 2].rearrange("p h e -> p (h e)"),
                                             qcT[:, c, :], start=(c == 0), stop=(c == 1))
                    last.then_inc(qr_mm, 1)

            project(0)
            for n in range(E_KV):
                x = n % 2
                pe.wait_ge(kn_cp, n + 1)
                pe.wait_ge(kr_cp, n + 1)
                pe.wait_ge(qn_cp, NP * (n + 1))
                pe.wait_ge(qr_cp, NP * (n + 1))
                pe.wait_ge(v_cp, B)
                for b in range(B):
                    if n:
                        pe.wait_ge(pv_cp, B * (n - 1) + b + 1)
                    tok = slice(b * P, (b + 1) * P)
                    for j in range(E_REP):
                        out = SC[b][:, j * P:(j + 1) * P]
                        pe.matmul(out, qnT[x][:, j, tok], knT[x][:, tok], start=True, stop=False)
                        last = pe.matmul(out, qrT[x][:, j // 2, tok], krT[j % 2][x][:, tok], start=False, stop=True)
                    last.then_inc(sc_mm, 1)
                if n + 1 < E_KV:
                    project(n + 1)
                for b in range(B):
                    pe.wait_ge(norm_done, B * n + b + 1)
                    for j in range(E_REP):
                        last = pe.transpose(SC[b][:, j * P:(j + 1) * P], S[b][:, j, :], ident)
                    last.then_inc(tr_mm, 1)
                for b in range(B):
                    pe.wait_ge(tr_cp, B * n + b + 1)
                    pe.matmul(SC[b], v[:, b, n * E_V:(n + 1) * E_V], PT[b][:].rearrange("p j q -> p (j q)"),
                              start=True, stop=True).then_inc(pv_mm, 1)
                pe.wait_ge(pv_cp, B * (n + 1))
                pe.wait_ge(qr_cp, min(NP * (n + 2), NP * E_KV))
                for b in range(B):
                    for j in range(E_REP):
                        last = pe.matmul(QR[0][:, b * D:(b + 1) * D], oT[b][:, j, :], wo[:, n * E_REP + j, :],
                                         start=(j == 0), stop=(j == E_REP - 1))
                last.then_inc(y_mm, 1)

        @block.scalar
        def _(act):
            env["ln_scalar"](4)
            act.wait_ge(c_mm, 1)
            act.copy(kvcT[:], KN[0:LAT, 0:TOK]).then_inc(c_cp, 1)
            act.copy(qcT[:].rearrange("p c t -> p (c t)"), KR[0:QH, :]).then_inc(c_cp, 1)
            for b in range(B):
                act.wait_ge(v_mm, b + 1)
                act.copy(v[:, b, :], SC[b]).then_inc(v_cp, 1)

            def copies(n):
                x = n % 2
                if n >= 2:
                    act.wait_ge(sc_mm, B * (n - 1))
                act.wait_ge(kn_mm, n + 1)
                act.copy(knT[x][:], KN[:, 0:TOK]).then_inc(kn_cp, 1)
                for k in range(NP):
                    act.wait_ge(qn_mm, NP * n + k + 1)
                    act.copy(qnT[x][:, 2 * k:2 * k + 2, :].rearrange("p h t -> p (h t)"), QN[k]).then_inc(qn_cp, 1)

            copies(0)
            for n in range(E_KV):
                for b in range(B):
                    act.wait_ge(nmax_done, B * n + b + 1)
                    for j in range(E_REP):
                        last = act.activation(S[b][:, j, :], S[b][:, j, :], ACT.Exp, bias=nmax[b][:, j:j + 1],
                                              accum_out=sums[b][:, j:j + 1])
                    last.then_inc(exp_done, 1)
                if n + 1 < E_KV:
                    copies(n + 1)
                for b in range(B):
                    act.wait_ge(pv_mm, B * n + b + 1)
                    if n:
                        act.wait_ge(y_mm, n)
                    act.copy(oT[b][:].rearrange("p j q -> p (j q)"), SC[b]).then_inc(pv_cp, 1)

        @block.vector
        def _(dve):
            env["ln_vector"](4)
            dve.wait_ge(kz, 4)
            cos, sin = cst[:, C_CE:C_CE + TOK], cst[:, C_SE:C_SE + TOK]
            causal = cst[:, C_CAUSAL:C_CAUSAL + P].unsqueeze(1).to_broadcast([P, E_REP, P])

            def rotate(n):
                x = n % 2
                if n >= 2:
                    dve.wait_ge(sc_mm, B * (n - 1))
                dve.wait_ge(kr_mm, n + 1)
                dve.tensor_tensor(r1[:], KR[:, 0:TOK], cos, ALU.mult)
                link(dve.tensor_tensor(r2[:], KR[:, TOK:2 * TOK], sin, ALU.mult))
                dve.tensor_tensor(krT[0][x][0:64, :], r1[0:64, :], r2[0:64, :], ALU.add)
                dve.tensor_tensor(krT[1][x][64:P, :], r1[64:P, :], r2[64:P, :], ALU.add).then_inc(kr_cp, 1)
                dve.wait_ge(kr_cp, n + 1)
                for k in range(NP):
                    dve.wait_ge(qr_mm, NP * n + k + 1)
                    dve.tensor_tensor(r1[:], QR[k][:, 0:TOK], cos, ALU.mult)
                    link(dve.tensor_tensor(r2[:], QR[k][:, TOK:2 * TOK], sin, ALU.mult))
                    dve.tensor_tensor(qrT[x][:, k, :], r1[:], r2[:], ALU.add).then_inc(qr_cp, 1)
                    dve.wait_ge(qr_cp, NP * n + k + 1)

            rotate(0)
            for n in range(E_KV):
                for b in range(B):
                    if n:
                        dve.wait_ge(tr_mm, B * (n - 1) + b + 1)
                    dve.wait_ge(sc_mm, B * n + b + 1)
                    dve.scalar_tensor_tensor(S[b][:], SC[b].rearrange("p (j k) -> p j k", j=E_REP), scale, causal,
                                             ALU.mult, ALU.add).then_inc(masked, 1)
                    dve.wait_ge(masked, B * n + b + 1)
                    dve.tensor_reduce(nmax[b][:], S[b][:], AX, ALU.max, negate=True).then_inc(nmax_done, 1)
                if n + 1 < E_KV:
                    rotate(n + 1)
                for b in range(B):
                    dve.wait_ge(exp_done, B * n + b + 1)
                    link(dve.reciprocal(rec[b][:], sums[b][:]))
                    dve.tensor_tensor(S[b][:], S[b][:], rec[b][:].unsqueeze(2).to_broadcast([P, E_REP, P]), ALU.mult).then_inc(norm_done, 1)
                for b in range(B):
                    dve.wait_ge(tr_mm, B * n + b + 1)
                    dve.tensor_copy(PT[b][:].rearrange("p j q -> p (j q)"), SC[b]).then_inc(tr_cp, 1)
                dve.wait_ge(y_mm, n + 1)
                dve.tensor_tensor(X[:].rearrange("p b d -> p (b d)"), X[:].rearrange("p b d -> p (b d)"), QR[0], ALU.add).then_inc(x_acc, 1)
                dve.wait_ge(x_acc, n + 1)


def stage_f(nc, a, env, own):
    X, xnT, bk, ident, cst, s = (env[k] for k in ("X", "xnT", "bk", "ident", "cst", "s"))
    link = env["dve_link"]
    ER = M_E * M_R
    EC = ER // P
    KTOK = M_K * TOK

    def sb(name, shape, dt=F32):
        return own.enter_context(nc.sbuf_tensor("f_" + name, shape, dt))

    def sem(name):
        env["used"].append(own.enter_context(nc.semaphore("f_" + name)))
        return env["used"][-1]

    wg = sb("wg", [P, DC, M_E])
    w1, w3 = sb("w1", [P, DC, M_F]), sb("w3", [P, DC, M_F])
    a1, a3 = sb("a1", [P, DC, ER]), sb("a3", [P, DC, ER])
    b1, b3 = sb("b1", [P, EC, M_F]), sb("b3", [P, EC, M_F])
    w2, a2, b2 = sb("w2", [P, FCH, D]), sb("a2", [P, FCH, ER]), sb("b2", [P, EC, D])
    nm, sums, rs = sb("nm", [P, B]), sb("sums", [P, B]), sb("rs", [P, B])
    pr = [sb(f"pr{k}", [P, B, M_E]) for k in range(3)]
    eq, oh = sb("eq", [P, B, M_E]), sb("oh", [P, M_K, B, M_E])
    top, ix, tot, rw = sb("top", [P, M_K, B]), sb("ix", [P, B]), sb("tot", [P, B]), sb("rw", [P, M_K, B])
    mk = sb("mk", [P, M_K * B, M_E, M_R])
    mkT = sb("mkT", [P, EC, KTOK])
    am = [sb(f"am{k}", [P, EC, KTOK]) for k in range(3)]
    g1 = [sb(f"g1{k}", [P, KTOK]) for k in range(2)]
    x2 = sb("x2", [P, FCH, KTOK])
    w_in = sem("w_in")
    (lg_mm, nm_done, ex_done, mk_done, mt_mm, mt_cp, a_mm, am_done, x1_mm, x3_mm, g_done, x2_done, a2_mm, a2_done, y_mm) = (
        sem(n) for n in "lg_mm nm_done ex_done mk_done mt_mm mt_cp a_mm am_done x1_mm x3_mm g_done x2_done a2_mm a2_done y_mm".split())
    loads = ((wg, "f_wg"), (a1, "f_a1"), (a3, "f_a3"), (w1, "f_w1"), (b1, "f_b1"), (w3, "f_w3"), (b3, "f_b3"),
             (w2, "f_w2"), (a2, "f_a2"), (b2, "f_b2"))
    G1, G3 = [bk[2], bk[3]], [bk[4], bk[5]]

    def slots(ap):
        return ap.unsqueeze(1).to_broadcast([P, M_K, TOK])

    with nc.Block() as block:
        @block.sync
        def _(sp):
            for t, d in loads:
                sp.dma_start(t[:], a[d]).then_inc(w_in, 16)

        @block.gpsimd
        def _(pool):
            env["ln_gpsimd"](5)

        @block.tensor
        def _(pe):
            env["ln_tensor"](5)
            pe.wait_ge(w_in, 16 * len(loads))
            pe.wait_ge(s["ln_xT"], env["turned"](5))
            for b in range(B):
                for c in range(DC):
                    last = pe.matmul(bk[0][:, b * M_E:(b + 1) * M_E], xnT[:, c, b * P:(b + 1) * P], wg[:, c, :],
                                     start=(c == 0), stop=(c == DC - 1))
            last.then_inc(lg_mm, 1)
            for k, w in enumerate((a1, a3)):
                for e in range(EC):
                    for c in range(DC):
                        last = pe.matmul(bk[6 + k][:, e * TOK:(e + 1) * TOK], w[:, c, e * P:(e + 1) * P], xnT[:, c, :],
                                         start=(c == 0), stop=(c == DC - 1))
                last.then_inc(a_mm, 1)
            pe.wait_ge(mk_done, M_K * B)
            for e in range(EC):
                for kb in range(M_K * B):
                    last = pe.transpose(bk[e][:, kb * P:(kb + 1) * P], mk[:, kb].rearrange("p e r -> p (e r)")[:, e * P:(e + 1) * P], ident)
                last.then_inc(mt_mm, 1)
            for f in range(FCH):
                cols = slice(f * P, (f + 1) * P)
                for bank, w, low, m, done in ((G1, w1, b1, am[0], x1_mm), (G3, w3, b3, am[1], x3_mm)):
                    if f >= 2:
                        pe.wait_ge(x2_done, f - 1)
                    out = bank[f % 2].rearrange("p (k t) -> p k t", k=M_K)
                    for c in range(DC):
                        pe.matmul(out, w[:, c, cols], slots(xnT[:, c, :]), start=(c == 0), stop=False)
                    if f == 0:
                        pe.wait_ge(am_done, EC * (1 if m is am[0] else 2))
                    for e in range(EC):
                        last = pe.matmul(bank[f % 2], low[:, e, cols], m[:, e, :], start=False, stop=(e == EC - 1))
                    last.then_inc(done, 1)
            pe.wait_ge(x2_done, FCH)
            for e in range(EC):
                for f in range(FCH):
                    last = pe.matmul(bk[6 + e], a2[:, f, e * P:(e + 1) * P], x2[:, f, :], start=(f == 0), stop=(f == FCH - 1))
                last.then_inc(a2_mm, 1)
            for k in range(M_K):
                for b in range(B):
                    t = slice((k * B + b) * P, (k * B + b + 1) * P)
                    out = bk[k * B + b][:, 0:D]
                    for f in range(FCH):
                        pe.matmul(out, x2[:, f, t], w2[:, f, :], start=(f == 0), stop=False)
                    pe.wait_ge(a2_done, EC)
                    for e in range(EC):
                        last = pe.matmul(out, am[2][:, e, t], b2[:, e, :], start=False, stop=(e == EC - 1))
                    last.then_inc(y_mm, 1)

        @block.scalar
        def _(act):
            env["ln_scalar"](5)
            act.wait_ge(nm_done, 1)
            for b in range(B):
                last = act.activation(pr[0][:, b, :], bk[0][:, b * M_E:(b + 1) * M_E], ACT.Exp, bias=nm[:, b:b + 1],
                                      accum_out=sums[:, b:b + 1])
            last.then_inc(ex_done, 1)
            for e in range(EC):
                act.wait_ge(mt_mm, e + 1)
                act.copy(mkT[:, e, :], bk[e]).then_inc(mt_cp, 1)
            for f in range(FCH):
                act.wait_ge(x1_mm, f + 1)
                if f >= 2:
                    act.wait_ge(x2_done, f - 1)
                act.activation(g1[f % 2][:], G1[f % 2], ACT.Silu).then_inc(g_done, 1)

        @block.vector
        def _(dve):
            env["ln_vector"](5)
            dve.wait_ge(lg_mm, 1)
            dve.tensor_reduce(nm[:], bk[0][:, 0:B * M_E].rearrange("p (b e) -> p b e", b=B), AX, ALU.max, negate=True).then_inc(nm_done, 1)
            dve.wait_ge(ex_done, 1)
            link(dve.reciprocal(rs[:], sums[:]))
            link(dve.tensor_tensor(pr[1][:], pr[0][:], rs[:].unsqueeze(2).to_broadcast([P, B, M_E]), ALU.mult))
            iota = cst[:, C_IOTA:C_IOTA + M_E].unsqueeze(1).to_broadcast([P, B, M_E])
            for k in range(M_K):
                p = pr[1 + k]
                link(dve.tensor_reduce(top[:, k, :], p[:], AX, ALU.max))
                link(dve.tensor_tensor(eq[:], p[:], top[:, k, :].unsqueeze(2).to_broadcast([P, B, M_E]), ALU.is_equal))
                link(dve.tensor_tensor(eq[:], eq[:], iota, ALU.mult))
                link(dve.tensor_reduce(ix[:], eq[:], AX, ALU.min))
                link(dve.tensor_tensor(oh[:, k], iota, ix[:].unsqueeze(2).to_broadcast([P, B, M_E]), ALU.is_equal))
                if k == 0:
                    link(dve.scalar_tensor_tensor(pr[2][:], oh[:, 0], -4.0, pr[1][:], ALU.mult, ALU.add))
            for k in range(M_K):
                for b in range(B):
                    dve.tensor_copy(mk[:, k * B + b], oh[:, k, b, :].unsqueeze(2).to_broadcast([P, M_E, M_R])).then_inc(mk_done, 1)
            link(dve.tensor_tensor(tot[:], top[:, 0, :], top[:, 1, :], ALU.add))
            link(dve.reciprocal(tot[:], tot[:]))
            link(dve.tensor_tensor(rw[:], top[:], tot[:].unsqueeze(1).to_broadcast([P, M_K, B]), ALU.mult))
            for k in range(2):
                dve.wait_ge(a_mm, k + 1)
                for e in range(EC):
                    dve.wait_ge(mt_cp, e + 1)
                    dve.tensor_tensor(am[k][:, e, :].rearrange("p (k t) -> p k t", k=M_K), slots(bk[6 + k][:, e * TOK:(e + 1) * TOK]),
                                      mkT[:, e, :].rearrange("p (k t) -> p k t", k=M_K), ALU.mult).then_inc(am_done, 1)
            for f in range(FCH):
                dve.wait_ge(x3_mm, f + 1)
                dve.wait_ge(g_done, f + 1)
                dve.tensor_tensor(x2[:, f, :], g1[f % 2][:], G3[f % 2], ALU.mult).then_inc(x2_done, 1)
            for e in range(EC):
                dve.wait_ge(a2_mm, e + 1)
                dve.tensor_tensor(am[2][:, e, :], bk[6 + e], mkT[:, e, :], ALU.mult).then_inc(a2_done, 1)
            for k in range(M_K):
                for b in range(B):
                    dve.wait_ge(y_mm, k * B + b + 1)
                    link(dve.scalar_tensor_tensor(X[:, b, :], bk[k * B + b][:, 0:D], rw[:, k, b:b + 1], X[:, b, :], ALU.mult, ALU.add))


def _constants():
    import numpy as np
    i = np.arange(P)
    c = np.zeros((P, C_ALL), np.float32)
    c[:, C_ID:C_ID + P] = np.eye(P)
    c[:, C_UP:C_UP + P] = i[:, None] <= i[None, :]
    c[:, C_LOW:C_LOW + P] = i[:, None] > i[None, :]
    c[:, C_CAUSAL:C_CAUSAL + P] = np.where(i[None, :] <= i[:, None], 0.0, MASKED)
    for level in range(LEVELS):
        w = 1 << level
        m = (i[:, None] // (2 * w) == i[None, :] // (2 * w)) & (i[:, None] // w % 2 == 1) & (i[None, :] // w % 2 == 0)
        c[:, C_LV + level * P:C_LV + (level + 1) * P] = m
        c[:, C_LVT + level * P:C_LVT + (level + 1) * P] = m.T
    inv = (1.0 / 10000.0 ** (np.arange(0, X_CQ, 2, dtype=np.float32) / X_CQ)).astype(np.float32)
    ang = np.repeat(i[:, None].astype(np.float32) * inv[None, :], 2, axis=-1)
    for half in range(2):
        cs = np.cos(ang[:, half * XQ:(half + 1) * XQ]).T
        sn = np.sin(ang[:, half * XQ:(half + 1) * XQ]).T * (-1.0 if half == 0 else 1.0)
        for b in range(B):
            c[0:XQ, C_CQ + half * TOK + b * P:C_CQ + half * TOK + (b + 1) * P] = cs
            c[0:XQ, C_SQ + half * TOK + b * P:C_SQ + half * TOK + (b + 1) * P] = sn
    theta = (1.0 / 10000.0 ** (np.arange(0, E_ROPE, 2, dtype=np.float32) / E_ROPE)).astype(np.float32)
    ang = i[:, None].astype(np.float32) * theta[None, :]
    cs, sn = np.cos(ang).T, np.sin(ang).T
    for b in range(B):
        c[:, C_CE + b * P:C_CE + (b + 1) * P] = np.concatenate([cs] * 4)
        c[:, C_SE + b * P:C_SE + (b + 1) * P] = np.concatenate([-sn, sn, -sn, sn])
    c[:, C_IOTA:C_IOTA + M_E] = np.arange(M_E) - BIG
    inv = (1.0 / 10000.0 ** (np.arange(0, LAT, 2, dtype=np.float32) / LAT)).astype(np.float32)
    ang = np.repeat(np.arange(CTX, dtype=np.float32)[:, None] * inv[None, :], 2, axis=-1)
    cs, sn = np.cos(ang), np.sin(ang)
    sn[:, 0:LAT // 2] = -sn[:, 0:LAT // 2]
    rope = np.stack([cs.reshape(KT, P, LAT).transpose(1, 0, 2), sn.reshape(KT, P, LAT).transpose(1, 0, 2)], 1)
    return c, np.ascontiguousarray(rope.astype(np.float32))


def _kmajor(w):
    k, n = w.shape
    return w.reshape(k // P, P, n).transpose(1, 0, 2)


def kernel(**inputs):
    import numpy as np
    import concourse.bacc as _bacc
    from concourse.bass_utils import run_bass_kernel_spmd as _run

    t = {k: np.asarray(v) for k, v in inputs.items()}
    cst, rope = _constants()
    ctx = t["ctx_512"]
    w = t["L0_attn_W_qkvz"].reshape(G_QK, 6 * P, DC, P)
    conv = t["L0_attn_conv_w"]
    nq = G_QK * G_HD
    conv = np.stack([conv[0:nq].reshape(G_QK, P, TAPS), conv[nq:2 * nq].reshape(G_QK, P, TAPS)]
                    + [conv[2 * nq:].reshape(G_QK, RATIO, P, TAPS)[:, r] for r in range(RATIO)], 2)
    ba = t["L0_attn_W_ba"].reshape(G_QK, 2, RATIO, D).transpose(1, 0, 2, 3).reshape(2 * G_V, D)
    arrays = {
        "x": t["x"], "cst": cst, "rope": rope,
        "a_ctxT": ctx[:, 0:P].transpose(2, 0, 1),
        "a_wq": _kmajor(t["L0_xattn_Wq"].T), "a_wkv": t["L0_xattn_Wkv_expand"].T, "a_wo": _kmajor(t["L0_xattn_Wout"].T),
        "b_slab": np.concatenate([w[:, 0:4 * P].transpose(0, 3, 2, 1).reshape(G_QK, P, DC * 4 * P),
                                  conv.reshape(G_QK, P, 4 * TAPS)], 2),
        "b_wz": w[:, 4 * P:6 * P].transpose(0, 3, 2, 1).reshape(G_QK, P, DC * 2 * P),
        "b_wo": t["L0_attn_W_out"].T.reshape(G_QK, RATIO, P, D).transpose(0, 2, 1, 3).reshape(G_QK, P, RATIO * D),
        "b_wba": _kmajor(ba.T),
        "b_dt": t["L0_attn_dt_bias"].reshape(1, G_V), "b_alog": t["L0_attn_A_log"].reshape(1, G_V),
        "b_norm": t["L0_attn_norm_w"].reshape(P, 1),
        "c_w1": _kmajor(t["L0_ffn_w1"].T), "c_w2": _kmajor(t["L0_ffn_w2"].T),
        "d_ctx": ctx.reshape(B, KT, P, LAT).transpose(2, 1, 0, 3),
        "d_w128": np.concatenate([t["L1_xattn_Wq"].reshape(X_H, X_K, DC, P).transpose(0, 3, 2, 1).reshape(X_H, P, DC * X_K),
                                  t["L1_xattn_w_kc_q"]], 2),
        "d_w64": np.concatenate([t["L1_xattn_W_qr"].transpose(0, 2, 1), t["L1_xattn_W_kr"].transpose(0, 2, 1)], 2),
        "d_wkv": t["L1_xattn_w_kc_kv"].reshape(X_H // 2, 2, X_K, LAT).transpose(1, 3, 0, 2),
        "d_wo": t["L1_xattn_Wo"].T.reshape(X_H, X_K, D).transpose(1, 0, 2),
        "e_wkvd": _kmajor(t["L1_attn_W_kv_down"]), "e_wqd": _kmajor(t["L1_attn_W_q_down"]),
        "e_wkn": t["L1_attn_W_k_nope"], "e_wkr": t["L1_attn_W_k_rope"], "e_wv": t["L1_attn_W_v"],
        "e_wqn": t["L1_attn_W_q_nope"].reshape(2, 96, E_H * E_NOPE).transpose(1, 0, 2),
        "e_wqr": t["L1_attn_W_q_rope"].reshape(2, 96, E_H * E_ROPE).transpose(1, 0, 2),
        "e_wo": t["L1_attn_W_o"].reshape(E_H, P, D).transpose(1, 0, 2),
        "f_wg": _kmajor(t["L1_ffn_Wg"].T),
        "f_w1": _kmajor(t["L1_ffn_W1"].T), "f_w3": _kmajor(t["L1_ffn_W3"].T), "f_w2": _kmajor(t["L1_ffn_W2"].T),
        "f_a1": _kmajor(t["L1_ffn_A1"].reshape(M_E * M_R, D).T), "f_a3": _kmajor(t["L1_ffn_A3"].reshape(M_E * M_R, D).T),
        "f_b1": _kmajor(t["L1_ffn_B1"].transpose(0, 2, 1).reshape(M_E * M_R, M_F)),
        "f_b3": _kmajor(t["L1_ffn_B3"].transpose(0, 2, 1).reshape(M_E * M_R, M_F)),
        "f_a2": _kmajor(t["L1_ffn_A2"].reshape(M_E * M_R, M_F).T),
        "f_b2": _kmajor(t["L1_ffn_B2"].transpose(0, 2, 1).reshape(M_E * M_R, D)),
    }
    nc = _bacc.Bacc("TRN2", target_bir_lowering=False, num_devices=1)
    arrays = {k: np.ascontiguousarray(v) for k, v in arrays.items()}
    a = {k: nc.dram_tensor(f"in_{k}", v.shape, mybir.dt.from_np(v.dtype), kind="ExternalInput").ap()
         for k, v in arrays.items()}
    a["out"] = nc.dram_tensor("out_0", (B, P, D), F32, kind="ExternalOutput").ap()
    build(nc, a, UPTO)
    r = _run(nc, [{f"in_{k}": v for k, v in arrays.items()}], core_ids=[0])
    return r.results[0]["out_0"]


UPTO = 6
```

```python
from contextlib import ExitStack

import concourse.bass as bass
from concourse import mybir

F32 = mybir.dt.float32
BF16 = mybir.dt.bfloat16
U32 = mybir.dt.uint32
ALU = mybir.AluOpType
ACT = mybir.ActivationFunctionType
AX = mybir.AxisListType.X

P = 128
B = 2
D = 256
DC = D // P
TOK = B * P
CTX = 2048
LAT = 64
MASKED = -1e30

A_H, A_HD, A_PAD = 16, 16, 32
G_QK, G_V, G_HD, TAPS = 16, 32, 128, 4
RATIO = G_V // G_QK
PAIRS = G_QK // 2
LEVELS = 7
SLAB = DC * 4 * P + 4 * TAPS
C_IN = 1024
ROUND = 12582912.0
X_H, X_K, X_CQ, X_R = 16, 128, 192, 64
XQ = X_CQ // 2
KT = CTX // P
E_H, E_KV, E_REP, E_NOPE, E_ROPE, E_V = 16, 4, 4, 128, 64, 128
E_QR = 192
M_F, M_E, M_R, M_K = 896, 8, 32, 2
FCH = M_F // P

C_ID = 0
C_UP = 128
C_LOW = 256
C_CAUSAL = 384
C_LV = 512
C_LVT = C_LV + LEVELS * P
C_CQ = C_LVT + LEVELS * P
C_SQ = C_CQ + 2 * TOK
C_CE = C_SQ + 2 * TOK
C_SE = C_CE + TOK
C_IOTA = C_SE + TOK
C_ALL = C_IOTA + M_E
BIG = 1024.0


class Chain:

    def __init__(self, eng, sem):
        self.eng, self.sem, self.n, self.at, self.per = eng, sem, 0, None, 0

    def __call__(self, ins):
        ins.then_inc(self.sem, 1)
        self.n += 1
        self.eng.wait_ge(self.sem, self.n if self.at is None else self.at * self.per + self.n)

    def enter(self, i, first, per):
        self.at, self.per, self.start = i, per, self.n
        self.n -= first * per
        self.shift = first * per

    def leave(self, turns):
        used = self.n + self.shift - self.start
        assert used == self.per, used
        self.n, self.at = self.start + self.per * turns, None


def build(nc, a, upto=6):
    ctx = ExitStack()

    def sem(name):
        return ctx.enter_context(nc.semaphore(name))

    def sb(name, shape, dt=F32):
        return ctx.enter_context(nc.sbuf_tensor(name, shape, dt))

    with ctx:
        bk = [ctx.enter_context(nc.psum_tensor(f"bank{i}", [P, 512], F32))[:] for i in range(4)]
        scores = ctx.enter_context(nc.psum_tensor("scores", [P, 4, 512], F32))
        bk += [scores[:, i, :] for i in range(4)]
        X = sb("X", [P, B, D])
        cst = sb("cst", [P, C_ALL])
        xn = sb("xn", [P, B, D])
        xnT = sb("xnT", [P, DC, TOK])
        stats = sb("stats", [P, B, 6])
        mv = sb("mv", [P, B, 2])
        veps = sb("veps", [P, B])
        rstd = sb("rstd", [P, B])
        mhalf = sb("mhalf", [P, 8])
        ones = sb("ones", [P, P])
        ident = cst[:, C_ID:C_ID + P]

        env = dict(locals())
        s = dict(
            x_in=sem("x_in"), cst_in=sem("cst_in"), ones_set=sem("ones_set"),
            ln_var=sem("ln_var"), ln_rstd=sem("ln_rstd"), ln_xn=sem("ln_xn"),
            ln_tr=sem("ln_tr"), ln_xT=sem("ln_xT"), dve_chain=sem("dve_chain"), act_chain=sem("act_chain"), pool_chain=sem("pool_chain"),
            out_done=sem("out_done"),
        )
        env["s"] = s
        env["dve_link"] = Chain(nc.vector, s["dve_chain"])
        env["act_link"] = Chain(nc.scalar, s["act_chain"])
        env["pool_link"] = Chain(nc.gpsimd, s["pool_chain"])

        def turned(n):
            return n + 1 - (n > 2)

        def ln_vector(n):
            link = env["dve_link"]
            for b in range(B):
                link(nc.vector.bn_stats(stats[:, b, :], X[:, b, :]))
            for b in range(B):
                link(nc.vector.bn_aggr(mv[:, b, :], stats[:, b, :]))
            nc.vector.tensor_scalar(veps[:], mv[:, :, 1], 1e-5, None, ALU.add).then_inc(s["ln_var"], 1)
            nc.vector.wait_ge(s["ln_rstd"], n + 1)
            for b in range(B):
                nc.vector.tensor_scalar(xn[:, b, :], X[:, b, :], mv[:, b, 0:1], rstd[:, b:b + 1],
                                        ALU.subtract, ALU.mult).then_inc(s["ln_xn"], 1)

        def ln_gpsimd(n):
            nc.gpsimd.wait_ge(s["ln_var"], n + 1)
            nc.gpsimd.tensor_tensor(rstd[:], veps[:], mhalf[:, 0:B], ALU.pow).then_inc(s["ln_rstd"], 1)

        def ln_tensor(n):
            nc.tensor.wait_ge(s["ln_xn"], B * (n + 1))
            for c in range(DC):
                for b in range(B):
                    last = nc.tensor.transpose(bk[7][:, c * TOK + b * P:c * TOK + (b + 1) * P],
                                               xn[:, b, c * P:(c + 1) * P], ident)
            last.then_inc(s["ln_tr"], 1)

        def ln_scalar(n):
            nc.scalar.wait_ge(s["ln_tr"], turned(n))
            nc.scalar.copy(xnT[:].rearrange("p c t -> p (c t)"), bk[7]).then_inc(s["ln_xT"], 1)

        env.update(ln_vector=ln_vector, ln_gpsimd=ln_gpsimd, ln_tensor=ln_tensor, ln_scalar=ln_scalar, turned=turned)

        with nc.Block() as block:
            @block.sync
            def _(sp):
                sp.dma_start(X[:], a["x"].rearrange("b t d -> t b d")).then_inc(s["x_in"], 16)
                sp.dma_start(cst[:], a["cst"]).then_inc(s["cst_in"], 16)
                sp.wait_ge(s["x_in"], 16)
                sp.wait_ge(s["cst_in"], 16)

            @block.vector
            def _(dve):
                dve.memset(ones[:], 1.0)
                dve.memset(mhalf[:], -0.5)

        stages = [stage_a, stage_b, stage_c, stage_d, stage_e, stage_f][:upto]
        for st in stages:
            with ExitStack() as own:
                env["used"] = []
                st(nc, a, env, own)
                with nc.Block() as block:
                    @block.vector
                    def _(dve):
                        for used in env["used"]:
                            dve.sem_clear(used)

        with nc.Block() as block:
            @block.sync
            def _(sp):
                sp.dma_start(a["out"].rearrange("b t d -> t b d"), X[:]).then_inc(s["out_done"], 16)
                sp.wait_ge(s["out_done"], 16)


def stage_a(nc, a, env, own):
    X, xnT, bk, ident, cst, s = (env[k] for k in ("X", "xnT", "bk", "ident", "cst", "s"))
    link = env["dve_link"]

    def sb(name, shape, dt=F32):
        return own.enter_context(nc.sbuf_tensor("a_" + name, shape, dt))

    def sem(name):
        env["used"].append(own.enter_context(nc.semaphore("a_" + name)))
        return env["used"][-1]

    HG = A_H // 4
    ctxT = sb("ctxT", [LAT, B, P])
    wq = sb("wq", [P, DC, D])
    wkv = sb("wkv", [LAT, 2 * D])
    wo = sb("wo", [P, DC, D])
    wq_pad = sb("wq_pad", [P, DC, A_H, A_PAD])
    wk_pad = sb("wk_pad", [LAT, A_H, A_PAD])
    qT = sb("qT", [P, HG, TOK])
    kT = sb("kT", [P, HG, TOK])
    v = sb("v", [P, B, D])
    S = sb("S", [P, B, 4, 4, P])
    nmax = sb("nmax", [P, B, 4, 4])
    sums = sb("sums", [P, B, 4, 4])
    rec = sb("rec", [P, B, 4, 4])
    PT = sb("PT", [P, B, 4, 4, P])
    o = sb("o", [P, B, D])
    oT = sb("oT", [P, DC, TOK])
    loads, padded, kq_mm, kq_cp, v_mm, v_cp = (sem(n) for n in "loads padded kq_mm kq_cp v_mm v_cp".split())
    sc_mm, sc_masked, nmax_done, exp_done, tr_mm, tr_cp = (sem(n) for n in "sc_mm sc_masked nmax_done exp_done tr_mm tr_cp".split())
    rec_done, pv_mm, o_cp, ot_mm, ot_cp, y_mm = (sem(n) for n in "rec_done pv_mm o_cp ot_mm ot_cp y_mm".split())

    with nc.Block() as block:
        @block.sync
        def _(sp):
            for t, d in ((ctxT, "a_ctxT"), (wq, "a_wq"), (wkv, "a_wkv"), (wo, "a_wo")):
                sp.dma_start(t[:], a[d]).then_inc(loads, 16)

        @block.gpsimd
        def _(pool):
            pool.memset(wq_pad[:], 0.0).then_inc(padded, 1)
            pool.memset(wk_pad[:], 0.0).then_inc(padded, 1)
            env["ln_gpsimd"](0)
            pool.wait_ge(padded, 2)
            pool.wait_ge(loads, 64)
            pool.tensor_copy(wk_pad[:, :, 0:A_HD], wkv[:, 0:D].rearrange("p (h e) -> p h e", h=A_H)).then_inc(padded, 1)
            for c in range(DC):
                pool.tensor_copy(wq_pad[:, c, :, 0:A_HD],
                                 wq[:, c, :].rearrange("p (h e) -> p h e", h=A_H)).then_inc(padded, 1)

        @block.tensor
        def _(pe):
            env["ln_tensor"](0)
            pe.wait_ge(loads, 64)
            for b in range(B):
                last = pe.matmul(bk[0][:, b * D:(b + 1) * D], ctxT[:, b, :], wkv[:, D:2 * D], start=True, stop=True)
            last.then_inc(v_mm, 1)
            pe.wait_ge(padded, 5)
            for m in range(HG):
                last = pe.matmul(bk[1 + m // 2][:, (m % 2) * TOK:(m % 2 + 1) * TOK],
                                 wk_pad[:, 4 * m:4 * m + 4, :].rearrange("p h e -> p (h e)"),
                                 ctxT[:].rearrange("p b t -> p (b t)"), start=True, stop=True)
                if m % 2:
                    last.then_inc(kq_mm, 1)
            pe.wait_ge(s["ln_xT"], env["turned"](0))
            for m in range(HG):
                for c in range(DC):
                    last = pe.matmul(bk[3 + m // 2][:, (m % 2) * TOK:(m % 2 + 1) * TOK],
                                     wq_pad[:, c, 4 * m:4 * m + 4, :].rearrange("p h e -> p (h e)"),
                                     xnT[:, c, :], start=(c == 0), stop=(c == DC - 1))
                if m % 2:
                    last.then_inc(kq_mm, 1)
            pe.wait_ge(kq_cp, 4)
            pe.wait_ge(v_cp, 1)
            for b in range(B):
                for j in range(4):
                    rows = slice(32 * j, 32 * j + 32)
                    for m in range(HG):
                        last = pe.matmul(bk[4 * b + j][:, m * P:(m + 1) * P], qT[rows, m, b * P:(b + 1) * P],
                                         kT[rows, m, b * P:(b + 1) * P], start=True, stop=True)
                    last.then_inc(sc_mm, 1)
            for b in range(B):
                for j in range(4):
                    n = 4 * b + j
                    pe.wait_ge(exp_done, n + 1)
                    for m in range(HG):
                        last = pe.transpose(bk[n][:, m * P:(m + 1) * P], S[:, b, j, m, :], ident)
                    last.then_inc(tr_mm, 1)
            for b in range(B):
                pe.wait_ge(tr_cp, 4 * b + 4)
                for h in range(A_H):
                    j, m = h % 4, h // 4
                    last = pe.matmul(bk[4 * b][:, h * A_HD:(h + 1) * A_HD], PT[:, b, j, m, :],
                                     v[:, b, h * A_HD:(h + 1) * A_HD], start=True, stop=True)
                last.then_inc(pv_mm, 1)
            pe.wait_ge(o_cp, 2)
            for c in range(DC):
                for b in range(B):
                    last = pe.transpose(bk[1][:, c * TOK + b * P:c * TOK + (b + 1) * P], o[:, b, c * P:(c + 1) * P], ident)
            last.then_inc(ot_mm, 1)
            pe.wait_ge(ot_cp, 1)
            for b in range(B):
                for c in range(DC):
                    last = pe.matmul(bk[2][:, b * D:(b + 1) * D], oT[:, c, b * P:(b + 1) * P], wo[:, c, :],
                                     start=(c == 0), stop=(c == DC - 1))
            last.then_inc(y_mm, 1)

        @block.scalar
        def _(act):
            env["ln_scalar"](0)
            for n in range(4):
                act.wait_ge(kq_mm, n + 1)
                dst = (kT if n < 2 else qT)[:, 2 * (n % 2):2 * (n % 2) + 2, :].rearrange("p m t -> p (m t)")
                act.copy(dst, bk[1 + n]).then_inc(kq_cp, 1)
            for b in range(B):
                for j in range(4):
                    act.wait_ge(nmax_done, 4 * b + j + 1)
                    for m in range(HG):
                        last = act.activation(S[:, b, j, m, :], S[:, b, j, m, :], ACT.Exp,
                                              bias=nmax[:, b, j, m:m + 1], accum_out=sums[:, b, j, m:m + 1])
                    last.then_inc(exp_done, 1)
            act.wait_ge(ot_mm, 1)
            act.copy(oT[:].rearrange("p c t -> p (c t)"), bk[1]).then_inc(ot_cp, 1)

        @block.vector
        def _(dve):
            env["ln_vector"](0)
            dve.wait_ge(v_mm, 1)
            dve.tensor_copy(v[:].rearrange("p b d -> p (b d)"), bk[0]).then_inc(v_cp, 1)
            causal = cst[:, C_CAUSAL:C_CAUSAL + P].unsqueeze(1).to_broadcast([P, 4, P])
            for b in range(B):
                for j in range(4):
                    n = 4 * b + j
                    dve.wait_ge(sc_mm, n + 1)
                    dve.scalar_tensor_tensor(S[:, b, j], bk[n].rearrange("p (m k) -> p m k", m=4), A_HD ** -0.5, causal,
                                             ALU.mult, ALU.add).then_inc(sc_masked, 1)
                    dve.wait_ge(sc_masked, n + 1)
                    dve.tensor_reduce(nmax[:, b, j, :], S[:, b, j], AX, ALU.max, negate=True).then_inc(nmax_done, 1)
            for b in range(B):
                for j in range(4):
                    n = 4 * b + j
                    dve.wait_ge(tr_mm, n + 1)
                    dve.tensor_copy(PT[:, b, j].rearrange("p m q -> p (m q)"), bk[n]).then_inc(tr_cp, 1)
                dve.reciprocal(rec[:, b], sums[:, b]).then_inc(rec_done, 1)
                dve.wait_ge(rec_done, b + 1)
                dve.wait_ge(pv_mm, b + 1)
                dve.tensor_tensor(o[:, b, :].rearrange("p (m j e) -> p m j e", m=4, j=4),
                                  bk[4 * b][:, 0:D].rearrange("p (m j e) -> p m j e", m=4, j=4),
                                  rec[:, b].rearrange("p j m -> p m j").unsqueeze(3).to_broadcast([P, 4, 4, A_HD]),
                                  ALU.mult).then_inc(o_cp, 1)
            dve.wait_ge(y_mm, 1)
            link(dve.tensor_tensor(X[:].rearrange("p b d -> p (b d)"), X[:].rearrange("p b d -> p (b d)"), bk[2], ALU.add))


def stage_b(nc, a, env, own):
    X, xnT, bk, ident, cst, s, mhalf, ones = (env[k] for k in ("X", "xnT", "bk", "ident", "cst", "s", "mhalf", "ones"))
    vlink, plink, alink = env["dve_link"], env["pool_link"], env["act_link"]
    INV = G_HD ** -0.5
    EPS = 1e-6
    HB = 2 * G_V
    LAST = LEVELS - 1

    def sb(name, shape, dt=F32):
        return own.enter_context(nc.sbuf_tensor("b_" + name, shape, dt))

    def two(name, shape):
        return [sb(f"{name}{x}", shape) for x in range(2)]

    def sem(name):
        env["used"].append(own.enter_context(nc.semaphore("b_" + name)))
        return env["used"][-1]

    slab, wz, wo = two("slab", [P, SLAB]), two("wz", [P, DC, 2 * P]), two("wo", [P, RATIO, D])
    wba = sb("wba", [P, DC, HB])
    dtb, alog, normw = sb("dtb", [P, G_V]), sb("alog", [P, G_V]), sb("normw", [P, 1])
    DT = sb("DT", [P, G_QK, 4 * P])
    beta = sb("beta", [P, G_QK, B, RATIO])
    gl = sb("gl", [P, G_QK, B, RATIO])
    t1, t2, t3 = sb("t1", [P, B, G_V]), sb("t2", [P, B, G_V]), sb("t3", [P, B, G_V])
    Gm = [sb(f"Gm{k}", [P, 4, P]) for k in range(4)]
    cpad = two("cpad", [P, 4, B, TAPS - 1 + P])
    yc, qkv = two("yc", [P, 4, B, P]), two("qkv", [P, 4, B, P])
    ssq, square = sb("ssq", [P, 2, 2, B]), two("square", [P, 4, P])
    Np, At, T, TT, Ys = two("Np", [P, 4, P]), two("At", [P, 4, P]), two("T", [P, 4, P]), two("TT", [P, 4, P]), two("Ys", [P, 4, P])
    Vh, vn, sz, hs = two("Vh", [P, 4, P]), two("vn", [P, 4, P]), two("sz", [P, 4, P]), two("hs", [P, 4, P])
    hT = two("hT", [P, 4, P])
    I4 = sb("I4", [P, 4, P])
    carrier = sb("carrier", [P, 2 * LEVELS])
    m8, r8 = sb("m8", [P, 2, 2, B]), sb("r8", [P, 2, 2, B])
    r2, vi = sb("r2", [P, 2, B]), sb("vi", [P, 2, B])
    rqs, rq2 = sb("rqs", [P, 2, B]), sb("rq2", [P, 2, B])
    nb = sb("nb", [P, 2, B, RATIO])
    so, hv, hr, hsc = two("so", [P, 4]), two("hv", [P, 4]), two("hr", [P, 4]), two("hsc", [P, 4])

    w_in, small_in = sem("w_in"), sem("small_in")
    slab_in, wz_in, wo_in = [sem(f"slab_in{x}") for x in range(2)], [sem(f"wz_in{x}") for x in range(2)], [sem(f"wo_in{x}") for x in range(2)]
    (i4_set, ba_mm, ba_act, ba_dve, gl_done, gm_done, dec_mm, dec_exp, dec_done, proj_mm, pads_set, pads_cp, conv_step,
     silu_done, sq_done, kk_mm, vt_mm, z_mm, qk_mm, sz_done, vh_done, norm_var, norm_pow, norm_done, np_done, at_done,
     mt_mm, t_reset, t_upd, tt_last, y_mm, y_cp, tr_mm, tt_cp, zz_mm, zt_mm, tv_mm, vn_done, o_mm, so_done, h_var, h_pow, h_done,
     ht_mm, ht_cp, yp_mm, x_acc) = (sem(n) for n in (
        "i4_set ba_mm ba_act ba_dve gl_done gm_done dec_mm dec_exp dec_done proj_mm pads_set pads_cp conv_step "
        "silu_done sq_done kk_mm vt_mm z_mm qk_mm sz_done vh_done norm_var norm_pow norm_done np_done at_done "
        "mt_mm t_reset t_upd tt_last y_mm y_cp tr_mm tt_cp zz_mm zt_mm tv_mm vn_done o_mm so_done h_var h_pow h_done "
        "ht_mm ht_cp yp_mm x_acc").split())

    PJ, PZ, PY, YZ, ZT = [bk[0], bk[1]], bk[2], bk[3], [bk[4], bk[6]], [bk[5], bk[7]]
    UP4 = cst[:, C_UP:C_UP + P].unsqueeze(1).to_broadcast([P, 4, P])

    def quad(ap):
        return ap.rearrange("p (u k) -> p u k", u=4)

    def mask(base, level):
        m = cst[:, base + level * P:base + (level + 1) * P].bitcast(U32)
        return m.unsqueeze(1).to_broadcast([P, 4, P])

    def loop(eng, body):
        body(0, True)
        with eng.Fori(1, PAIRS - 1) as i:
            body(i, True)
        body(PAIRS - 1, False)

    with nc.Block() as block:
        @block.sync
        def _(sp):
            sp.dma_start(wba[:], a["b_wba"]).then_inc(w_in, 16)
            sp.dma_start(dtb[:], a["b_dt"].to_broadcast([P, G_V])).then_inc(small_in, 16)
            sp.dma_start(alog[:], a["b_alog"].to_broadcast([P, G_V])).then_inc(small_in, 16)
            sp.dma_start(normw[:], a["b_norm"]).then_inc(small_in, 16)
            for x in range(2):
                sp.dma_start(slab[x][:], a["b_slab"][x]).then_inc(slab_in[x], 16)
                sp.dma_start(wz[x][:].rearrange("p c n -> p (c n)"), a["b_wz"][x]).then_inc(wz_in[x], 16)
                sp.dma_start(wo[x][:].rearrange("p r n -> p (r n)"), a["b_wo"][x]).then_inc(wo_in[x], 16)

            def next_slabs(i):
                for x in range(2):
                    sp.wait_ge(conv_step, 32 * i + 16 * x + 16)
                    sp.dma_start(slab[x][:], a["b_slab"][bass.ds(2 * i + 2 + x, 1)].rearrange("g p n -> (g p) n")).then_inc(slab_in[x], 16)

            def next_wz(i, x):
                sp.wait_ge(z_mm, 2 * i + x + 1)
                sp.dma_start(wz[x][:].rearrange("p c n -> p (c n)"),
                             a["b_wz"][bass.ds(2 * i + 2 + x, 1)].rearrange("g p n -> (g p) n")).then_inc(wz_in[x], 16)

            def next_wo(i):
                sp.wait_ge(yp_mm, i)
                for x in range(2):
                    sp.dma_start(wo[x][:].rearrange("p r n -> p (r n)"),
                                 a["b_wo"][bass.ds(2 * i + x, 1)].rearrange("g p n -> (g p) n")).then_inc(wo_in[x], 16)

            next_slabs(0)
            next_wz(0, 0)
            next_wz(0, 1)
            with sp.Fori(1, PAIRS - 1) as i:
                next_slabs(i)
                next_wz(i, 0)
                next_wo(i)
                next_wz(i, 1)
            next_wo(PAIRS - 1)

        @block.gpsimd
        def _(pool):
            for x in range(2):
                pool.memset(cpad[x][:], 0.0).then_inc(pads_set, 1)
            pool.wait_ge(s["cst_in"], 16)
            for u in range(4):
                pool.tensor_copy(I4[:, u, :], ident).then_inc(i4_set, 1)
            env["ln_gpsimd"](1)
            pool.wait_ge(i4_set, 4)
            for x in range(2):
                pool.tensor_copy(T[x][:], I4[:]).then_inc(t_reset, 1)

            def causal(i, x):
                pool.wait_ge(dec_exp, 2 * i + x + 1)
                t = DT[:, bass.ds(2 * i + x, 1), :].rearrange("p g (u k) -> p (g u) k", u=4)
                pool.tensor_tensor(t, t, UP4, ALU.mult).then_inc(dec_done, 1)

            with pool.Fori(0, PAIRS) as i:
                for x in range(2):
                    causal(i, x)

            def norm(i):
                pool.wait_ge(norm_var, i + 1)
                pool.tensor_tensor(r8[:].rearrange("p x q b -> p (x q b)"), m8[:].rearrange("p x q b -> p (x q b)"),
                                   mhalf[:, 0:8], ALU.pow).then_inc(norm_pow, 1)

            norm(0)

            def body(i, more):
                if more:
                    for x in range(2):
                        pool.wait_ge(tr_mm, 12 * i + 2 * LAST - 1 + x)
                        pool.tensor_tensor(T[x][:], I4[:], I4[:], ALU.mult).then_inc(t_reset, 1)
                    norm(i + 1)
                for x in range(2):
                    pool.wait_ge(h_var, 2 * i + x + 1)
                    pool.tensor_tensor(hr[x][:], hv[x][:], mhalf[:, 0:4], ALU.pow).then_inc(h_pow, 1)

            loop(pool, body)

        @block.tensor
        def _(pe):
            env["ln_tensor"](1)
            pe.wait_ge(w_in, 16)
            pe.wait_ge(s["ln_xT"], env["turned"](1))
            for b in range(B):
                for c in range(DC):
                    last = pe.matmul(bk[0][:, b * HB:(b + 1) * HB], xnT[:, c, b * P:(b + 1) * P], wba[:, c, :],
                                     start=(c == 0), stop=(c == DC - 1))
            last.then_inc(ba_mm, 1)
            def decays(f):
                for k in range(4):
                    pe.wait_ge(gm_done, 4 * f + k + 1)
                    if not isinstance(f, int):
                        pe.wait_ge(dec_exp, 4 * f + k - 3)
                    pe.matmul(bk[4 + k], cst[:, C_LOW:C_LOW + P], Gm[k][:].rearrange("p u k -> p (u k)"),
                              start=True, stop=True).then_inc(dec_mm, 1)

            def project(i, x, chunks=range(4)):
                if 0 in chunks:
                    pe.wait_ge(slab_in[x], 16 * i + 16)
                    if x or not isinstance(i, int) or i > 0:
                        pe.wait_ge(pads_cp, 2 * i + x)
                for ch in chunks:
                    for c in range(DC):
                        last = pe.matmul(PJ[ch // 2][:, ch % 2 * TOK:(ch % 2 + 1) * TOK],
                                         slab[x][:, (c * 4 + ch) * P:(c * 4 + ch + 1) * P], xnT[:, c, :],
                                         start=(c == 0), stop=(c == DC - 1))
                if 3 in chunks:
                    last.then_inc(proj_mm, 1)

            def squares(i):
                for x in range(2):
                    pe.wait_ge(silu_done, 2 * i + x + 1)
                    for q in range(2):
                        for b in range(B):
                            n = 2 * q + b
                            last = pe.transpose([PZ, PY][x][:, n * P:(n + 1) * P], qkv[x][:, q, b, :], ident)
                    last.then_inc(qk_mm, 1)

            def key_products(i, x):
                for b in range(B):
                    last = pe.matmul(PJ[x][:, b * 2 * P:(b + 1) * 2 * P].rearrange("p (q k) -> p q k", q=2),
                                     qkv[x][:, 1, b, :], qkv[x][:, 0:2, b, :], start=True, stop=True)
                last.then_inc(kk_mm, 1)

            def gate(i, x):
                pe.wait_ge(wz_in[x], 16 * i + 16)
                if x:
                    pe.wait_ge(vh_done, 2 * i + 2)
                else:
                    pe.wait_ge(sq_done, i + 1)
                for b in range(B):
                    for c in range(DC):
                        last = pe.matmul(PZ[:, b * 2 * P:(b + 1) * 2 * P], xnT[:, c, b * P:(b + 1) * P], wz[x][:, c, :],
                                         start=(c == 0), stop=(c == DC - 1))
                last.then_inc(z_mm, 1)

            def values(i, x):
                if x:
                    pe.wait_ge(vh_done, 2 * i + 1)
                else:
                    pe.wait_ge(sz_done, 2 * i + 1)
                for b in range(B):
                    for r in range(RATIO):
                        u = b * RATIO + r
                        last = pe.transpose(PZ[:, u * P:(u + 1) * P], qkv[x][:, 2 + r, b, :], ident)
                last.then_inc(vt_mm, 1)

            def turn_m(i):
                for x in range(2):
                    pe.wait_ge(np_done, 2 * i + x + 1)
                    for u in range(4):
                        last = pe.transpose(YZ[x][:, u * P:(u + 1) * P], Np[x][:, u, :], ident)
                    last.then_inc(mt_mm, 1)

            def turn_h(i):
                for x in range(2):
                    pe.wait_ge(h_done, 2 * i + x + 1)
                    for u in range(4):
                        last = pe.transpose(ZT[x][:, u * P:(u + 1) * P], hs[x][:, u, :], ident)
                    last.then_inc(ht_mm, 1)

            def y_out(i):
                pe.wait_ge(ht_cp, 2 * i + 2)
                for x in range(2):
                    pe.wait_ge(wo_in[x], 16 * i + 16)
                for b in range(B):
                    for x in range(2):
                        for r in range(RATIO):
                            last = pe.matmul(PY[:, b * D:(b + 1) * D], hT[x][:, b * RATIO + r, :], wo[x][:, r, :],
                                             start=(x + r == 0), stop=(x + r == 2))
                last.then_inc(yp_mm, 1)

            pe.wait_ge(ba_dve, 1)
            project(0, 0)
            decays(0)
            project(0, 1)
            with pe.Fori(1, G_QK // 4) as f:
                decays(f)
            squares(0)
            for x in range(2):
                key_products(0, x)
            pe.wait_ge(dec_exp, 2 * PAIRS)
            turn_m(0)

            def body(i, more):
                again = not isinstance(i, int) or i > 0
                for lv in range(1, LEVELS):
                    def level_y(x):
                        pe.wait_ge(t_upd, 12 * i + 2 * (lv - 1) + x + 1)
                        for u in range(4):
                            last = pe.matmul(YZ[x][:, u * P:(u + 1) * P], Np[x][:, u, :], T[x][:, u, :], start=True, stop=True)
                        last.then_inc(y_mm, 1)

                    def level_turn(x):
                        if lv == 1 and again:
                            pe.wait_ge(ht_cp, 2 * i + x - 1)
                        for u in range(4):
                            last = pe.transpose(ZT[x][:, u * P:(u + 1) * P], T[x][:, u, :], ident)
                        last.then_inc(tr_mm, 1)

                    if lv == 1:
                        level_y(0)
                        level_y(1)
                        if more:
                            pe.wait_ge(at_done, 2 * i + 2)
                            project(i + 1, 0, (0, 1))
                        if again:
                            turn_h(i - 1)
                        if more:
                            project(i + 1, 0, (2, 3))
                        level_turn(0)
                        level_turn(1)
                        gate(i, 0)
                    else:
                        for x in range(2):
                            level_y(x)
                            level_turn(x)
                    if lv in (2, 3):
                        values(i, lv - 2)
                    if lv == 2 and more:
                        project(i + 1, 1)
                    if lv == 4 and again:
                        y_out(i - 1)
                    if lv == 5:
                        gate(i, 1)
                    for x in range(2):
                        pe.wait_ge(y_cp, 12 * i + 2 * (lv - 1) + x + 1)
                        pe.wait_ge(tt_cp, 12 * i + 2 * (lv - 1) + x + 1)
                        if lv < LAST:
                            for u in range(4):
                                last = pe.matmul(YZ[x][:, u * P:(u + 1) * P], TT[x][:, u, :], Ys[x][:, u, :], start=True, stop=True)
                            last.then_inc(zz_mm, 1)
                        else:
                            for u in range(4):
                                last = pe.matmul(YZ[x][:, u * P:(u + 1) * P], Ys[x][:, u, :], TT[x][:, u, :], start=True, stop=True)
                            last.then_inc(zt_mm, 1)
                if more:
                    if again:
                        pe.wait_ge(x_acc, i)
                    pe.wait_ge(sz_done, 2 * i + 2)
                    squares(i + 1)
                for x in range(2):
                    pe.wait_ge(tt_last, 2 * i + x + 1)
                    for u in range(4):
                        last = pe.matmul(YZ[x][:, u * P:(u + 1) * P], TT[x][:, u, :], Vh[x][:, u, :], start=True, stop=True)
                    last.then_inc(tv_mm, 1)
                if more:
                    pe.wait_ge(pads_cp, 2 * i + 4)
                    for x in range(2):
                        key_products(i + 1, x)
                for x in range(2):
                    pe.wait_ge(vn_done, 2 * i + x + 1)
                    for u in range(4):
                        last = pe.matmul(ZT[x][:, u * P:(u + 1) * P], At[x][:, u, :], vn[x][:, u, :], start=True, stop=True)
                    last.then_inc(o_mm, 1)
                if more:
                    turn_m(i + 1)

            loop(pe, body)
            turn_h(PAIRS - 1)
            pe.wait_ge(x_acc, PAIRS - 1)
            y_out(PAIRS - 1)

        @block.scalar
        def _(act):
            env["ln_scalar"](1)
            act.wait_ge(small_in, 48)
            act.activation(alog[:], alog[:], ACT.Exp).then_inc(ba_act, 1)
            act.wait_ge(ba_mm, 1)
            act.activation(t1[:], bk[0][:, 0:B * HB].rearrange("p (b n) -> p b n", b=B)[:, :, 0:G_V], ACT.Exp, scale=-1.0).then_inc(ba_act, 1)
            act.wait_ge(ba_dve, 1)
            alink(act.activation(t3[:], t2[:], ACT.Abs))
            alink(act.activation(t3[:], t3[:], ACT.Exp, scale=-1.0))
            act.activation(t3[:], t3[:], ACT.Ln, bias=1.0).then_inc(ba_act, 1)
            def pads(i, x):
                act.wait_ge(proj_mm, 2 * i + x + 1)
                for k in range(2):
                    last = act.copy(cpad[x][:, 2 * k:2 * k + 2, :, TAPS - 1:].rearrange("p c b t -> p (c b) t"),
                                    PJ[k].rearrange("p (c t) -> p c t", t=P))
                last.then_inc(pads_cp, 1)

            def silu(i, x):
                act.wait_ge(conv_step, 32 * i + 16 * x + 16)
                act.activation(qkv[x][:].rearrange("p c b t -> p (c b t)"), yc[x][:].rearrange("p c b t -> p (c b t)"),
                               ACT.Silu).then_inc(silu_done, 1)

            def squares(i):
                for x in range(2):
                    act.wait_ge(qk_mm, 2 * i + x + 1)
                    for q in range(2):
                        for b in range(B):
                            n = 2 * q + b
                            last = act.activation(square[x][:, n, :], [PZ, PY][x][:, n * P:(n + 1) * P], ACT.Square,
                                                  accum_out=ssq[:, x, q, b:b + 1])
                last.then_inc(sq_done, 1)

            def gates(i, x):
                act.wait_ge(z_mm, 2 * i + x + 1)
                act.activation(sz[x][:].rearrange("p u k -> p (u k)"), PZ, ACT.Silu).then_inc(sz_done, 1)

            def values(i, x):
                if x == 0:
                    act.wait_ge(norm_done, i + 1)
                act.wait_ge(vt_mm, 2 * i + x + 1)
                for b in range(B):
                    last = act.activation(Vh[x][:, b * RATIO:(b + 1) * RATIO, :],
                                          quad(PZ)[:, b * RATIO:(b + 1) * RATIO, :], ACT.Copy, scale=vi[:, x, b:b + 1])
                last.then_inc(vh_done, 1)

            def turn_h(i):
                for x in range(2):
                    act.wait_ge(ht_mm, 2 * i + x + 1)
                    act.activation(hT[x][:], quad(ZT[x]), ACT.Copy, scale=normw[:, 0:1]).then_inc(ht_cp, 1)

            act.wait_ge(pads_set, 2)
            def decays(f):
                for k in range(4):
                    act.wait_ge(dec_mm, 4 * f + k + 1)
                    act.activation(DT[:, bass.ds(4 * f + k, 1), :].rearrange("p g k -> p (g k)"), bk[4 + k], ACT.Exp).then_inc(dec_exp, 1)

            pads(0, 0)
            decays(0)
            pads(0, 1)
            with act.Fori(1, G_QK // 4) as f:
                decays(f)
            silu(0, 0)
            silu(0, 1)
            squares(0)

            def body(i, more):
                again = not isinstance(i, int) or i > 0
                for lv in range(1, LEVELS):
                    def level_y(x):
                        act.wait_ge(y_mm, 12 * i + 2 * (lv - 1) + x + 1)
                        act.copy(Ys[x][:], quad(YZ[x])).then_inc(y_cp, 1)

                    def level_turn(x):
                        act.wait_ge(tr_mm, 12 * i + 2 * (lv - 1) + x + 1)
                        act.copy(TT[x][:], quad(ZT[x])).then_inc(tt_cp, 1)

                    if lv == 1:
                        level_y(0)
                        level_y(1)
                        if again:
                            turn_h(i - 1)
                        level_turn(0)
                        level_turn(1)
                        gates(i, 0)
                    else:
                        for x in range(2):
                            level_y(x)
                            level_turn(x)
                    if lv in (2, 3):
                        values(i, lv - 2)
                    if lv == 5:
                        gates(i, 1)
                    if more and lv in (1, 2):
                        pads(i + 1, lv - 1)
                    if more and lv in (4, 6):
                        silu(i + 1, lv // 2 - 2)
                if more:
                    squares(i + 1)
                for x in range(2):
                    act.wait_ge(o_mm, 2 * i + x + 1)
                    for u in range(4):
                        last = act.activation(Ys[x][:, u, :], quad(ZT[x])[:, u, :], ACT.Square, accum_out=so[x][:, u:u + 1])
                    last.then_inc(so_done, 1)

            loop(act, body)
            turn_h(PAIRS - 1)

        @block.vector
        def _(dve):
            env["ln_vector"](1)
            dve.wait_ge(ba_act, 1)
            vlink(dve.tensor_scalar(alog[:], alog[:], -1.0, None, ALU.mult))
            dve.wait_ge(ba_act, 2)
            ba = bk[0][:, 0:B * HB].rearrange("p (b n) -> p b n", b=B)
            dve.tensor_tensor(t2[:], ba[:, :, G_V:HB], dtb[:].unsqueeze(1).to_broadcast([P, B, G_V]), ALU.add).then_inc(ba_dve, 1)
            vlink(dve.tensor_scalar(t1[:], t1[:], 1.0, None, ALU.add))
            vlink(dve.reciprocal(t1[:], t1[:]))
            for b in range(B):
                vlink(dve.tensor_scalar(beta[:, :, b, :], t1[:, b, :].rearrange("p (g r) -> p g r", r=RATIO), -INV * INV, None, ALU.mult))
            dve.wait_ge(ba_act, 3)
            vlink(dve.scalar_tensor_tensor(t3[:], t2[:], 0.0, t3[:], ALU.max, ALU.add))
            for b in range(B):
                dve.tensor_tensor(gl[:, :, b, :], t3[:, b, :].rearrange("p (g r) -> p g r", r=RATIO),
                                  alog[:].rearrange("p (g r) -> p g r", r=RATIO), ALU.mult).then_inc(gl_done, 1)
            dve.wait_ge(gl_done, 2)
            flat = gl[:].rearrange("p g b r -> p (g b r)")

            def decays(f):
                for k in range(4):
                    if not isinstance(f, int):
                        dve.wait_ge(dec_mm, 4 * f + k - 3)
                    dve.tensor_tensor(Gm[k][:], UP4, flat[:, bass.ds(16 * f + 4 * k, 4)].unsqueeze(2).to_broadcast([P, 4, P]),
                                      ALU.mult).then_inc(gm_done, 1)

            def conv(i, x, taps=range(TAPS)):
                if 0 in taps:
                    dve.wait_ge(pads_cp, 2 * i + x + 1)
                for n in taps:
                    for ch in range(4):
                        w = slab[x][:, DC * 4 * P + ch * TAPS + n:DC * 4 * P + ch * TAPS + n + 1]
                        src = cpad[x][:, ch, :, n:n + P]
                        if n == 0:
                            last = dve.tensor_scalar(yc[x][:, ch], src, w, None, ALU.mult)
                        else:
                            dve.wait_ge(conv_step, 32 * i + 16 * x + 4 * n + ch - 3)
                            last = dve.scalar_tensor_tensor(yc[x][:, ch], src, w, yc[x][:, ch], ALU.mult, ALU.add)
                        last.then_inc(conv_step, 1)

            decays(0)
            conv(0, 0)
            with dve.Fori(1, G_QK // 4) as f:
                decays(f)
            conv(0, 1)

            def wait_masks(signal, count, cell):
                dve.wait_ge(signal, count)
                dve.memset(carrier[:, cell:cell + 1], 0.0)

            def mean_squares(i):
                dve.wait_ge(sq_done, i + 1)
                dve.tensor_scalar(m8[:].rearrange("p x q b -> p (x q b)"), ssq[:].rearrange("p x q b -> p (x q b)"), 1.0 / G_HD, EPS, ALU.mult, ALU.add).then_inc(norm_var, 1)

            def norm(i):
                dve.wait_ge(norm_pow, i + 1)
                vlink(dve.tensor_tensor(r2[:], r8[:, :, 1, :], r8[:, :, 1, :], ALU.mult))
                vlink(dve.tensor_tensor(nb[:].rearrange("p x b r -> p (x b) r"), beta[:, bass.ds(2 * i, 2)].rearrange("p x b r -> p (x b) r"),
                                        r2[:].rearrange("p x b -> p (x b)").unsqueeze(2).to_broadcast([P, 2 * B, RATIO]), ALU.mult))
                dve.scalar_tensor_tensor(vi[:], m8[:, :, 1, :], -1.0 / INV, r8[:, :, 1, :], ALU.mult, ALU.mult).then_inc(norm_done, 1)

            def norm_q(i):
                vlink(dve.tensor_scalar(rqs[:], r8[:, :, 0, :], INV * INV, None, ALU.mult))
                vlink(dve.scalar_tensor_tensor(rq2[:], rqs[:], 1.0 / G_HD, rqs[:], ALU.mult, ALU.mult))

            def keys(i):
                for x in range(2):
                    dve.wait_ge(kk_mm, 2 * i + x + 1)
                    dt = DT[:, bass.ds(2 * i + x, 1), :].rearrange("p g k -> p (g k)")
                    for b in range(B):
                        for r in range(RATIO):
                            u = b * RATIO + r
                            last = dve.scalar_tensor_tensor(Np[x][:, u, :], PJ[x][:, (2 * b + 1) * P:(2 * b + 2) * P], nb[:, x, b, r:r + 1],
                                                            dt[:, u * P:(u + 1) * P], ALU.mult, ALU.mult)
                    last.then_inc(np_done, 1)

            def attention(i):
                for x in range(2):
                    dt = DT[:, bass.ds(2 * i + x, 1), :].rearrange("p g (u k) -> p (g u) k", u=4)
                    for b in range(B):
                        last = dve.tensor_tensor(At[x][:, b * RATIO:(b + 1) * RATIO, :],
                                                 PJ[x][:, 2 * b * P:(2 * b + 1) * P].unsqueeze(1).to_broadcast([P, RATIO, P]),
                                                 dt[:, b * RATIO:(b + 1) * RATIO, :], ALU.mult)
                    last.then_inc(at_done, 1)

            def first_level(i):
                for x in range(2):
                    dve.wait_ge(t_reset, 2 * i + x + 1)
                    wait_masks(mt_mm, 2 * i + x + 1, x)
                    dve.copy_predicated(T[x][:], mask(C_LV, 0), quad(YZ[x])).then_inc(t_upd, 1)

            def add_y(i):
                dve.wait_ge(yp_mm, i + 1)
                dve.tensor_tensor(X[:].rearrange("p b d -> p (b d)"), X[:].rearrange("p b d -> p (b d)"), PY, ALU.add).then_inc(x_acc, 1)

            mean_squares(0)
            norm(0)
            norm_q(0)
            dve.wait_ge(dec_done, 2 * PAIRS)
            keys(0)
            first_level(0)
            attention(0)

            def body(i, more):
                again = not isinstance(i, int) or i > 0
                for lv in range(1, LEVELS):
                    for x in range(2):
                        if lv < LAST:
                            wait_masks(zz_mm, 10 * i + 2 * (lv - 1) + x + 1, 2 * lv + x)
                            dve.copy_predicated(T[x][:], mask(C_LV, lv), quad(YZ[x])).then_inc(t_upd, 1)
                        else:
                            wait_masks(zt_mm, 2 * i + x + 1, 2 * lv + x)
                            dve.copy_predicated(TT[x][:], mask(C_LVT, lv), quad(YZ[x])).then_inc(tt_last, 1)
                    if lv == 4 and again:
                        add_y(i - 1)
                    if more and lv in (2, 3, 4, 5):
                        conv(i + 1, lv // 2 - 1, range(2, 4) if lv % 2 else range(0, 2))
                if more:
                    mean_squares(i + 1)
                for x in range(2):
                    dve.wait_ge(tv_mm, 2 * i + x + 1)
                    dve.tensor_tensor(vn[x][:], quad(YZ[x]), nb[:, x].rearrange("p b r -> p (b r)").unsqueeze(2).to_broadcast([P, 4, P]),
                                      ALU.mult).then_inc(vn_done, 1)
                if more:
                    norm(i + 1)
                    keys(i + 1)
                for x in range(2):
                    dve.wait_ge(so_done, 2 * i + x + 1)
                    vlink(dve.tensor_tensor(hv[x][:].rearrange("p (b r) -> p b r", b=B), so[x][:].rearrange("p (b r) -> p b r", b=B),
                                            rq2[:, x, :].unsqueeze(2).to_broadcast([P, B, RATIO]), ALU.mult))
                    dve.tensor_scalar(hv[x][:], hv[x][:], EPS, None, ALU.add).then_inc(h_var, 1)
                if more:
                    first_level(i + 1)
                    attention(i + 1)
                for x in range(2):
                    dve.wait_ge(h_pow, 2 * i + x + 1)
                    vlink(dve.tensor_tensor(hsc[x][:].rearrange("p (b r) -> p b r", b=B), hr[x][:].rearrange("p (b r) -> p b r", b=B),
                                            rqs[:, x, :].unsqueeze(2).to_broadcast([P, B, RATIO]), ALU.mult))
                    for u in range(4):
                        last = dve.scalar_tensor_tensor(hs[x][:, u, :], quad(ZT[x])[:, u, :], hsc[x][:, u:u + 1], sz[x][:, u, :],
                                                        ALU.mult, ALU.mult)
                    last.then_inc(h_done, 1)
                if more:
                    norm_q(i + 1)

            PER = 8
            body(0, True)
            with dve.Fori(1, PAIRS - 1) as i:
                vlink.enter(i, 1, PER)
                body(i, True)
                vlink.leave(PAIRS - 2)
            body(PAIRS - 1, False)
            add_y(PAIRS - 1)


def stage_c(nc, a, env, own):
    X, bk, cst, s, xn, mhalf, ones = (env[k] for k in ("X", "bk", "cst", "s", "xn", "mhalf", "ones"))
    link, alink, plink = env["dve_link"], env["act_link"], env["pool_link"]
    FC = C_IN // P

    def sb(name, shape, dt=F32):
        return own.enter_context(nc.sbuf_tensor("c_" + name, shape, dt))

    def sem(name):
        env["used"].append(own.enter_context(nc.semaphore("c_" + name)))
        return env["used"][-1]

    w = [sb("w1", [P, DC * C_IN]), sb("w2", [P, FC * D])]
    wr = [sb("w1r", [P, DC * C_IN]), sb("w2r", [P, FC * D])]
    wq = [sb("w1q", [P, DC * C_IN], BF16), sb("w2q", [P, FC * D], BF16)]
    wsum, wmean, wscale = sb("wsum", [P, 2]), sb("wmean", [P, 2]), sb("wscale", [P, 2])
    identb = sb("identb", [P, P], BF16)
    H, xs, xr = sb("H", [P, B, C_IN]), sb("xs", [P, B, C_IN]), sb("xr", [P, B, C_IN])
    xq = sb("xq", [P, B, C_IN], BF16)
    xqT = sb("xqT", [P, FC, TOK], BF16)
    ss, ssg, rn, am, sc, f = (sb(n, [P, 2, B]) for n in "ss ssg rn am sc f".split())
    w_in, wsum_done, tot_mm, wq_done, sq_done, ss_done, rn_done = (sem(n) for n in "w_in wsum_done tot_mm wq_done sq_done ss_done rn_done".split())
    xq_done, tr_mm, tr_cp, h_mm, h_done, f_done, y_mm, idb = (sem(n) for n in "xq_done tr_mm tr_cp h_mm h_done f_done y_mm idb".split())

    with nc.Block() as block:
        @block.sync
        def _(sp):
            sp.dma_start(w[0][:], a["c_w1"].rearrange("p c n -> p (c n)")).then_inc(w_in, 16)
            sp.dma_start(w[1][:], a["c_w2"].rearrange("p c n -> p (c n)")).then_inc(w_in, 16)

        @block.gpsimd
        def _(pool):
            env["ln_gpsimd"](2)
            for k in range(2):
                pool.wait_ge(ss_done, k + 1)
                pool.tensor_tensor(rn[:, k, :], ssg[:, k, :], mhalf[:, 0:B], ALU.pow).then_inc(rn_done, 1)

        @block.scalar
        def _(act):
            act.wait_ge(w_in, 32)
            for k in range(2):
                act.activation(wr[k][:], w[k][:], ACT.Abs, accum_out=wsum[:, k:k + 1]).then_inc(wsum_done, 1)
            act.wait_ge(s["ln_xn"], B * 3)
            for b in range(B):
                act.activation(xs[:, b, 0:D], xn[:, b, :], ACT.Square, accum_out=ss[:, 0, b:b + 1]).then_inc(sq_done, 1)
            act.wait_ge(tr_mm, 1)
            act.copy(xqT[:, 0:DC, :].rearrange("p c t -> p (c t)"), bk[0].bitcast(BF16)[:, 0:DC * TOK]).then_inc(tr_cp, 1)
            act.wait_ge(f_done, 1)
            for b in range(B):
                act.wait_ge(h_mm, b + 1)
                for n in range(2):
                    alink(act.activation(H[:, b, n * 512:(n + 1) * 512], bk[2 + 2 * b + n], ACT.Gelu, scale=f[:, 0, b:b + 1]))
                act.activation(H[:, b, :], H[:, b, :], ACT.Gelu).then_inc(h_done, 1)
                act.wait_ge(h_done, b + 1)
                act.activation(xs[:, b, :], H[:, b, :], ACT.Square, accum_out=ss[:, 1, b:b + 1]).then_inc(sq_done, 1)
            for n in range(2):
                act.wait_ge(tr_mm, 2 + n)
                act.copy(xqT[:, 4 * n:4 * n + 4, :].rearrange("p c t -> p (c t)"), bk[n].bitcast(BF16)).then_inc(tr_cp, 1)

        @block.tensor
        def _(pe):
            pe.wait_ge(wsum_done, 2)
            pe.matmul(bk[1][:, 0:2], ones[:], wsum[:], start=True, stop=True).then_inc(tot_mm, 1)
            pe.wait_ge(idb, 1)
            pe.wait_ge(xq_done, B)
            for c in range(DC):
                for b in range(B):
                    last = pe.transpose(bk[0].bitcast(BF16)[:, c * TOK + b * P:c * TOK + (b + 1) * P],
                                        xq[:, b, c * P:(c + 1) * P], identb[:])
            last.then_inc(tr_mm, 1)
            pe.wait_ge(tr_cp, 1)
            pe.wait_ge(wq_done, 1)
            for b in range(B):
                for n in range(2):
                    for c in range(DC):
                        last = pe.matmul(bk[2 + 2 * b + n], xqT[:, c, b * P:(b + 1) * P],
                                         wq[0][:, c * C_IN + n * 512:c * C_IN + (n + 1) * 512], start=(c == 0), stop=(c == DC - 1))
                last.then_inc(h_mm, 1)
            pe.wait_ge(xq_done, 2 * B)
            for n in range(2):
                for c in range(4):
                    for b in range(B):
                        last = pe.transpose(bk[n].bitcast(BF16)[:, c * TOK + b * P:c * TOK + (b + 1) * P],
                                            xq[:, b, (4 * n + c) * P:(4 * n + c + 1) * P], identb[:])
                last.then_inc(tr_mm, 1)
            pe.wait_ge(tr_cp, 3)
            pe.wait_ge(wq_done, 2)
            for b in range(B):
                for c in range(FC):
                    last = pe.matmul(bk[6][:, b * D:(b + 1) * D], xqT[:, c, b * P:(b + 1) * P], wq[1][:, c * D:(c + 1) * D],
                                     start=(c == 0), stop=(c == FC - 1))
            last.then_inc(y_mm, 1)

        @block.vector
        def _(dve):
            dve.tensor_copy(identb[:], cst[:, C_ID:C_ID + P]).then_inc(idb, 1)
            env["ln_vector"](2)

            def quantise(k, src, n):
                dve.wait_ge(sq_done, B * (k + 1))
                dve.tensor_scalar(ssg[:, k, :], ss[:, k, :], 1e-24, None, ALU.max).then_inc(ss_done, 1)
                dve.wait_ge(rn_done, k + 1)
                for b in range(B):
                    link(dve.tensor_scalar(xs[:, b, 0:n], src[:, b, :], rn[:, k, b:b + 1], float(n) ** 0.5, ALU.mult, ALU.mult))
                link(dve.tensor_reduce(am[:, k, :], xs[:, :, 0:n], AX, ALU.max, apply_absolute_value=True))
                link(dve.tensor_scalar(am[:, k, :], am[:, k, :], 1e-5, None, ALU.max))
                link(dve.reciprocal(sc[:, k, :], am[:, k, :]))
                link(dve.tensor_scalar(sc[:, k, :], sc[:, k, :], 127.0, None, ALU.mult))
                for b in range(B):
                    link(dve.tensor_scalar(xr[:, b, 0:n], xs[:, b, 0:n], sc[:, k, b:b + 1], ROUND, ALU.mult, ALU.add))
                    link(dve.tensor_scalar(xr[:, b, 0:n], xr[:, b, 0:n], -ROUND, 127.0, ALU.add, ALU.min))
                    dve.tensor_scalar(xq[:, b, 0:n], xr[:, b, 0:n], -128.0, None, ALU.max).then_inc(xq_done, 1)
                dve.tensor_scalar(f[:, k, :], am[:, k, :], wmean[:, k:k + 1], 1.0 / 127.0, ALU.mult, ALU.mult).then_inc(f_done, 1)

            dve.wait_ge(tot_mm, 1)
            link(dve.tensor_scalar(wmean[:], bk[1][:, 0:2], 1.0 / (C_IN * D), 1e-5, ALU.mult, ALU.max))
            link(dve.reciprocal(wscale[:], wmean[:]))
            quantise(0, xn, D)
            for k in range(2):
                link(dve.tensor_scalar(wr[k][:], w[k][:], wscale[:, k:k + 1], ROUND, ALU.mult, ALU.add))
                link(dve.tensor_scalar(wr[k][:], wr[k][:], -ROUND, 1.0, ALU.add, ALU.min))
                dve.tensor_scalar(wq[k][:], wr[k][:], -1.0, None, ALU.max).then_inc(wq_done, 1)
            quantise(1, H, C_IN)
            dve.wait_ge(f_done, 2)
            dve.wait_ge(y_mm, 1)
            for b in range(B):
                link(dve.scalar_tensor_tensor(X[:, b, :], bk[6][:, b * D:(b + 1) * D], f[:, 1, b:b + 1], X[:, b, :], ALU.mult, ALU.add))


def stage_d(nc, a, env, own):
    X, xnT, bk, ident, cst, s, scores = (env[k] for k in ("X", "xnT", "bk", "ident", "cst", "s", "scores"))
    link, alink = env["dve_link"], env["act_link"]
    HP = X_H // 2
    KG = KT // 4

    def sb(name, shape, dt=F32):
        return own.enter_context(nc.sbuf_tensor("d_" + name, shape, dt))

    def two(name, shape):
        return [sb(f"{name}{x}", shape) for x in range(2)]

    def sem(name):
        env["used"].append(own.enter_context(nc.semaphore("d_" + name)))
        return env["used"][-1]

    raw, KV, tmp = sb("raw", [P, KT, B, LAT]), sb("KV", [P, KT, B, LAT]), sb("tmp", [P, KT, B, LAT])
    rope = sb("rope", [P, 2, KT, LAT])
    KVT = sb("KVT", [P, CTX])
    w128, w64 = two("w128", [P, DC * X_K + X_CQ]), two("w64", [X_R, X_CQ + LAT])
    qh, wc = sb("qh", [P, TOK]), sb("wc", [XQ, 2, P])
    r1, r2, qr = sb("r1", [XQ, 2, TOK]), sb("r2", [XQ, 2, TOK]), sb("qr", [XQ, 2, TOK])
    qp = two("qp", [P, P])
    Pr = two("Pr", [P, CTX])
    Pt = [sb(f"Pt{g}", [P, 4, P]) for g in range(KG)]
    nm2, negm, sums, rc = sb("nm2", [P, B, 2]), sb("negm", [P, B]), sb("sums", [P, B]), sb("rc", [P, B])
    ctxc = sb("ctxc", [P, B, X_H * LAT])
    wkv, wo = sb("wkv", [P, HP, 2, X_K]), sb("wo", [P, X_H, D])
    ccT, cl = two("ccT", [P, TOK]), two("cl", [P, 2, TOK])

    raw_in, rope_in, w_in = sem("raw_in"), sem("rope_in"), [sem(f"w_in{x}") for x in range(2)]
    tail_in = sem("tail_in")
    (kv_done, kvt_mm, kvt_cp, f1_mm, f1_cp, f2_mm, rope_done, f3_mm, q_done, sc_mm, max_done, exp_done, rc_done, tr_mm,
     tr_act, tr_dve, pv_mm, ev_done, wkv_zero) = (sem(n) for n in (
         "kv_done kvt_mm kvt_cp f1_mm f1_cp f2_mm rope_done f3_mm q_done sc_mm max_done exp_done rc_done tr_mm "
         "tr_act tr_dve pv_mm ev_done wkv_zero").split())
    TP, CT, FB = [bk[0], bk[1]], bk[2], bk[3]

    def pairs(eng, body):
        body(0, True, False)
        with eng.Fori(1, HP - 1) as p:
            body(p, False, False)
        body(HP - 1, False, True)

    with nc.Block() as block:
        @block.sync
        def _(sp):
            sp.dma_start(raw[:], a["d_ctx"]).then_inc(raw_in, 16)
            sp.dma_start(rope[:], a["rope"]).then_inc(rope_in, 16)
            for x in range(2):
                sp.dma_start(w128[x][:], a["d_w128"][x]).then_inc(w_in[x], 16)
                sp.dma_start(w64[x][:], a["d_w64"][x]).then_inc(w_in[x], 16)
            sp.dma_start(wo[:], a["d_wo"]).then_inc(tail_in, 16)
            sp.wait_ge(wkv_zero, 1)
            for hh in range(2):
                sp.dma_start(wkv[64 * hh:64 * hh + 64, :, hh, :], a["d_wkv"][hh]).then_inc(tail_in, 16)
            with sp.Fori(0, HP - 1) as p:
                for x in range(2):
                    sp.wait_ge(f2_mm, 2 * p + x + 1)
                    sp.dma_start(w128[x][:], a["d_w128"][bass.ds(2 * p + 2 + x, 1)].rearrange("h p n -> (h p) n")).then_inc(w_in[x], 16)
                    sp.dma_start(w64[x][:], a["d_w64"][bass.ds(2 * p + 2 + x, 1)].rearrange("h p n -> (h p) n")).then_inc(w_in[x], 16)

        @block.gpsimd
        def _(pool):
            pool.memset(wkv[:], 0.0).then_inc(wkv_zero, 1)
            env["ln_gpsimd"](3)

        @block.tensor
        def _(pe):
            pe.wait_ge(kv_done, 1)
            for g in range(KG):
                for j in range(4):
                    last = pe.transpose(scores[:, g, j * P:(j + 1) * P], KV[:, 4 * g + j].rearrange("p b d -> p (b d)"), ident)
                last.then_inc(kvt_mm, 1)
            pe.wait_ge(kvt_cp, KG)
            env["ln_tensor"](3)
            pe.wait_ge(s["ln_xT"], env["turned"](3))

            def front1(p, x):
                h = 2 * p + x
                pe.wait_ge(w_in[x], 32 * p + 32)
                pe.wait_ge(q_done, h)
                for c in range(DC):
                    pe.matmul(FB[:, 0:TOK], w128[x][:, c * X_K:(c + 1) * X_K], xnT[:, c, :], start=(c == 0), stop=(c == DC - 1))
                for half in range(2):
                    last = pe.matmul(FB[0:XQ, TOK + half * P:TOK + (half + 1) * P].rearrange("p (b d) -> p b d", b=B),
                                     w64[x][:, half * XQ:(half + 1) * XQ],
                                     w64[x][:, X_CQ:].unsqueeze(1).to_broadcast([X_R, B, LAT]), start=True, stop=True)
                last.then_inc(f1_mm, 1)

            def front2(p, x):
                pe.wait_ge(f1_cp, 2 * p + x + 1)
                for half in range(2):
                    last = pe.matmul(FB[0:XQ, half * TOK:(half + 1) * TOK], w128[x][:, DC * X_K + half * XQ:DC * X_K + (half + 1) * XQ],
                                     qh[:], start=True, stop=True)
                last.then_inc(f2_mm, 1)

            def front3(p, x):
                pe.wait_ge(rope_done, 2 * p + x + 1)
                for half in range(2):
                    last = pe.matmul(FB[:, 0:TOK], wc[:, half, :], qr[:, half, :], start=(half == 0), stop=(half == 1))
                last.then_inc(f3_mm, 1)

            def turn(m, b, g):
                if g >= 2:
                    pe.wait_ge(tr_act, 2 * m + g - 1)
                elif not (isinstance(m, int) and m == 0):
                    pe.wait_ge(tr_dve, 2 * m + g - 1)
                for j in range(4):
                    at = (4 * g + j) * P
                    last = pe.transpose(TP[g % 2][:, j * P:(j + 1) * P], Pr[b][:, at:at + P], ident)
                last.then_inc(tr_mm, 1)

            def weigh(m, b):
                pe.wait_ge(ev_done, m)
                for g in range(KG):
                    pe.wait_ge(tr_act if g < 2 else tr_dve, 2 * m + g % 2 + 1)
                    for j in range(4):
                        t = 4 * g + j
                        last = pe.matmul(CT[:, 0:LAT], Pt[g][:, j, :], KV[:, t, b, :], start=(t == 0), stop=(t == KT - 1))
                last.then_inc(pv_mm, 1)

            front1(0, 0)
            front2(0, 0)
            front3(0, 0)

            def body(p, first, last_pair):
                for x in range(2):
                    for b in range(B):
                        n = 4 * p + 2 * x + b
                        nxt = (p, 1) if x == 0 else (p + 1, 0)
                        more = not (last_pair and x == 1)
                        pe.wait_ge(q_done, 2 * p + x + 1)
                        pe.wait_ge(exp_done, n)
                        before = not (first and x == 0 and b == 0)
                        if before:
                            turn(n - 1, 1 - b, 0)
                            turn(n - 1, 1 - b, 1)
                        rows = slice(LAT * b, LAT * (b + 1))
                        for g in range(KG):
                            pe.matmul(scores[:, g, :], qp[x][rows, :], KVT[rows, g * 512:(g + 1) * 512],
                                      start=True, stop=True).then_inc(sc_mm, 1)
                        if before:
                            turn(n - 1, 1 - b, 2)
                            turn(n - 1, 1 - b, 3)
                        if more and b == 0:
                            front1(*nxt)
                        if more and b == 1:
                            front3(*nxt)
                        if before:
                            weigh(n - 1, 1 - b)
                        if more and b == 0:
                            front2(*nxt)

            pairs(pe, body)
            pe.wait_ge(exp_done, 4 * HP)
            for g in range(KG):
                turn(4 * HP - 1, 1, g)
            weigh(4 * HP - 1, 1)

        @block.scalar
        def _(act):
            for g in range(KG):
                act.wait_ge(kvt_mm, g + 1)
                act.copy(KVT[:, g * 512:(g + 1) * 512], scores[:, g, :]).then_inc(kvt_cp, 1)
            env["ln_scalar"](3)

            def front1(p, x):
                act.wait_ge(f1_mm, 2 * p + x + 1)
                act.copy(qh[:], FB[:, 0:TOK])
                act.copy(wc[:].rearrange("p f d -> p (f d)"), FB[0:XQ, TOK:2 * TOK]).then_inc(f1_cp, 1)

            def front3(p, x):
                act.wait_ge(f3_mm, 2 * p + x + 1)
                act.copy(qp[x][0:LAT, :], FB[0:LAT, 0:P])
                act.copy(qp[x][LAT:P, :], FB[LAT:P, P:TOK]).then_inc(q_done, 1)

            def keep(m, h, b):
                act.wait_ge(rc_done, m + 1)
                act.wait_ge(pv_mm, m + 1)
                at = slice(h * LAT, (h + 1) * LAT) if isinstance(h, int) else bass.ds(h * LAT, LAT)
                act.activation(ctxc[:, b, at], CT[:, 0:LAT], ACT.Copy, scale=rc[:, b:b + 1]).then_inc(ev_done, 1)

            def turn(m):
                for g in range(2):
                    act.wait_ge(tr_mm, 4 * m + g + 1)
                    act.copy(Pt[g][:].rearrange("p j q -> p (j q)"), TP[g]).then_inc(tr_act, 1)

            front1(0, 0)
            front3(0, 0)

            def body(p, first, last_pair):
                for x in range(2):
                    for b in range(B):
                        n = 4 * p + 2 * x + b
                        nxt = (p, 1) if x == 0 else (p + 1, 0)
                        more = not (last_pair and x == 1)
                        if not (first and x == 0 and b == 0):
                            turn(n - 1)
                        if more:
                            (front1 if b == 0 else front3)(*nxt)
                        act.wait_ge(max_done, n + 1)
                        act.activation(Pr[b][:], scores[:].rearrange("p g k -> p (g k)"), ACT.Exp, bias=negm[:, b:b + 1],
                                       accum_out=sums[:, b:b + 1]).then_inc(exp_done, 1)
                        if not (first and x == 0 and b == 0):
                            keep(n - 1, 2 * p + x - (b == 0), 1 - b)

            pairs(act, body)
            turn(4 * HP - 1)
            keep(4 * HP - 1, X_H - 1, 1)

        @block.vector
        def _(dve):
            dve.wait_ge(raw_in, 16)
            dve.wait_ge(rope_in, 16)
            HL = LAT // 2
            cos, sin = rope[:, 0].unsqueeze(2).to_broadcast([P, KT, B, LAT]), rope[:, 1].unsqueeze(2).to_broadcast([P, KT, B, LAT])
            dve.tensor_tensor(tmp[:, :, :, 0:HL], raw[:, :, :, HL:LAT], sin[:, :, :, 0:HL], ALU.mult)
            link(dve.tensor_tensor(tmp[:, :, :, HL:LAT], raw[:, :, :, 0:HL], sin[:, :, :, HL:LAT], ALU.mult))
            link(dve.tensor_tensor(KV[:], raw[:], cos, ALU.mult))
            dve.tensor_tensor(KV[:], KV[:], tmp[:], ALU.add).then_inc(kv_done, 1)
            env["ln_vector"](3)

            def rotate(p, x):
                dve.wait_ge(f2_mm, 2 * p + x + 1)
                q = FB[0:XQ].rearrange("p (f t) -> p f t", f=2)
                cq = cst[0:XQ, C_CQ:C_CQ + 2 * TOK].rearrange("p (f t) -> p f t", f=2)
                sq = cst[0:XQ, C_SQ:C_SQ + 2 * TOK].rearrange("p (f t) -> p f t", f=2)
                dve.tensor_tensor(r1[:], q, cq, ALU.mult)
                for half in range(2):
                    last = dve.tensor_tensor(r2[:, half, :], q[:, 1 - half, :], sq[:, half, :], ALU.mult)
                link(last)
                dve.tensor_tensor(qr[:], r1[:], r2[:], ALU.add).then_inc(rope_done, 1)

            def turn(m):
                for g in range(2, KG):
                    dve.wait_ge(tr_mm, 4 * m + g + 1)
                    dve.tensor_copy(Pt[g][:].rearrange("p j q -> p (j q)"), TP[g % 2]).then_inc(tr_dve, 1)

            rotate(0, 0)

            def body(p, first, last_pair):
                for x in range(2):
                    for b in range(B):
                        n = 4 * p + 2 * x + b
                        nxt = (p, 1) if x == 0 else (p + 1, 0)
                        if b == 1 and not (last_pair and x == 1):
                            rotate(*nxt)
                        for k in range(2):
                            dve.wait_ge(sc_mm, 4 * n + 2 * k + 2)
                            last = dve.tensor_reduce(nm2[:, b, k:k + 1], scores[:, 2 * k:2 * k + 2, :].rearrange("p g k -> p (g k)"),
                                                     AX, ALU.max, negate=True)
                        link(last)
                        dve.tensor_tensor(negm[:, b:b + 1], nm2[:, b, 0:1], nm2[:, b, 1:2], ALU.min).then_inc(max_done, 1)
                        if not (first and x == 0 and b == 0):
                            dve.wait_ge(exp_done, n)
                            dve.reciprocal(rc[:, 1 - b:2 - b], sums[:, 1 - b:2 - b]).then_inc(rc_done, 1)
                            turn(n - 1)

            body(0, True, False)
            per = 6
            with dve.Fori(1, HP - 1) as p:
                link.enter(p, 1, per)
                body(p, False, False)
                link.leave(HP - 2)
            body(HP - 1, False, True)
            dve.wait_ge(exp_done, 4 * HP)
            dve.reciprocal(rc[:, 1:2], sums[:, 1:2]).then_inc(rc_done, 1)
            turn(4 * HP - 1)

    ct_mm, ct_cp, cl_mm, cl_cp, y_mm = (sem(n) for n in "ct_mm ct_cp cl_mm cl_cp y_mm".split())
    with nc.Block() as block:
        @block.tensor
        def _(pe):
            pe.wait_ge(tail_in, 48)
            for q in range(HP + 2):
                if q < HP:
                    if q >= 2:
                        pe.wait_ge(ct_cp, q - 1)
                    for b in range(B):
                        last = pe.transpose(bk[q % 2][:, b * P:(b + 1) * P], ctxc[:, b, q * P:(q + 1) * P], ident)
                    last.then_inc(ct_mm, 1)
                if 1 <= q <= HP:
                    k = q - 1
                    pe.wait_ge(ct_cp, k + 1)
                    if k >= 2:
                        pe.wait_ge(cl_cp, k - 1)
                    for hh in range(2):
                        last = pe.matmul(bk[2 + k % 2][:, hh * TOK:(hh + 1) * TOK], wkv[:, k, hh, :], ccT[k % 2][:], start=True, stop=True)
                    last.then_inc(cl_mm, 1)
                if q >= 2:
                    k = q - 2
                    pe.wait_ge(cl_cp, k + 1)
                    for hh in range(2):
                        for b in range(B):
                            last = pe.matmul(bk[4 + b][:, 0:D], cl[k % 2][:, hh, b * P:(b + 1) * P], wo[:, 2 * k + hh, :],
                                             start=(k + hh == 0), stop=(k == HP - 1 and hh == 1))
                    last.then_inc(y_mm, 1)

        @block.scalar
        def _(act):
            for k in range(HP):
                act.wait_ge(ct_mm, k + 1)
                if k >= 2:
                    act.wait_ge(cl_mm, k - 1)
                act.copy(ccT[k % 2][:], bk[k % 2][:, 0:TOK]).then_inc(ct_cp, 1)

        @block.vector
        def _(dve):
            for k in range(HP):
                dve.wait_ge(cl_mm, k + 1)
                if k >= 2:
                    dve.wait_ge(y_mm, k - 1)
                dve.tensor_copy(cl[k % 2][:].rearrange("p h t -> p (h t)"), bk[2 + k % 2]).then_inc(cl_cp, 1)
            dve.wait_ge(y_mm, HP)
            for b in range(B):
                link(dve.tensor_tensor(X[:, b, :], X[:, b, :], bk[4 + b][:, 0:D], ALU.add))


def stage_e(nc, a, env, own):
    X, xnT, bk, ident, cst, s = (env[k] for k in ("X", "xnT", "bk", "ident", "cst", "s"))
    link = env["dve_link"]
    QH, RH = E_QR // 2, E_ROPE // 2
    NP = E_REP // 2

    def sb(name, shape, dt=F32):
        return own.enter_context(nc.sbuf_tensor("e_" + name, shape, dt))

    def two(name, shape):
        return [sb(f"{name}{x}", shape) for x in range(2)]

    def sem(name):
        env["used"].append(own.enter_context(nc.semaphore("e_" + name)))
        return env["used"][-1]

    wkvd, wqd = sb("wkvd", [P, DC, LAT]), sb("wqd", [P, DC, E_QR])
    wkn, wv = sb("wkn", [LAT, E_KV * E_NOPE]), sb("wv", [LAT, E_KV * E_V])
    wkr = sb("wkr", [LAT, E_KV, 2, 2, E_ROPE])
    wqn = sb("wqn", [QH, 2, E_H * E_NOPE])
    wqr = sb("wqr", [QH, 2, 2, E_H, E_ROPE])
    wo = sb("wo", [P, E_H, D])
    kvcT, qcT = sb("kvcT", [LAT, TOK]), sb("qcT", [QH, 2, TOK])
    v = sb("v", [P, B, E_KV * E_V])
    knT = two("knT", [P, TOK])
    krT = [two(f"krT{x}", [P, TOK]) for x in range(2)]
    qnT, qrT = two("qnT", [P, E_REP, TOK]), two("qrT", [P, NP, TOK])
    r1, r2 = sb("r1", [P, TOK]), sb("r2", [P, TOK])
    S, PT, oT = (two(n, [P, E_REP, P]) for n in ("S", "PT", "oT"))
    nmax, sums, rec = (two(n, [P, E_REP]) for n in ("nmax", "sums", "rec"))
    w_in = sem("w_in")
    (kz, c_mm, c_cp, v_mm, v_cp, kn_mm, kr_mm, qn_mm, qr_mm, kn_cp, kr_cp, qn_cp, qr_cp, sc_mm, masked, nmax_done, exp_done,
     rec_done, norm_done, tr_mm, tr_cp, pv_mm, pv_cp, y_mm, x_acc) = (sem(n) for n in (
         "kz c_mm c_cp v_mm v_cp kn_mm kr_mm qn_mm qr_mm kn_cp kr_cp qn_cp qr_cp sc_mm masked nmax_done exp_done "
         "rec_done norm_done tr_mm tr_cp pv_mm pv_cp y_mm x_acc").split())
    KN, KR, QN, QR, SC = bk[0], bk[1], [bk[2], bk[3]], [bk[4], bk[5]], [bk[6], bk[7]]
    LOADS = 5 + 2 * 3 + 2 * 3 + 1
    scale = (E_NOPE + E_ROPE) ** -0.5

    with nc.Block() as block:
        @block.sync
        def _(sp):
            for t, d in ((wkvd, "e_wkvd"), (wqd, "e_wqd"), (wkn, "e_wkn"), (wv, "e_wv"), (wqn, "e_wqn")):
                sp.dma_start(t[:], a[d]).then_inc(w_in, 16)
            kr = a["e_wkr"].rearrange("l (n e) -> l n e", n=E_KV)
            for twice in range(2):
                sp.dma_start(wkr[:, :, 0, twice, :], kr).then_inc(w_in, 16)
                for half in range(2):
                    sp.dma_start(wkr[:, :, 1, twice, half * RH:(half + 1) * RH], kr[:, :, (1 - half) * RH:(2 - half) * RH]).then_inc(w_in, 16)
            for c in range(2):
                qr = a["e_wqr"][:, c, :].rearrange("p (h e) -> p h e", h=E_H)
                sp.dma_start(wqr[:, c, 0], qr).then_inc(w_in, 16)
                for half in range(2):
                    sp.dma_start(wqr[:, c, 1, :, half * RH:(half + 1) * RH], qr[:, :, (1 - half) * RH:(2 - half) * RH]).then_inc(w_in, 16)
            sp.dma_start(wo[:], a["e_wo"]).then_inc(w_in, 16)

        @block.gpsimd
        def _(pool):
            env["ln_gpsimd"](4)
            for x in range(2):
                for hh in range(2):
                    pool.memset(krT[hh][x][:], 0.0).then_inc(kz, 1)

        @block.tensor
        def _(pe):
            env["ln_tensor"](4)
            pe.wait_ge(w_in, 16 * LOADS)
            pe.wait_ge(s["ln_xT"], env["turned"](4))
            for c in range(DC):
                pe.matmul(KN[0:LAT, 0:TOK], wkvd[:, c, :], xnT[:, c, :], start=(c == 0), stop=(c == DC - 1))
            for half in range(2):
                for c in range(DC):
                    last = pe.matmul(KR[0:QH, half * TOK:(half + 1) * TOK], wqd[:, c, half * QH:(half + 1) * QH], xnT[:, c, :],
                                     start=(c == 0), stop=(c == DC - 1))
            last.then_inc(c_mm, 1)
            pe.wait_ge(c_cp, 2)
            for b in range(B):
                pe.matmul(SC[b], kvcT[:, b * P:(b + 1) * P], wv[:], start=True, stop=True).then_inc(v_mm, 1)

            def project(n):
                if n:
                    pe.wait_ge(kn_cp, n)
                pe.matmul(KN[:, 0:TOK], wkn[:, n * E_NOPE:(n + 1) * E_NOPE], kvcT[:], start=True, stop=True).then_inc(kn_mm, 1)
                if n:
                    pe.wait_ge(kr_cp, n)
                for sw in range(2):
                    last = pe.matmul(KR[:, sw * TOK:(sw + 1) * TOK], wkr[:, n, sw].rearrange("l t e -> l (t e)"), kvcT[:],
                                     start=True, stop=True)
                last.then_inc(kr_mm, 1)
                for k in range(NP):
                    if n:
                        pe.wait_ge(qn_cp, NP * (n - 1) + k + 1)
                    for hh in range(2):
                        h = n * E_REP + 2 * k + hh
                        for c in range(2):
                            last = pe.matmul(QN[k][:, hh * TOK:(hh + 1) * TOK], wqn[:, c, h * E_NOPE:(h + 1) * E_NOPE], qcT[:, c, :],
                                             start=(c == 0), stop=(c == 1))
                    last.then_inc(qn_mm, 1)
                for k in range(NP):
                    if n:
                        pe.wait_ge(qr_cp, NP * (n - 1) + k + 1)
                        pe.wait_ge(x_acc, n - 1)
                    h = n * E_REP + 2 * k
                    for sw in range(2):
                        for c in range(2):
                            last = pe.matmul(QR[k][:, sw * TOK:(sw + 1) * TOK], wqr[:, c, sw, h:h + 2].rearrange("p h e -> p (h e)"),
                                             qcT[:, c, :], start=(c == 0), stop=(c == 1))
                    last.then_inc(qr_mm, 1)

            project(0)
            for n in range(E_KV):
                x = n % 2
                pe.wait_ge(kn_cp, n + 1)
                pe.wait_ge(kr_cp, n + 1)
                pe.wait_ge(qn_cp, NP * (n + 1))
                pe.wait_ge(qr_cp, NP * (n + 1))
                pe.wait_ge(v_cp, B)
                for b in range(B):
                    if n:
                        pe.wait_ge(pv_cp, B * (n - 1) + b + 1)
                    tok = slice(b * P, (b + 1) * P)
                    for j in range(E_REP):
                        out = SC[b][:, j * P:(j + 1) * P]
                        pe.matmul(out, qnT[x][:, j, tok], knT[x][:, tok], start=True, stop=False)
                        last = pe.matmul(out, qrT[x][:, j // 2, tok], krT[j % 2][x][:, tok], start=False, stop=True)
                    last.then_inc(sc_mm, 1)
                if n + 1 < E_KV:
                    project(n + 1)
                for b in range(B):
                    pe.wait_ge(norm_done, B * n + b + 1)
                    for j in range(E_REP):
                        last = pe.transpose(SC[b][:, j * P:(j + 1) * P], S[b][:, j, :], ident)
                    last.then_inc(tr_mm, 1)
                for b in range(B):
                    pe.wait_ge(tr_cp, B * n + b + 1)
                    pe.matmul(SC[b], v[:, b, n * E_V:(n + 1) * E_V], PT[b][:].rearrange("p j q -> p (j q)"),
                              start=True, stop=True).then_inc(pv_mm, 1)
                pe.wait_ge(pv_cp, B * (n + 1))
                pe.wait_ge(qr_cp, min(NP * (n + 2), NP * E_KV))
                for b in range(B):
                    for j in range(E_REP):
                        last = pe.matmul(QR[0][:, b * D:(b + 1) * D], oT[b][:, j, :], wo[:, n * E_REP + j, :],
                                         start=(j == 0), stop=(j == E_REP - 1))
                last.then_inc(y_mm, 1)

        @block.scalar
        def _(act):
            env["ln_scalar"](4)
            act.wait_ge(c_mm, 1)
            act.copy(kvcT[:], KN[0:LAT, 0:TOK]).then_inc(c_cp, 1)
            act.copy(qcT[:].rearrange("p c t -> p (c t)"), KR[0:QH, :]).then_inc(c_cp, 1)
            for b in range(B):
                act.wait_ge(v_mm, b + 1)
                act.copy(v[:, b, :], SC[b]).then_inc(v_cp, 1)

            def copies(n):
                x = n % 2
                if n >= 2:
                    act.wait_ge(sc_mm, B * (n - 1))
                act.wait_ge(kn_mm, n + 1)
                act.copy(knT[x][:], KN[:, 0:TOK]).then_inc(kn_cp, 1)
                for k in range(NP):
                    act.wait_ge(qn_mm, NP * n + k + 1)
                    act.copy(qnT[x][:, 2 * k:2 * k + 2, :].rearrange("p h t -> p (h t)"), QN[k]).then_inc(qn_cp, 1)

            copies(0)
            for n in range(E_KV):
                for b in range(B):
                    act.wait_ge(nmax_done, B * n + b + 1)
                    for j in range(E_REP):
                        last = act.activation(S[b][:, j, :], S[b][:, j, :], ACT.Exp, bias=nmax[b][:, j:j + 1],
                                              accum_out=sums[b][:, j:j + 1])
                    last.then_inc(exp_done, 1)
                if n + 1 < E_KV:
                    copies(n + 1)
                for b in range(B):
                    act.wait_ge(pv_mm, B * n + b + 1)
                    if n:
                        act.wait_ge(y_mm, n)
                    act.copy(oT[b][:].rearrange("p j q -> p (j q)"), SC[b]).then_inc(pv_cp, 1)

        @block.vector
        def _(dve):
            env["ln_vector"](4)
            dve.wait_ge(kz, 4)
            cos, sin = cst[:, C_CE:C_CE + TOK], cst[:, C_SE:C_SE + TOK]
            causal = cst[:, C_CAUSAL:C_CAUSAL + P].unsqueeze(1).to_broadcast([P, E_REP, P])

            def rotate(n):
                x = n % 2
                if n >= 2:
                    dve.wait_ge(sc_mm, B * (n - 1))
                dve.wait_ge(kr_mm, n + 1)
                dve.tensor_tensor(r1[:], KR[:, 0:TOK], cos, ALU.mult)
                link(dve.tensor_tensor(r2[:], KR[:, TOK:2 * TOK], sin, ALU.mult))
                dve.tensor_tensor(krT[0][x][0:64, :], r1[0:64, :], r2[0:64, :], ALU.add)
                dve.tensor_tensor(krT[1][x][64:P, :], r1[64:P, :], r2[64:P, :], ALU.add).then_inc(kr_cp, 1)
                dve.wait_ge(kr_cp, n + 1)
                for k in range(NP):
                    dve.wait_ge(qr_mm, NP * n + k + 1)
                    dve.tensor_tensor(r1[:], QR[k][:, 0:TOK], cos, ALU.mult)
                    link(dve.tensor_tensor(r2[:], QR[k][:, TOK:2 * TOK], sin, ALU.mult))
                    dve.tensor_tensor(qrT[x][:, k, :], r1[:], r2[:], ALU.add).then_inc(qr_cp, 1)
                    dve.wait_ge(qr_cp, NP * n + k + 1)

            rotate(0)
            for n in range(E_KV):
                for b in range(B):
                    if n:
                        dve.wait_ge(tr_mm, B * (n - 1) + b + 1)
                    dve.wait_ge(sc_mm, B * n + b + 1)
                    dve.scalar_tensor_tensor(S[b][:], SC[b].rearrange("p (j k) -> p j k", j=E_REP), scale, causal,
                                             ALU.mult, ALU.add).then_inc(masked, 1)
                    dve.wait_ge(masked, B * n + b + 1)
                    dve.tensor_reduce(nmax[b][:], S[b][:], AX, ALU.max, negate=True).then_inc(nmax_done, 1)
                if n + 1 < E_KV:
                    rotate(n + 1)
                for b in range(B):
                    dve.wait_ge(exp_done, B * n + b + 1)
                    link(dve.reciprocal(rec[b][:], sums[b][:]))
                    dve.tensor_tensor(S[b][:], S[b][:], rec[b][:].unsqueeze(2).to_broadcast([P, E_REP, P]), ALU.mult).then_inc(norm_done, 1)
                for b in range(B):
                    dve.wait_ge(tr_mm, B * n + b + 1)
                    dve.tensor_copy(PT[b][:].rearrange("p j q -> p (j q)"), SC[b]).then_inc(tr_cp, 1)
                dve.wait_ge(y_mm, n + 1)
                dve.tensor_tensor(X[:].rearrange("p b d -> p (b d)"), X[:].rearrange("p b d -> p (b d)"), QR[0], ALU.add).then_inc(x_acc, 1)
                dve.wait_ge(x_acc, n + 1)


def stage_f(nc, a, env, own):
    X, xnT, bk, ident, cst, s = (env[k] for k in ("X", "xnT", "bk", "ident", "cst", "s"))
    link = env["dve_link"]
    ER = M_E * M_R
    EC = ER // P
    KTOK = M_K * TOK

    def sb(name, shape, dt=F32):
        return own.enter_context(nc.sbuf_tensor("f_" + name, shape, dt))

    def sem(name):
        env["used"].append(own.enter_context(nc.semaphore("f_" + name)))
        return env["used"][-1]

    wg = sb("wg", [P, DC, M_E])
    w1, w3 = sb("w1", [P, DC, M_F]), sb("w3", [P, DC, M_F])
    a1, a3 = sb("a1", [P, DC, ER]), sb("a3", [P, DC, ER])
    b1, b3 = sb("b1", [P, EC, M_F]), sb("b3", [P, EC, M_F])
    w2, a2, b2 = sb("w2", [P, FCH, D]), sb("a2", [P, FCH, ER]), sb("b2", [P, EC, D])
    nm, sums, rs = sb("nm", [P, B]), sb("sums", [P, B]), sb("rs", [P, B])
    pr = [sb(f"pr{k}", [P, B, M_E]) for k in range(3)]
    eq, oh = sb("eq", [P, B, M_E]), sb("oh", [P, M_K, B, M_E])
    top, ix, tot, rw = sb("top", [P, M_K, B]), sb("ix", [P, B]), sb("tot", [P, B]), sb("rw", [P, M_K, B])
    mk = sb("mk", [P, M_K * B, M_E, M_R])
    mkT = sb("mkT", [P, EC, KTOK])
    am = [sb(f"am{k}", [P, EC, KTOK]) for k in range(3)]
    g1 = [sb(f"g1{k}", [P, KTOK]) for k in range(2)]
    x2 = sb("x2", [P, FCH, KTOK])
    w_in = sem("w_in")
    (lg_mm, nm_done, ex_done, mk_done, mt_mm, mt_cp, a_mm, am_done, x1_mm, x3_mm, g_done, x2_done, a2_mm, a2_done, y_mm) = (
        sem(n) for n in "lg_mm nm_done ex_done mk_done mt_mm mt_cp a_mm am_done x1_mm x3_mm g_done x2_done a2_mm a2_done y_mm".split())
    loads = ((wg, "f_wg"), (a1, "f_a1"), (a3, "f_a3"), (w1, "f_w1"), (b1, "f_b1"), (w3, "f_w3"), (b3, "f_b3"),
             (w2, "f_w2"), (a2, "f_a2"), (b2, "f_b2"))
    G1, G3 = [bk[2], bk[3]], [bk[4], bk[5]]

    def slots(ap):
        return ap.unsqueeze(1).to_broadcast([P, M_K, TOK])

    with nc.Block() as block:
        @block.sync
        def _(sp):
            for t, d in loads:
                sp.dma_start(t[:], a[d]).then_inc(w_in, 16)

        @block.gpsimd
        def _(pool):
            env["ln_gpsimd"](5)

        @block.tensor
        def _(pe):
            env["ln_tensor"](5)
            pe.wait_ge(w_in, 16 * len(loads))
            pe.wait_ge(s["ln_xT"], env["turned"](5))
            for b in range(B):
                for c in range(DC):
                    last = pe.matmul(bk[0][:, b * M_E:(b + 1) * M_E], xnT[:, c, b * P:(b + 1) * P], wg[:, c, :],
                                     start=(c == 0), stop=(c == DC - 1))
            last.then_inc(lg_mm, 1)
            for k, w in enumerate((a1, a3)):
                for e in range(EC):
                    for c in range(DC):
                        last = pe.matmul(bk[6 + k][:, e * TOK:(e + 1) * TOK], w[:, c, e * P:(e + 1) * P], xnT[:, c, :],
                                         start=(c == 0), stop=(c == DC - 1))
                last.then_inc(a_mm, 1)
            pe.wait_ge(mk_done, M_K * B)
            for e in range(EC):
                for kb in range(M_K * B):
                    last = pe.transpose(bk[e][:, kb * P:(kb + 1) * P], mk[:, kb].rearrange("p e r -> p (e r)")[:, e * P:(e + 1) * P], ident)
                last.then_inc(mt_mm, 1)
            for f in range(FCH):
                cols = slice(f * P, (f + 1) * P)
                for bank, w, low, m, done in ((G1, w1, b1, am[0], x1_mm), (G3, w3, b3, am[1], x3_mm)):
                    if f >= 2:
                        pe.wait_ge(x2_done, f - 1)
                    out = bank[f % 2].rearrange("p (k t) -> p k t", k=M_K)
                    for c in range(DC):
                        pe.matmul(out, w[:, c, cols], slots(xnT[:, c, :]), start=(c == 0), stop=False)
                    if f == 0:
                        pe.wait_ge(am_done, EC * (1 if m is am[0] else 2))
                    for e in range(EC):
                        last = pe.matmul(bank[f % 2], low[:, e, cols], m[:, e, :], start=False, stop=(e == EC - 1))
                    last.then_inc(done, 1)
            pe.wait_ge(x2_done, FCH)
            for e in range(EC):
                for f in range(FCH):
                    last = pe.matmul(bk[6 + e], a2[:, f, e * P:(e + 1) * P], x2[:, f, :], start=(f == 0), stop=(f == FCH - 1))
                last.then_inc(a2_mm, 1)
            for k in range(M_K):
                for b in range(B):
                    t = slice((k * B + b) * P, (k * B + b + 1) * P)
                    out = bk[k * B + b][:, 0:D]
                    for f in range(FCH):
                        pe.matmul(out, x2[:, f, t], w2[:, f, :], start=(f == 0), stop=False)
                    pe.wait_ge(a2_done, EC)
                    for e in range(EC):
                        last = pe.matmul(out, am[2][:, e, t], b2[:, e, :], start=False, stop=(e == EC - 1))
                    last.then_inc(y_mm, 1)

        @block.scalar
        def _(act):
            env["ln_scalar"](5)
            act.wait_ge(nm_done, 1)
            for b in range(B):
                last = act.activation(pr[0][:, b, :], bk[0][:, b * M_E:(b + 1) * M_E], ACT.Exp, bias=nm[:, b:b + 1],
                                      accum_out=sums[:, b:b + 1])
            last.then_inc(ex_done, 1)
            for e in range(EC):
                act.wait_ge(mt_mm, e + 1)
                act.copy(mkT[:, e, :], bk[e]).then_inc(mt_cp, 1)
            for f in range(FCH):
                act.wait_ge(x1_mm, f + 1)
                if f >= 2:
                    act.wait_ge(x2_done, f - 1)
                act.activation(g1[f % 2][:], G1[f % 2], ACT.Silu).then_inc(g_done, 1)

        @block.vector
        def _(dve):
            env["ln_vector"](5)
            dve.wait_ge(lg_mm, 1)
            dve.tensor_reduce(nm[:], bk[0][:, 0:B * M_E].rearrange("p (b e) -> p b e", b=B), AX, ALU.max, negate=True).then_inc(nm_done, 1)
            dve.wait_ge(ex_done, 1)
            link(dve.reciprocal(rs[:], sums[:]))
            link(dve.tensor_tensor(pr[1][:], pr[0][:], rs[:].unsqueeze(2).to_broadcast([P, B, M_E]), ALU.mult))
            iota = cst[:, C_IOTA:C_IOTA + M_E].unsqueeze(1).to_broadcast([P, B, M_E])
            for k in range(M_K):
                p = pr[1 + k]
                link(dve.tensor_reduce(top[:, k, :], p[:], AX, ALU.max))
                link(dve.tensor_tensor(eq[:], p[:], top[:, k, :].unsqueeze(2).to_broadcast([P, B, M_E]), ALU.is_equal))
                link(dve.tensor_tensor(eq[:], eq[:], iota, ALU.mult))
                link(dve.tensor_reduce(ix[:], eq[:], AX, ALU.min))
                link(dve.tensor_tensor(oh[:, k], iota, ix[:].unsqueeze(2).to_broadcast([P, B, M_E]), ALU.is_equal))
                if k == 0:
                    link(dve.scalar_tensor_tensor(pr[2][:], oh[:, 0], -4.0, pr[1][:], ALU.mult, ALU.add))
            for k in range(M_K):
                for b in range(B):
                    dve.tensor_copy(mk[:, k * B + b], oh[:, k, b, :].unsqueeze(2).to_broadcast([P, M_E, M_R])).then_inc(mk_done, 1)
            link(dve.tensor_tensor(tot[:], top[:, 0, :], top[:, 1, :], ALU.add))
            link(dve.reciprocal(tot[:], tot[:]))
            link(dve.tensor_tensor(rw[:], top[:], tot[:].unsqueeze(1).to_broadcast([P, M_K, B]), ALU.mult))
            for k in range(2):
                dve.wait_ge(a_mm, k + 1)
                for e in range(EC):
                    dve.wait_ge(mt_cp, e + 1)
                    dve.tensor_tensor(am[k][:, e, :].rearrange("p (k t) -> p k t", k=M_K), slots(bk[6 + k][:, e * TOK:(e + 1) * TOK]),
                                      mkT[:, e, :].rearrange("p (k t) -> p k t", k=M_K), ALU.mult).then_inc(am_done, 1)
            for f in range(FCH):
                dve.wait_ge(x3_mm, f + 1)
                dve.wait_ge(g_done, f + 1)
                dve.tensor_tensor(x2[:, f, :], g1[f % 2][:], G3[f % 2], ALU.mult).then_inc(x2_done, 1)
            for e in range(EC):
                dve.wait_ge(a2_mm, e + 1)
                dve.tensor_tensor(am[2][:, e, :], bk[6 + e], mkT[:, e, :], ALU.mult).then_inc(a2_done, 1)
            for k in range(M_K):
                for b in range(B):
                    dve.wait_ge(y_mm, k * B + b + 1)
                    link(dve.scalar_tensor_tensor(X[:, b, :], bk[k * B + b][:, 0:D], rw[:, k, b:b + 1], X[:, b, :], ALU.mult, ALU.add))


def _constants():
    import numpy as np
    i = np.arange(P)
    c = np.zeros((P, C_ALL), np.float32)
    c[:, C_ID:C_ID + P] = np.eye(P)
    c[:, C_UP:C_UP + P] = i[:, None] <= i[None, :]
    c[:, C_LOW:C_LOW + P] = i[:, None] > i[None, :]
    c[:, C_CAUSAL:C_CAUSAL + P] = np.where(i[None, :] <= i[:, None], 0.0, MASKED)
    for level in range(LEVELS):
        w = 1 << level
        m = (i[:, None] // (2 * w) == i[None, :] // (2 * w)) & (i[:, None] // w % 2 == 1) & (i[None, :] // w % 2 == 0)
        c[:, C_LV + level * P:C_LV + (level + 1) * P] = m
        c[:, C_LVT + level * P:C_LVT + (level + 1) * P] = m.T
    inv = (1.0 / 10000.0 ** (np.arange(0, X_CQ, 2, dtype=np.float32) / X_CQ)).astype(np.float32)
    ang = np.repeat(i[:, None].astype(np.float32) * inv[None, :], 2, axis=-1)
    for half in range(2):
        cs = np.cos(ang[:, half * XQ:(half + 1) * XQ]).T
        sn = np.sin(ang[:, half * XQ:(half + 1) * XQ]).T * (-1.0 if half == 0 else 1.0)
        for b in range(B):
            c[0:XQ, C_CQ + half * TOK + b * P:C_CQ + half * TOK + (b + 1) * P] = cs
            c[0:XQ, C_SQ + half * TOK + b * P:C_SQ + half * TOK + (b + 1) * P] = sn
    theta = (1.0 / 10000.0 ** (np.arange(0, E_ROPE, 2, dtype=np.float32) / E_ROPE)).astype(np.float32)
    ang = i[:, None].astype(np.float32) * theta[None, :]
    cs, sn = np.cos(ang).T, np.sin(ang).T
    for b in range(B):
        c[:, C_CE + b * P:C_CE + (b + 1) * P] = np.concatenate([cs] * 4)
        c[:, C_SE + b * P:C_SE + (b + 1) * P] = np.concatenate([-sn, sn, -sn, sn])
    c[:, C_IOTA:C_IOTA + M_E] = np.arange(M_E) - BIG
    inv = (1.0 / 10000.0 ** (np.arange(0, LAT, 2, dtype=np.float32) / LAT)).astype(np.float32)
    ang = np.repeat(np.arange(CTX, dtype=np.float32)[:, None] * inv[None, :], 2, axis=-1)
    cs, sn = np.cos(ang), np.sin(ang)
    sn[:, 0:LAT // 2] = -sn[:, 0:LAT // 2]
    rope = np.stack([cs.reshape(KT, P, LAT).transpose(1, 0, 2), sn.reshape(KT, P, LAT).transpose(1, 0, 2)], 1)
    return c, np.ascontiguousarray(rope.astype(np.float32))


def _kmajor(w):
    k, n = w.shape
    return w.reshape(k // P, P, n).transpose(1, 0, 2)


def kernel(**inputs):
    import numpy as np
    import concourse.bacc as _bacc
    from concourse.bass_utils import run_bass_kernel_spmd as _run

    t = {k: np.asarray(v) for k, v in inputs.items()}
    cst, rope = _constants()
    ctx = t["ctx_512"]
    w = t["L0_attn_W_qkvz"].reshape(G_QK, 6 * P, DC, P)
    conv = t["L0_attn_conv_w"]
    nq = G_QK * G_HD
    conv = np.stack([conv[0:nq].reshape(G_QK, P, TAPS), conv[nq:2 * nq].reshape(G_QK, P, TAPS)]
                    + [conv[2 * nq:].reshape(G_QK, RATIO, P, TAPS)[:, r] for r in range(RATIO)], 2)
    ba = t["L0_attn_W_ba"].reshape(G_QK, 2, RATIO, D).transpose(1, 0, 2, 3).reshape(2 * G_V, D)
    arrays = {
        "x": t["x"], "cst": cst, "rope": rope,
        "a_ctxT": ctx[:, 0:P].transpose(2, 0, 1),
        "a_wq": _kmajor(t["L0_xattn_Wq"].T), "a_wkv": t["L0_xattn_Wkv_expand"].T, "a_wo": _kmajor(t["L0_xattn_Wout"].T),
        "b_slab": np.concatenate([w[:, 0:4 * P].transpose(0, 3, 2, 1).reshape(G_QK, P, DC * 4 * P),
                                  conv.reshape(G_QK, P, 4 * TAPS)], 2),
        "b_wz": w[:, 4 * P:6 * P].transpose(0, 3, 2, 1).reshape(G_QK, P, DC * 2 * P),
        "b_wo": t["L0_attn_W_out"].T.reshape(G_QK, RATIO, P, D).transpose(0, 2, 1, 3).reshape(G_QK, P, RATIO * D),
        "b_wba": _kmajor(ba.T),
        "b_dt": t["L0_attn_dt_bias"].reshape(1, G_V), "b_alog": t["L0_attn_A_log"].reshape(1, G_V),
        "b_norm": t["L0_attn_norm_w"].reshape(P, 1),
        "c_w1": _kmajor(t["L0_ffn_w1"].T), "c_w2": _kmajor(t["L0_ffn_w2"].T),
        "d_ctx": ctx.reshape(B, KT, P, LAT).transpose(2, 1, 0, 3),
        "d_w128": np.concatenate([t["L1_xattn_Wq"].reshape(X_H, X_K, DC, P).transpose(0, 3, 2, 1).reshape(X_H, P, DC * X_K),
                                  t["L1_xattn_w_kc_q"]], 2),
        "d_w64": np.concatenate([t["L1_xattn_W_qr"].transpose(0, 2, 1), t["L1_xattn_W_kr"].transpose(0, 2, 1)], 2),
        "d_wkv": t["L1_xattn_w_kc_kv"].reshape(X_H // 2, 2, X_K, LAT).transpose(1, 3, 0, 2),
        "d_wo": t["L1_xattn_Wo"].T.reshape(X_H, X_K, D).transpose(1, 0, 2),
        "e_wkvd": _kmajor(t["L1_attn_W_kv_down"]), "e_wqd": _kmajor(t["L1_attn_W_q_down"]),
        "e_wkn": t["L1_attn_W_k_nope"], "e_wkr": t["L1_attn_W_k_rope"], "e_wv": t["L1_attn_W_v"],
        "e_wqn": t["L1_attn_W_q_nope"].reshape(2, 96, E_H * E_NOPE).transpose(1, 0, 2),
        "e_wqr": t["L1_attn_W_q_rope"].reshape(2, 96, E_H * E_ROPE).transpose(1, 0, 2),
        "e_wo": t["L1_attn_W_o"].reshape(E_H, P, D).transpose(1, 0, 2),
        "f_wg": _kmajor(t["L1_ffn_Wg"].T),
        "f_w1": _kmajor(t["L1_ffn_W1"].T), "f_w3": _kmajor(t["L1_ffn_W3"].T), "f_w2": _kmajor(t["L1_ffn_W2"].T),
        "f_a1": _kmajor(t["L1_ffn_A1"].reshape(M_E * M_R, D).T), "f_a3": _kmajor(t["L1_ffn_A3"].reshape(M_E * M_R, D).T),
        "f_b1": _kmajor(t["L1_ffn_B1"].transpose(0, 2, 1).reshape(M_E * M_R, M_F)),
        "f_b3": _kmajor(t["L1_ffn_B3"].transpose(0, 2, 1).reshape(M_E * M_R, M_F)),
        "f_a2": _kmajor(t["L1_ffn_A2"].reshape(M_E * M_R, M_F).T),
        "f_b2": _kmajor(t["L1_ffn_B2"].transpose(0, 2, 1).reshape(M_E * M_R, D)),
    }
    nc = _bacc.Bacc("TRN2", target_bir_lowering=False, num_devices=1)
    arrays = {k: np.ascontiguousarray(v) for k, v in arrays.items()}
    a = {k: nc.dram_tensor(f"in_{k}", v.shape, mybir.dt.from_np(v.dtype), kind="ExternalInput").ap()
         for k, v in arrays.items()}
    a["out"] = nc.dram_tensor("out_0", (B, P, D), F32, kind="ExternalOutput").ap()
    build(nc, a, UPTO)
    r = _run(nc, [{f"in_{k}": v for k, v in arrays.items()}], core_ids=[0])
    return r.results[0]["out_0"]


UPTO = 6
```

```python
from contextlib import ExitStack

import concourse.bass as bass
from concourse import mybir

F32 = mybir.dt.float32
BF16 = mybir.dt.bfloat16
U32 = mybir.dt.uint32
ALU = mybir.AluOpType
ACT = mybir.ActivationFunctionType
AX = mybir.AxisListType.X

P = 128
B = 2
D = 256
DC = D // P
TOK = B * P
CTX = 2048
LAT = 64
MASKED = -1e30

A_H, A_HD, A_PAD = 16, 16, 32
G_QK, G_V, G_HD, TAPS = 16, 32, 128, 4
RATIO = G_V // G_QK
PAIRS = G_QK // 2
LEVELS = 7
SLAB = DC * 4 * P + 4 * TAPS
C_IN = 1024
ROUND = 12582912.0
X_H, X_K, X_CQ, X_R = 16, 128, 192, 64
XQ = X_CQ // 2
KT = CTX // P
E_H, E_KV, E_REP, E_NOPE, E_ROPE, E_V = 16, 4, 4, 128, 64, 128
E_QR = 192
M_F, M_E, M_R, M_K = 896, 8, 32, 2
FCH = M_F // P

C_ID = 0
C_UP = 128
C_LOW = 256
C_CAUSAL = 384
C_LV = 512
C_LVT = C_LV + LEVELS * P
C_CQ = C_LVT + LEVELS * P
C_SQ = C_CQ + 2 * TOK
C_CE = C_SQ + 2 * TOK
C_SE = C_CE + TOK
C_IOTA = C_SE + TOK
C_ALL = C_IOTA + M_E
BIG = 1024.0


class Chain:

    def __init__(self, eng, sem):
        self.eng, self.sem, self.n, self.at, self.per = eng, sem, 0, None, 0

    def __call__(self, ins):
        ins.then_inc(self.sem, 1)
        self.n += 1
        self.eng.wait_ge(self.sem, self.n if self.at is None else self.at * self.per + self.n)

    def enter(self, i, first, per):
        self.at, self.per, self.start = i, per, self.n
        self.n -= first * per
        self.shift = first * per

    def leave(self, turns):
        used = self.n + self.shift - self.start
        assert used == self.per, used
        self.n, self.at = self.start + self.per * turns, None


def build(nc, a, upto=6):
    ctx = ExitStack()

    def sem(name):
        return ctx.enter_context(nc.semaphore(name))

    def sb(name, shape, dt=F32):
        return ctx.enter_context(nc.sbuf_tensor(name, shape, dt))

    with ctx:
        bk = [ctx.enter_context(nc.psum_tensor(f"bank{i}", [P, 512], F32))[:] for i in range(4)]
        scores = ctx.enter_context(nc.psum_tensor("scores", [P, 4, 512], F32))
        bk += [scores[:, i, :] for i in range(4)]
        X = sb("X", [P, B, D])
        cst = sb("cst", [P, C_ALL])
        xn = sb("xn", [P, B, D])
        xnT = sb("xnT", [P, DC, TOK])
        stats = sb("stats", [P, B, 6])
        mv = sb("mv", [P, B, 2])
        veps = sb("veps", [P, B])
        rstd = sb("rstd", [P, B])
        mhalf = sb("mhalf", [P, 8])
        ones = sb("ones", [P, P])
        ident = cst[:, C_ID:C_ID + P]

        env = dict(locals())
        s = dict(
            x_in=sem("x_in"), cst_in=sem("cst_in"), ones_set=sem("ones_set"),
            ln_var=sem("ln_var"), ln_rstd=sem("ln_rstd"), ln_xn=sem("ln_xn"),
            ln_tr=sem("ln_tr"), ln_xT=sem("ln_xT"), dve_chain=sem("dve_chain"), act_chain=sem("act_chain"), pool_chain=sem("pool_chain"),
            out_done=sem("out_done"),
        )
        env["s"] = s
        env["dve_link"] = Chain(nc.vector, s["dve_chain"])
        env["act_link"] = Chain(nc.scalar, s["act_chain"])
        env["pool_link"] = Chain(nc.gpsimd, s["pool_chain"])

        def turned(n):
            return n + 1 - (n > 2)

        def ln_vector(n):
            link = env["dve_link"]
            for b in range(B):
                link(nc.vector.bn_stats(stats[:, b, :], X[:, b, :]))
            for b in range(B):
                link(nc.vector.bn_aggr(mv[:, b, :], stats[:, b, :]))
            nc.vector.tensor_scalar(veps[:], mv[:, :, 1], 1e-5, None, ALU.add).then_inc(s["ln_var"], 1)
            nc.vector.wait_ge(s["ln_rstd"], n + 1)
            for b in range(B):
                nc.vector.tensor_scalar(xn[:, b, :], X[:, b, :], mv[:, b, 0:1], rstd[:, b:b + 1],
                                        ALU.subtract, ALU.mult).then_inc(s["ln_xn"], 1)

        def ln_gpsimd(n):
            nc.gpsimd.wait_ge(s["ln_var"], n + 1)
            nc.gpsimd.tensor_tensor(rstd[:], veps[:], mhalf[:, 0:B], ALU.pow).then_inc(s["ln_rstd"], 1)

        def ln_tensor(n):
            nc.tensor.wait_ge(s["ln_xn"], B * (n + 1))
            for c in range(DC):
                for b in range(B):
                    last = nc.tensor.transpose(bk[7][:, c * TOK + b * P:c * TOK + (b + 1) * P],
                                               xn[:, b, c * P:(c + 1) * P], ident)
            last.then_inc(s["ln_tr"], 1)

        def ln_scalar(n):
            nc.scalar.wait_ge(s["ln_tr"], turned(n))
            nc.scalar.copy(xnT[:].rearrange("p c t -> p (c t)"), bk[7]).then_inc(s["ln_xT"], 1)

        env.update(ln_vector=ln_vector, ln_gpsimd=ln_gpsimd, ln_tensor=ln_tensor, ln_scalar=ln_scalar, turned=turned)

        kept, bc = ctx.enter_context(ExitStack()), ctx.enter_context(ExitStack())

        def sb_kept(name, shape, dt=F32):
            return kept.enter_context(nc.sbuf_tensor(name, shape, dt))

        def sb_bc(name, shape, dt=F32):
            return bc.enter_context(nc.sbuf_tensor(name, shape, dt))

        env["w_d"] = early_d(a, sb_kept, sb_bc, sem, nc, env["pool_link"])
        env["w_b"] = early_b(a, sb_bc, sem)
        env["w_c"] = early_c(a, sb_bc, sem)

        def prefetch(sp, stage):
            if stage == "a":
                sp.dma_start(cst[:, C_LV:], a["cst"][:, C_LV:]).then_inc(s["cst_in"], 16)
                env["w_b"]["load"](sp)
                sp.wait_ge(s["cst_in"], 32)
            elif stage == "b":
                env["w_c"]["load"](sp)
                env["w_d"]["load"](sp)
            elif stage in "de":
                env["w_" + chr(ord(stage) + 1)]["load"](sp)

        env["prefetch"] = prefetch

        with nc.Block() as block:
            @block.sync
            def _(sp):
                sp.dma_start(X[:], a["x"].rearrange("b t d -> t b d")).then_inc(s["x_in"], 16)
                sp.dma_start(cst[:, 0:C_LV], a["cst"][:, 0:C_LV]).then_inc(s["cst_in"], 16)
                sp.wait_ge(s["x_in"], 16)
                sp.wait_ge(s["cst_in"], 16)

            @block.vector
            def _(dve):
                dve.memset(ones[:], 1.0)
                dve.memset(mhalf[:], -0.5)

        stages = [stage_a, stage_b, stage_c, stage_d, stage_e, stage_f][:upto]
        for n, st in enumerate(stages):
            if n == 3:
                bc.close()
                env["w_e"] = early_e(a, sb_kept, sem)
            if n == 4:
                env["w_f"] = early_f(a, sb_kept, sem)
            with ExitStack() as own:
                env["used"] = []
                st(nc, a, env, own)
                with nc.Block() as block:
                    @block.vector
                    def _(dve):
                        for used in env["used"]:
                            dve.sem_clear(used)

        with nc.Block() as block:
            @block.sync
            def _(sp):
                sp.dma_start(a["out"].rearrange("b t d -> t b d"), X[:]).then_inc(s["out_done"], 16)
                sp.wait_ge(s["out_done"], 16)


def stage_a(nc, a, env, own):
    X, xnT, bk, ident, cst, s = (env[k] for k in ("X", "xnT", "bk", "ident", "cst", "s"))
    link = env["dve_link"]

    def sb(name, shape, dt=F32):
        return own.enter_context(nc.sbuf_tensor("a_" + name, shape, dt))

    def sem(name):
        env["used"].append(own.enter_context(nc.semaphore("a_" + name)))
        return env["used"][-1]

    HG = A_H // 4
    ctxT = sb("ctxT", [LAT, B, P])
    wq = sb("wq", [P, DC, D])
    wkv = sb("wkv", [LAT, 2 * D])
    wo = sb("wo", [P, DC, D])
    wq_pad = sb("wq_pad", [P, DC, A_H, A_PAD])
    wk_pad = sb("wk_pad", [LAT, A_H, A_PAD])
    qT = sb("qT", [P, HG, TOK])
    kT = sb("kT", [P, HG, TOK])
    v = sb("v", [P, B, D])
    S = sb("S", [P, B, 4, 4, P])
    nmax = sb("nmax", [P, B, 4, 4])
    sums = sb("sums", [P, B, 4, 4])
    rec = sb("rec", [P, B, 4, 4])
    PT = sb("PT", [P, B, 4, 4, P])
    o = sb("o", [P, B, D])
    oT = sb("oT", [P, DC, TOK])
    loads, padded, kq_mm, kq_cp, v_mm, v_cp = (sem(n) for n in "loads padded kq_mm kq_cp v_mm v_cp".split())
    sc_mm, sc_masked, nmax_done, exp_done, tr_mm, tr_cp = (sem(n) for n in "sc_mm sc_masked nmax_done exp_done tr_mm tr_cp".split())
    rec_done, pv_mm, o_cp, ot_mm, ot_cp, y_mm = (sem(n) for n in "rec_done pv_mm o_cp ot_mm ot_cp y_mm".split())

    with nc.Block() as block:
        @block.sync
        def _(sp):
            for t, d in ((ctxT, "a_ctxT"), (wq, "a_wq"), (wkv, "a_wkv"), (wo, "a_wo")):
                sp.dma_start(t[:], a[d]).then_inc(loads, 16)
            env["prefetch"](sp, "a")

        @block.gpsimd
        def _(pool):
            pool.memset(wq_pad[:], 0.0).then_inc(padded, 1)
            pool.memset(wk_pad[:], 0.0).then_inc(padded, 1)
            env["ln_gpsimd"](0)
            pool.wait_ge(padded, 2)
            pool.wait_ge(loads, 64)
            pool.tensor_copy(wk_pad[:, :, 0:A_HD], wkv[:, 0:D].rearrange("p (h e) -> p h e", h=A_H)).then_inc(padded, 1)
            for c in range(DC):
                pool.tensor_copy(wq_pad[:, c, :, 0:A_HD],
                                 wq[:, c, :].rearrange("p (h e) -> p h e", h=A_H)).then_inc(padded, 1)

        @block.tensor
        def _(pe):
            env["ln_tensor"](0)
            pe.wait_ge(loads, 64)
            for b in range(B):
                last = pe.matmul(bk[0][:, b * D:(b + 1) * D], ctxT[:, b, :], wkv[:, D:2 * D], start=True, stop=True)
            last.then_inc(v_mm, 1)
            pe.wait_ge(padded, 5)
            for m in range(HG):
                last = pe.matmul(bk[1 + m // 2][:, (m % 2) * TOK:(m % 2 + 1) * TOK],
                                 wk_pad[:, 4 * m:4 * m + 4, :].rearrange("p h e -> p (h e)"),
                                 ctxT[:].rearrange("p b t -> p (b t)"), start=True, stop=True)
                if m % 2:
                    last.then_inc(kq_mm, 1)
            pe.wait_ge(s["ln_xT"], env["turned"](0))
            for m in range(HG):
                for c in range(DC):
                    last = pe.matmul(bk[3 + m // 2][:, (m % 2) * TOK:(m % 2 + 1) * TOK],
                                     wq_pad[:, c, 4 * m:4 * m + 4, :].rearrange("p h e -> p (h e)"),
                                     xnT[:, c, :], start=(c == 0), stop=(c == DC - 1))
                if m % 2:
                    last.then_inc(kq_mm, 1)
            pe.wait_ge(kq_cp, 4)
            pe.wait_ge(v_cp, 1)
            for b in range(B):
                for j in range(4):
                    rows = slice(32 * j, 32 * j + 32)
                    for m in range(HG):
                        last = pe.matmul(bk[4 * b + j][:, m * P:(m + 1) * P], qT[rows, m, b * P:(b + 1) * P],
                                         kT[rows, m, b * P:(b + 1) * P], start=True, stop=True)
                    last.then_inc(sc_mm, 1)
            for b in range(B):
                for j in range(4):
                    n = 4 * b + j
                    pe.wait_ge(exp_done, n + 1)
                    for m in range(HG):
                        last = pe.transpose(bk[n][:, m * P:(m + 1) * P], S[:, b, j, m, :], ident)
                    last.then_inc(tr_mm, 1)
            for b in range(B):
                pe.wait_ge(tr_cp, 4 * b + 4)
                for h in range(A_H):
                    j, m = h % 4, h // 4
                    last = pe.matmul(bk[4 * b][:, h * A_HD:(h + 1) * A_HD], PT[:, b, j, m, :],
                                     v[:, b, h * A_HD:(h + 1) * A_HD], start=True, stop=True)
                last.then_inc(pv_mm, 1)
            pe.wait_ge(o_cp, 2)
            for c in range(DC):
                for b in range(B):
                    last = pe.transpose(bk[1][:, c * TOK + b * P:c * TOK + (b + 1) * P], o[:, b, c * P:(c + 1) * P], ident)
            last.then_inc(ot_mm, 1)
            pe.wait_ge(ot_cp, 1)
            for b in range(B):
                for c in range(DC):
                    last = pe.matmul(bk[2][:, b * D:(b + 1) * D], oT[:, c, b * P:(b + 1) * P], wo[:, c, :],
                                     start=(c == 0), stop=(c == DC - 1))
            last.then_inc(y_mm, 1)

        @block.scalar
        def _(act):
            env["ln_scalar"](0)
            for n in range(4):
                act.wait_ge(kq_mm, n + 1)
                dst = (kT if n < 2 else qT)[:, 2 * (n % 2):2 * (n % 2) + 2, :].rearrange("p m t -> p (m t)")
                act.copy(dst, bk[1 + n]).then_inc(kq_cp, 1)
            for b in range(B):
                for j in range(4):
                    act.wait_ge(nmax_done, 4 * b + j + 1)
                    for m in range(HG):
                        last = act.activation(S[:, b, j, m, :], S[:, b, j, m, :], ACT.Exp,
                                              bias=nmax[:, b, j, m:m + 1], accum_out=sums[:, b, j, m:m + 1])
                    last.then_inc(exp_done, 1)
            act.wait_ge(ot_mm, 1)
            act.copy(oT[:].rearrange("p c t -> p (c t)"), bk[1]).then_inc(ot_cp, 1)

        @block.vector
        def _(dve):
            env["ln_vector"](0)
            dve.wait_ge(v_mm, 1)
            dve.tensor_copy(v[:].rearrange("p b d -> p (b d)"), bk[0]).then_inc(v_cp, 1)
            causal = cst[:, C_CAUSAL:C_CAUSAL + P].unsqueeze(1).to_broadcast([P, 4, P])
            for b in range(B):
                for j in range(4):
                    n = 4 * b + j
                    dve.wait_ge(sc_mm, n + 1)
                    dve.scalar_tensor_tensor(S[:, b, j], bk[n].rearrange("p (m k) -> p m k", m=4), A_HD ** -0.5, causal,
                                             ALU.mult, ALU.add).then_inc(sc_masked, 1)
                    dve.wait_ge(sc_masked, n + 1)
                    dve.tensor_reduce(nmax[:, b, j, :], S[:, b, j], AX, ALU.max, negate=True).then_inc(nmax_done, 1)
            for b in range(B):
                for j in range(4):
                    n = 4 * b + j
                    dve.wait_ge(tr_mm, n + 1)
                    dve.tensor_copy(PT[:, b, j].rearrange("p m q -> p (m q)"), bk[n]).then_inc(tr_cp, 1)
                dve.reciprocal(rec[:, b], sums[:, b]).then_inc(rec_done, 1)
                dve.wait_ge(rec_done, b + 1)
                dve.wait_ge(pv_mm, b + 1)
                dve.tensor_tensor(o[:, b, :].rearrange("p (m j e) -> p m j e", m=4, j=4),
                                  bk[4 * b][:, 0:D].rearrange("p (m j e) -> p m j e", m=4, j=4),
                                  rec[:, b].rearrange("p j m -> p m j").unsqueeze(3).to_broadcast([P, 4, 4, A_HD]),
                                  ALU.mult).then_inc(o_cp, 1)
            dve.wait_ge(y_mm, 1)
            link(dve.tensor_tensor(X[:].rearrange("p b d -> p (b d)"), X[:].rearrange("p b d -> p (b d)"), bk[2], ALU.add))


def early_b(a, sb, sem):
    w = dict(
        slab=[sb(f"b_slab{x}", [P, SLAB]) for x in range(2)], wz=[sb(f"b_wz{x}", [P, DC, 2 * P]) for x in range(2)],
        wo=[sb(f"b_wo{x}", [P, RATIO, D]) for x in range(2)], wba=sb("b_wba", [P, DC, 2 * G_V]),
        dtb=sb("b_dtb", [P, G_V]), alog=sb("b_alog", [P, G_V]), normw=sb("b_normw", [P, 1]),
        w_in=sem("b_w_in"), small_in=sem("b_small_in"), slab_in=[sem(f"b_slab_in{x}") for x in range(2)],
        wz_in=[sem(f"b_wz_in{x}") for x in range(2)], wo_in=[sem(f"b_wo_in{x}") for x in range(2)])

    def load(sp):
        sp.dma_start(w["wba"][:], a["b_wba"]).then_inc(w["w_in"], 16)
        sp.dma_start(w["dtb"][:], a["b_dt"].to_broadcast([P, G_V])).then_inc(w["small_in"], 16)
        sp.dma_start(w["alog"][:], a["b_alog"].to_broadcast([P, G_V])).then_inc(w["small_in"], 16)
        sp.dma_start(w["normw"][:], a["b_norm"]).then_inc(w["small_in"], 16)
        for x in range(2):
            sp.dma_start(w["slab"][x][:], a["b_slab"][x]).then_inc(w["slab_in"][x], 16)
            sp.dma_start(w["wz"][x][:].rearrange("p c n -> p (c n)"), a["b_wz"][x]).then_inc(w["wz_in"][x], 16)
            sp.dma_start(w["wo"][x][:].rearrange("p r n -> p (r n)"), a["b_wo"][x]).then_inc(w["wo_in"][x], 16)

    w["load"] = load
    return w


def stage_b(nc, a, env, own):
    X, xnT, bk, ident, cst, s, mhalf, ones = (env[k] for k in ("X", "xnT", "bk", "ident", "cst", "s", "mhalf", "ones"))
    vlink, plink, alink = env["dve_link"], env["pool_link"], env["act_link"]
    INV = G_HD ** -0.5
    EPS = 1e-6
    HB = 2 * G_V
    LAST = LEVELS - 1
    HALF = P // 2

    def sb(name, shape, dt=F32):
        return own.enter_context(nc.sbuf_tensor("b_" + name, shape, dt))

    def two(name, shape):
        return [sb(f"{name}{x}", shape) for x in range(2)]

    def sem(name):
        env["used"].append(own.enter_context(nc.semaphore("b_" + name)))
        return env["used"][-1]

    w = env["w_b"]
    slab, wz, wo, wba, dtb, alog, normw = w["slab"], w["wz"], w["wo"], w["wba"], w["dtb"], w["alog"], w["normw"]
    w_in, small_in, slab_in, wz_in, wo_in = w["w_in"], w["small_in"], w["slab_in"], w["wz_in"], w["wo_in"]
    DT = sb("DT", [P, G_QK, 4 * P])
    beta = sb("beta", [P, G_QK, B, RATIO])
    gl = sb("gl", [P, G_QK, B, RATIO])
    t1, t2, t3 = sb("t1", [P, B, G_V]), sb("t2", [P, B, G_V]), sb("t3", [P, B, G_V])
    cpad = two("cpad", [P, 4, B, TAPS - 1 + P])
    yc, qkv = two("yc", [P, 4, B, P]), two("qkv", [P, 4, B, P])
    ssq = sb("ssq", [P, 2, 2, B])
    Np, At, T, TT, Ys = two("Np", [P, 4, P]), two("At", [P, 4, P]), two("T", [P, 4, P]), two("TT", [P, 4, P]), two("Ys", [P, 4, P])
    Vh, vn, sz, hs = two("Vh", [P, 4, P]), two("vn", [P, 4, P]), two("sz", [P, 4, P]), two("hs", [P, 4, P])
    hT = two("hT", [P, 4, P])
    Gm = vn + hs
    I4 = sb("I4", [P, 4, P])
    carrier = sb("carrier", [P, 2 * LEVELS])
    m8, r8 = sb("m8", [P, 2, 2, B]), sb("r8", [P, 2, 2, B])
    r2, vi = sb("r2", [P, 2, B]), sb("vi", [P, 2, B])
    rqs, rq2 = sb("rqs", [P, 2, B]), sb("rq2", [P, 2, B])
    nb = sb("nb", [P, 2, B, RATIO])
    so, hv, hr, hsc = two("so", [P, 4]), two("hv", [P, 4]), two("hr", [P, 4]), two("hsc", [P, 4])

    (i4_set, ba_mm, ba_act, ba_dve, gl_done, gm_done, dec_mm, dec_exp, dec_done, proj_mm, pads_set, pads_cp, conv_step,
     silu_done, sq_done, kk_mm, vt_mm, z_mm, qk_mm, sz_done, vh_done, norm_var, norm_pow, norm_done, np_done, at_done,
     mt_mm, t_reset, t_upd, tt_last, y_mm, y_cp, tr_mm, tt_cp, zz_mm, zt_mm, tv_mm, vn_done, o_mm, so_done, h_var, h_pow, h_done,
     ht_mm, ht_cp, yp_mm, x_acc) = (sem(n) for n in (
        "i4_set ba_mm ba_act ba_dve gl_done gm_done dec_mm dec_exp dec_done proj_mm pads_set pads_cp conv_step "
        "silu_done sq_done kk_mm vt_mm z_mm qk_mm sz_done vh_done norm_var norm_pow norm_done np_done at_done "
        "mt_mm t_reset t_upd tt_last y_mm y_cp tr_mm tt_cp zz_mm zt_mm tv_mm vn_done o_mm so_done h_var h_pow h_done "
        "ht_mm ht_cp yp_mm x_acc").split())

    PJ, PZ, PY, YZ, ZT = [bk[0], bk[1]], bk[2], bk[3], [bk[4], bk[6]], [bk[5], bk[7]]
    UP4 = cst[:, C_UP:C_UP + P].unsqueeze(1).to_broadcast([P, 4, P])

    def quad(ap):
        return ap.rearrange("p (u k) -> p u k", u=4)

    def mask(base, level):
        m = cst[:, base + level * P:base + (level + 1) * P].bitcast(U32)
        return m.unsqueeze(1).to_broadcast([P, 4, P])

    def loop(eng, body):
        body(0, True)
        with eng.Fori(1, PAIRS - 1) as i:
            body(i, True)
        body(PAIRS - 1, False)

    with nc.Block() as block:
        @block.sync
        def _(sp):
            env["prefetch"](sp, "b")

            def next_slabs(i):
                for x in range(2):
                    sp.wait_ge(conv_step, 32 * i + 16 * x + 16)
                    sp.dma_start(slab[x][:], a["b_slab"][bass.ds(2 * i + 2 + x, 1)].rearrange("g p n -> (g p) n")).then_inc(slab_in[x], 16)

            def next_wz(i, x):
                sp.wait_ge(z_mm, 2 * i + x + 1)
                sp.dma_start(wz[x][:].rearrange("p c n -> p (c n)"),
                             a["b_wz"][bass.ds(2 * i + 2 + x, 1)].rearrange("g p n -> (g p) n")).then_inc(wz_in[x], 16)

            def next_wo(i):
                sp.wait_ge(yp_mm, i)
                for x in range(2):
                    sp.dma_start(wo[x][:].rearrange("p r n -> p (r n)"),
                                 a["b_wo"][bass.ds(2 * i + x, 1)].rearrange("g p n -> (g p) n")).then_inc(wo_in[x], 16)

            next_slabs(0)
            next_wz(0, 0)
            next_wz(0, 1)
            with sp.Fori(1, PAIRS - 1) as i:
                next_slabs(i)
                next_wz(i, 0)
                next_wo(i)
                next_wz(i, 1)
            next_wo(PAIRS - 1)

        @block.gpsimd
        def _(pool):
            for x in range(2):
                pool.memset(cpad[x][:], 0.0).then_inc(pads_set, 1)
            pool.wait_ge(s["cst_in"], 16)
            for u in range(4):
                pool.tensor_copy(I4[:, u, :], ident).then_inc(i4_set, 1)
            env["ln_gpsimd"](1)
            pool.wait_ge(i4_set, 4)
            for x in range(2):
                pool.tensor_copy(T[x][:], I4[:]).then_inc(t_reset, 1)

            def causal(i, x):
                pool.wait_ge(dec_exp, 2 * i + x + 1)
                t = DT[:, bass.ds(2 * i + x, 1), :].rearrange("p g (u k) -> p (g u) k", u=4)
                pool.tensor_tensor(t, t, UP4, ALU.mult).then_inc(dec_done, 1)

            with pool.Fori(0, PAIRS) as i:
                for x in range(2):
                    causal(i, x)

            def norm(i):
                pool.wait_ge(norm_var, i + 1)
                pool.tensor_tensor(r8[:].rearrange("p x q b -> p (x q b)"), m8[:].rearrange("p x q b -> p (x q b)"),
                                   mhalf[:, 0:8], ALU.pow).then_inc(norm_pow, 1)

            norm(0)

            def body(i, more):
                if more:
                    for x in range(2):
                        pool.wait_ge(y_mm, 12 * i + 2 * LAST - 1 + x)
                        pool.tensor_tensor(T[x][:], I4[:], I4[:], ALU.mult).then_inc(t_reset, 1)
                    norm(i + 1)
                else:
                    env["w_d"]["rotate_latents"]()
                for x in range(2):
                    pool.wait_ge(h_var, 2 * i + x + 1)
                    pool.tensor_tensor(hr[x][:], hv[x][:], mhalf[:, 0:4], ALU.pow).then_inc(h_pow, 1)

            loop(pool, body)

        @block.tensor
        def _(pe):
            env["ln_tensor"](1)
            pe.wait_ge(w_in, 16)
            pe.wait_ge(s["ln_xT"], env["turned"](1))
            for b in range(B):
                for c in range(DC):
                    last = pe.matmul(bk[0][:, b * HB:(b + 1) * HB], xnT[:, c, b * P:(b + 1) * P], wba[:, c, :],
                                     start=(c == 0), stop=(c == DC - 1))
            last.then_inc(ba_mm, 1)
            def decays(f):
                for k in range(4):
                    pe.wait_ge(gm_done, 4 * f + k + 1)
                    if not isinstance(f, int):
                        pe.wait_ge(dec_exp, 4 * f + k - 3)
                    pe.matmul(bk[4 + k], cst[:, C_LOW:C_LOW + P], Gm[k][:].rearrange("p u k -> p (u k)"),
                              start=True, stop=True).then_inc(dec_mm, 1)

            def project(i, x, chunks=range(4)):
                if 0 in chunks:
                    pe.wait_ge(slab_in[x], 16 * i + 16)
                    if x or not isinstance(i, int) or i > 0:
                        pe.wait_ge(pads_cp, 2 * i + x)
                for ch in chunks:
                    for c in range(DC):
                        last = pe.matmul(PJ[ch // 2][:, ch % 2 * TOK:(ch % 2 + 1) * TOK],
                                         slab[x][:, (c * 4 + ch) * P:(c * 4 + ch + 1) * P], xnT[:, c, :],
                                         start=(c == 0), stop=(c == DC - 1))
                if 3 in chunks:
                    last.then_inc(proj_mm, 1)

            def squares(i, x):
                if not isinstance(i, int) or i > 0:
                    if x == 0:
                        pe.wait_ge(sz_done, 2 * i)
                    elif not isinstance(i, int) or i > 1:
                        pe.wait_ge(x_acc, i - 1)
                pe.wait_ge(silu_done, 2 * i + x + 1)
                for q in range(2):
                    for b in range(B):
                        n = 2 * q + b
                        last = pe.transpose([PZ, PY][x][:, n * P:(n + 1) * P], qkv[x][:, q, b, :], ident)
                last.then_inc(qk_mm, 1)

            def key_products(i, x):
                for b in range(B):
                    last = pe.matmul(PJ[x][:, b * 2 * P:(b + 1) * 2 * P].rearrange("p (q k) -> p q k", q=2),
                                     qkv[x][:, 1, b, :], qkv[x][:, 0:2, b, :], start=True, stop=True)
                last.then_inc(kk_mm, 1)

            def gate(i, x):
                pe.wait_ge(wz_in[x], 16 * i + 16)
                if x:
                    pe.wait_ge(vh_done, 2 * i + 2)
                else:
                    pe.wait_ge(sq_done, i + 1)
                for b in range(B):
                    for c in range(DC):
                        last = pe.matmul(PZ[:, b * 2 * P:(b + 1) * 2 * P], xnT[:, c, b * P:(b + 1) * P], wz[x][:, c, :],
                                         start=(c == 0), stop=(c == DC - 1))
                last.then_inc(z_mm, 1)

            def values(i, x):
                if x:
                    pe.wait_ge(vh_done, 2 * i + 1)
                else:
                    pe.wait_ge(sz_done, 2 * i + 1)
                for b in range(B):
                    for r in range(RATIO):
                        u = b * RATIO + r
                        last = pe.transpose(PZ[:, u * P:(u + 1) * P], qkv[x][:, 2 + r, b, :], ident)
                last.then_inc(vt_mm, 1)

            def turn_m(i):
                for x in range(2):
                    pe.wait_ge(np_done, 2 * i + x + 1)
                    for u in range(4):
                        last = pe.transpose(YZ[x][:, u * P:(u + 1) * P], Np[x][:, u, :], ident)
                    last.then_inc(mt_mm, 1)

            def turn_h(i):
                for x in range(2):
                    pe.wait_ge(h_done, 2 * i + x + 1)
                    for u in range(4):
                        last = pe.transpose(ZT[x][:, u * P:(u + 1) * P], hs[x][:, u, :], ident)
                    last.then_inc(ht_mm, 1)

            def y_out(i):
                pe.wait_ge(ht_cp, 2 * i + 2)
                for x in range(2):
                    pe.wait_ge(wo_in[x], 16 * i + 16)
                for b in range(B):
                    for x in range(2):
                        for r in range(RATIO):
                            last = pe.matmul(PY[:, b * D:(b + 1) * D], hT[x][:, b * RATIO + r, :], wo[x][:, r, :],
                                             start=(x + r == 0), stop=(x + r == 2))
                last.then_inc(yp_mm, 1)

            pe.wait_ge(ba_dve, 1)
            project(0, 0)
            decays(0)
            project(0, 1)
            with pe.Fori(1, G_QK // 4) as f:
                decays(f)
            for x in range(2):
                squares(0, x)
            for x in range(2):
                key_products(0, x)
            pe.wait_ge(dec_exp, 2 * PAIRS)
            turn_m(0)

            def body(i, more):
                again = not isinstance(i, int) or i > 0
                for lv in range(1, LEVELS):
                    def level_y(x):
                        if lv < LAST:
                            pe.wait_ge(t_upd, 12 * i + 2 * (lv - 1) + x + 1)
                        for u in range(4):
                            if lv < LAST:
                                last = pe.matmul(YZ[x][:, u * P:(u + 1) * P], Np[x][:, u, :], T[x][:, u, :], start=True, stop=True)
                            else:
                                last = pe.matmul(YZ[x][HALF:, u * P:u * P + HALF], Np[x][:HALF, u, HALF:], T[x][:HALF, u, :HALF],
                                                 start=True, stop=True)
                        last.then_inc(y_mm, 1)

                    def level_turn(x):
                        if lv == 1 and again:
                            pe.wait_ge(ht_cp, 2 * i + x - 1)
                        if lv == LAST:
                            pe.wait_ge(t_upd, 12 * i + 2 * (lv - 1) + x + 1)
                        for u in range(4):
                            last = pe.transpose(ZT[x][:, u * P:(u + 1) * P], T[x][:, u, :], ident)
                        last.then_inc(tr_mm, 1)

                    if lv == 1:
                        level_y(0)
                        level_y(1)
                        if more:
                            pe.wait_ge(at_done, 2 * i + 2)
                            project(i + 1, 0, (0, 1))
                        if again:
                            turn_h(i - 1)
                        if more:
                            project(i + 1, 0, (2, 3))
                        level_turn(0)
                        level_turn(1)
                        gate(i, 0)
                    elif lv < LAST:
                        for x in range(2):
                            level_y(x)
                            level_turn(x)
                    else:
                        for x in range(2):
                            level_turn(x)
                            level_y(x)
                    if lv in (2, 3):
                        values(i, lv - 2)
                    if lv == 2 and more:
                        project(i + 1, 1)
                    if lv == 4 and again:
                        y_out(i - 1)
                    if lv == 5:
                        gate(i, 1)
                    for x in range(2):
                        pe.wait_ge(y_cp, 12 * i + 2 * (lv - 1) + x + 1)
                        pe.wait_ge(tt_cp, 12 * i + 2 * (lv - 1) + x + 1)
                        if lv == LAST and more:
                            squares(i + 1, x)
                        if lv < LAST:
                            for u in range(4):
                                last = pe.matmul(YZ[x][:, u * P:(u + 1) * P], TT[x][:, u, :], Ys[x][:, u, :], start=True, stop=True)
                            last.then_inc(zz_mm, 1)
                        else:
                            for u in range(4):
                                last = pe.matmul(YZ[x][:HALF, u * P + HALF:(u + 1) * P], Ys[x][HALF:, u, :HALF], TT[x][HALF:, u, HALF:],
                                                 start=True, stop=True)
                            last.then_inc(zt_mm, 1)
                for x in range(2):
                    pe.wait_ge(tt_last, 2 * i + x + 1)
                    for u in range(4):
                        last = pe.matmul(YZ[x][:, u * P:(u + 1) * P], TT[x][:, u, :], Vh[x][:, u, :], start=True, stop=True)
                    last.then_inc(tv_mm, 1)
                if more:
                    pe.wait_ge(pads_cp, 2 * i + 4)
                    for x in range(2):
                        key_products(i + 1, x)
                for x in range(2):
                    pe.wait_ge(vn_done, 2 * i + x + 1)
                    for u in range(4):
                        last = pe.matmul(ZT[x][:, u * P:(u + 1) * P], At[x][:, u, :], vn[x][:, u, :], start=True, stop=True)
                    last.then_inc(o_mm, 1)
                if more:
                    turn_m(i + 1)

            loop(pe, body)
            turn_h(PAIRS - 1)
            pe.wait_ge(x_acc, PAIRS - 1)
            y_out(PAIRS - 1)

        @block.scalar
        def _(act):
            env["ln_scalar"](1)
            act.wait_ge(small_in, 48)
            act.activation(alog[:], alog[:], ACT.Exp).then_inc(ba_act, 1)
            act.wait_ge(ba_mm, 1)
            act.activation(t1[:], bk[0][:, 0:B * HB].rearrange("p (b n) -> p b n", b=B)[:, :, 0:G_V], ACT.Exp, scale=-1.0).then_inc(ba_act, 1)
            act.wait_ge(ba_dve, 1)
            alink(act.activation(t3[:], t2[:], ACT.Abs))
            alink(act.activation(t3[:], t3[:], ACT.Exp, scale=-1.0))
            act.activation(t3[:], t3[:], ACT.Ln, bias=1.0).then_inc(ba_act, 1)
            def pads(i, x):
                act.wait_ge(proj_mm, 2 * i + x + 1)
                for k in range(2):
                    last = act.copy(cpad[x][:, 2 * k:2 * k + 2, :, TAPS - 1:].rearrange("p c b t -> p (c b) t"),
                                    PJ[k].rearrange("p (c t) -> p c t", t=P))
                last.then_inc(pads_cp, 1)

            def silu(i, x):
                act.wait_ge(conv_step, 32 * i + 16 * x + 16)
                act.activation(qkv[x][:].rearrange("p c b t -> p (c b t)"), yc[x][:].rearrange("p c b t -> p (c b t)"),
                               ACT.Silu).then_inc(silu_done, 1)

            def squares(i):
                for x in range(2):
                    act.wait_ge(qk_mm, 2 * i + x + 1)
                    for q in range(2):
                        for b in range(B):
                            n = 2 * q + b
                            last = act.activation(yc[x][:, q, b, :], [PZ, PY][x][:, n * P:(n + 1) * P], ACT.Square,
                                                  accum_out=ssq[:, x, q, b:b + 1])
                last.then_inc(sq_done, 1)

            def gates(i, x):
                act.wait_ge(z_mm, 2 * i + x + 1)
                act.activation(sz[x][:].rearrange("p u k -> p (u k)"), PZ, ACT.Silu).then_inc(sz_done, 1)

            def values(i, x):
                if x == 0:
                    act.wait_ge(norm_done, i + 1)
                act.wait_ge(vt_mm, 2 * i + x + 1)
                for b in range(B):
                    last = act.activation(Vh[x][:, b * RATIO:(b + 1) * RATIO, :],
                                          quad(PZ)[:, b * RATIO:(b + 1) * RATIO, :], ACT.Copy, scale=vi[:, x, b:b + 1])
                last.then_inc(vh_done, 1)

            def turn_h(i):
                for x in range(2):
                    act.wait_ge(ht_mm, 2 * i + x + 1)
                    act.activation(hT[x][:], quad(ZT[x]), ACT.Copy, scale=normw[:, 0:1]).then_inc(ht_cp, 1)

            act.wait_ge(pads_set, 2)
            def decays(f):
                for k in range(4):
                    act.wait_ge(dec_mm, 4 * f + k + 1)
                    act.activation(DT[:, bass.ds(4 * f + k, 1), :].rearrange("p g k -> p (g k)"), bk[4 + k], ACT.Exp).then_inc(dec_exp, 1)

            pads(0, 0)
            decays(0)
            pads(0, 1)
            with act.Fori(1, G_QK // 4) as f:
                decays(f)
            silu(0, 0)
            silu(0, 1)
            squares(0)

            def body(i, more):
                again = not isinstance(i, int) or i > 0
                for lv in range(1, LEVELS):
                    def level_y(x):
                        act.wait_ge(y_mm, 12 * i + 2 * (lv - 1) + x + 1)
                        if lv < LAST:
                            act.copy(Ys[x][:], quad(YZ[x])).then_inc(y_cp, 1)
                        else:
                            act.copy(Ys[x][HALF:, :, :HALF], quad(YZ[x])[HALF:, :, :HALF]).then_inc(y_cp, 1)

                    def level_turn(x):
                        act.wait_ge(tr_mm, 12 * i + 2 * (lv - 1) + x + 1)
                        act.copy(TT[x][:], quad(ZT[x])).then_inc(tt_cp, 1)

                    if lv == 1:
                        level_y(0)
                        level_y(1)
                        if again:
                            turn_h(i - 1)
                        level_turn(0)
                        level_turn(1)
                        gates(i, 0)
                    elif lv < LAST:
                        for x in range(2):
                            level_y(x)
                            level_turn(x)
                    else:
                        for x in range(2):
                            level_turn(x)
                            level_y(x)
                    if lv in (2, 3):
                        values(i, lv - 2)
                    if lv == 5:
                        gates(i, 1)
                    if more and lv in (1, 2):
                        pads(i + 1, lv - 1)
                    if more and lv in (3, 5):
                        silu(i + 1, (lv - 3) // 2)
                if more:
                    squares(i + 1)
                for x in range(2):
                    act.wait_ge(o_mm, 2 * i + x + 1)
                    for u in range(4):
                        last = act.activation(yc[x][:, 2 + u // 2, u % 2, :], quad(ZT[x])[:, u, :], ACT.Square, accum_out=so[x][:, u:u + 1])
                    last.then_inc(so_done, 1)

            loop(act, body)
            turn_h(PAIRS - 1)

        @block.vector
        def _(dve):
            env["ln_vector"](1)
            dve.wait_ge(ba_act, 1)
            vlink(dve.tensor_scalar(alog[:], alog[:], -1.0, None, ALU.mult))
            dve.wait_ge(ba_act, 2)
            ba = bk[0][:, 0:B * HB].rearrange("p (b n) -> p b n", b=B)
            dve.tensor_tensor(t2[:], ba[:, :, G_V:HB], dtb[:].unsqueeze(1).to_broadcast([P, B, G_V]), ALU.add).then_inc(ba_dve, 1)
            vlink(dve.tensor_scalar(t1[:], t1[:], 1.0, None, ALU.add))
            vlink(dve.reciprocal(t1[:], t1[:]))
            for b in range(B):
                vlink(dve.tensor_scalar(beta[:, :, b, :], t1[:, b, :].rearrange("p (g r) -> p g r", r=RATIO), -INV * INV, None, ALU.mult))
            dve.wait_ge(ba_act, 3)
            vlink(dve.scalar_tensor_tensor(t3[:], t2[:], 0.0, t3[:], ALU.max, ALU.add))
            for b in range(B):
                dve.tensor_tensor(gl[:, :, b, :], t3[:, b, :].rearrange("p (g r) -> p g r", r=RATIO),
                                  alog[:].rearrange("p (g r) -> p g r", r=RATIO), ALU.mult).then_inc(gl_done, 1)
            dve.wait_ge(gl_done, 2)
            flat = gl[:].rearrange("p g b r -> p (g b r)")

            def decays(f):
                for k in range(4):
                    if not isinstance(f, int):
                        dve.wait_ge(dec_mm, 4 * f + k - 3)
                    dve.tensor_tensor(Gm[k][:], UP4, flat[:, bass.ds(16 * f + 4 * k, 4)].unsqueeze(2).to_broadcast([P, 4, P]),
                                      ALU.mult).then_inc(gm_done, 1)

            def conv(i, x, taps=range(TAPS)):
                if 0 in taps:
                    dve.wait_ge(pads_cp, 2 * i + x + 1)
                for n in taps:
                    for ch in range(4):
                        w = slab[x][:, DC * 4 * P + ch * TAPS + n:DC * 4 * P + ch * TAPS + n + 1]
                        src = cpad[x][:, ch, :, n:n + P]
                        if n == 0:
                            last = dve.tensor_scalar(yc[x][:, ch], src, w, None, ALU.mult)
                        else:
                            dve.wait_ge(conv_step, 32 * i + 16 * x + 4 * n + ch - 3)
                            last = dve.scalar_tensor_tensor(yc[x][:, ch], src, w, yc[x][:, ch], ALU.mult, ALU.add)
                        last.then_inc(conv_step, 1)

            decays(0)
            conv(0, 0)
            with dve.Fori(1, G_QK // 4) as f:
                decays(f)
            conv(0, 1)

            def wait_masks(signal, count, cell):
                dve.wait_ge(signal, count)
                dve.memset(carrier[:, cell:cell + 1], 0.0)

            def mean_squares(i):
                dve.wait_ge(sq_done, i + 1)
                dve.tensor_scalar(m8[:].rearrange("p x q b -> p (x q b)"), ssq[:].rearrange("p x q b -> p (x q b)"), 1.0 / G_HD, EPS, ALU.mult, ALU.add).then_inc(norm_var, 1)

            def norm(i):
                dve.wait_ge(norm_pow, i + 1)
                vlink(dve.tensor_tensor(r2[:], r8[:, :, 1, :], r8[:, :, 1, :], ALU.mult))
                vlink(dve.tensor_tensor(nb[:].rearrange("p x b r -> p (x b) r"), beta[:, bass.ds(2 * i, 2)].rearrange("p x b r -> p (x b) r"),
                                        r2[:].rearrange("p x b -> p (x b)").unsqueeze(2).to_broadcast([P, 2 * B, RATIO]), ALU.mult))
                dve.scalar_tensor_tensor(vi[:], m8[:, :, 1, :], -1.0 / INV, r8[:, :, 1, :], ALU.mult, ALU.mult).then_inc(norm_done, 1)

            def norm_q(i):
                vlink(dve.tensor_scalar(rqs[:], r8[:, :, 0, :], INV * INV, None, ALU.mult))
                vlink(dve.scalar_tensor_tensor(rq2[:], rqs[:], 1.0 / G_HD, rqs[:], ALU.mult, ALU.mult))

            def keys(i):
                for x in range(2):
                    dve.wait_ge(kk_mm, 2 * i + x + 1)
                    dt = DT[:, bass.ds(2 * i + x, 1), :].rearrange("p g k -> p (g k)")
                    for b in range(B):
                        for r in range(RATIO):
                            u = b * RATIO + r
                            last = dve.scalar_tensor_tensor(Np[x][:, u, :], PJ[x][:, (2 * b + 1) * P:(2 * b + 2) * P], nb[:, x, b, r:r + 1],
                                                            dt[:, u * P:(u + 1) * P], ALU.mult, ALU.mult)
                    last.then_inc(np_done, 1)

            def attention(i):
                for x in range(2):
                    dt = DT[:, bass.ds(2 * i + x, 1), :].rearrange("p g (u k) -> p (g u) k", u=4)
                    for b in range(B):
                        last = dve.tensor_tensor(At[x][:, b * RATIO:(b + 1) * RATIO, :],
                                                 PJ[x][:, 2 * b * P:(2 * b + 1) * P].unsqueeze(1).to_broadcast([P, RATIO, P]),
                                                 dt[:, b * RATIO:(b + 1) * RATIO, :], ALU.mult)
                    last.then_inc(at_done, 1)

            def first_level(i):
                for x in range(2):
                    dve.wait_ge(t_reset, 2 * i + x + 1)
                    wait_masks(mt_mm, 2 * i + x + 1, x)
                    dve.copy_predicated(T[x][:], mask(C_LV, 0), quad(YZ[x])).then_inc(t_upd, 1)

            def add_y(i):
                dve.wait_ge(yp_mm, i + 1)
                dve.tensor_tensor(X[:].rearrange("p b d -> p (b d)"), X[:].rearrange("p b d -> p (b d)"), PY, ALU.add).then_inc(x_acc, 1)

            mean_squares(0)
            norm(0)
            norm_q(0)
            dve.wait_ge(dec_done, 2 * PAIRS)
            keys(0)
            first_level(0)
            attention(0)

            def body(i, more):
                again = not isinstance(i, int) or i > 0
                for lv in range(1, LEVELS):
                    for x in range(2):
                        if lv < LAST:
                            wait_masks(zz_mm, 10 * i + 2 * (lv - 1) + x + 1, 2 * lv + x)
                            dve.copy_predicated(T[x][:], mask(C_LV, lv), quad(YZ[x])).then_inc(t_upd, 1)
                        else:
                            dve.wait_ge(zt_mm, 2 * i + x + 1)
                            dve.tensor_copy(TT[x][:HALF, :, HALF:], quad(YZ[x])[:HALF, :, HALF:]).then_inc(tt_last, 1)
                    if lv == 4 and again:
                        add_y(i - 1)
                    if more and lv in (1, 2, 3, 4):
                        conv(i + 1, (lv - 1) // 2, range(0, 2) if lv % 2 else range(2, 4))
                if more:
                    mean_squares(i + 1)
                for x in range(2):
                    dve.wait_ge(tv_mm, 2 * i + x + 1)
                    dve.tensor_tensor(vn[x][:], quad(YZ[x]), nb[:, x].rearrange("p b r -> p (b r)").unsqueeze(2).to_broadcast([P, 4, P]),
                                      ALU.mult).then_inc(vn_done, 1)
                if more:
                    norm(i + 1)
                    keys(i + 1)
                    first_level(i + 1)
                for x in range(2):
                    dve.wait_ge(so_done, 2 * i + x + 1)
                    vlink(dve.tensor_tensor(hv[x][:].rearrange("p (b r) -> p b r", b=B), so[x][:].rearrange("p (b r) -> p b r", b=B),
                                            rq2[:, x, :].unsqueeze(2).to_broadcast([P, B, RATIO]), ALU.mult))
                    dve.tensor_scalar(hv[x][:], hv[x][:], EPS, None, ALU.add).then_inc(h_var, 1)
                if more:
                    attention(i + 1)
                for x in range(2):
                    dve.wait_ge(h_pow, 2 * i + x + 1)
                    vlink(dve.tensor_tensor(hsc[x][:].rearrange("p (b r) -> p b r", b=B), hr[x][:].rearrange("p (b r) -> p b r", b=B),
                                            rqs[:, x, :].unsqueeze(2).to_broadcast([P, B, RATIO]), ALU.mult))
                    for u in range(4):
                        last = dve.scalar_tensor_tensor(hs[x][:, u, :], quad(ZT[x])[:, u, :], hsc[x][:, u:u + 1], sz[x][:, u, :],
                                                        ALU.mult, ALU.mult)
                    last.then_inc(h_done, 1)
                if more:
                    norm_q(i + 1)

            PER = 8
            body(0, True)
            with dve.Fori(1, PAIRS - 1) as i:
                vlink.enter(i, 1, PER)
                body(i, True)
                vlink.leave(PAIRS - 2)
            body(PAIRS - 1, False)
            add_y(PAIRS - 1)


def early_c(a, sb, sem):
    w = dict(w=[sb("c_w1", [P, DC * C_IN]), sb("c_w2", [P, C_IN // P * D])], w_in=sem("c_w_in"))

    def load(sp):
        sp.dma_start(w["w"][0][:], a["c_w1"].rearrange("p c n -> p (c n)")).then_inc(w["w_in"], 16)
        sp.dma_start(w["w"][1][:], a["c_w2"].rearrange("p c n -> p (c n)")).then_inc(w["w_in"], 16)

    w["load"] = load
    return w


def stage_c(nc, a, env, own):
    X, bk, cst, s, xn, mhalf, ones = (env[k] for k in ("X", "bk", "cst", "s", "xn", "mhalf", "ones"))
    link, alink, plink = env["dve_link"], env["act_link"], env["pool_link"]
    FC = C_IN // P

    def sb(name, shape, dt=F32):
        return own.enter_context(nc.sbuf_tensor("c_" + name, shape, dt))

    def sem(name):
        env["used"].append(own.enter_context(nc.semaphore("c_" + name)))
        return env["used"][-1]

    w, w_in = env["w_c"]["w"], env["w_c"]["w_in"]
    wr = [sb("w1r", [P, DC * C_IN]), sb("w2r", [P, FC * D])]
    wq = [sb("w1q", [P, DC * C_IN], BF16), sb("w2q", [P, FC * D], BF16)]
    wsum, wmean, wscale = sb("wsum", [P, 2]), sb("wmean", [P, 2]), sb("wscale", [P, 2])
    identb = sb("identb", [P, P], BF16)
    H, xs, xr = sb("H", [P, B, C_IN]), sb("xs", [P, B, C_IN]), sb("xr", [P, B, C_IN])
    xq = sb("xq", [P, B, C_IN], BF16)
    xqT = sb("xqT", [P, FC, TOK], BF16)
    ss, ssg, rn, am, sc, f = (sb(n, [P, 2, B]) for n in "ss ssg rn am sc f".split())
    wsum_done, tot_mm, wq_done, sq_done, ss_done, rn_done = (sem(n) for n in "wsum_done tot_mm wq_done sq_done ss_done rn_done".split())
    xq_done, tr_mm, tr_cp, h_mm, h_done, f_done, y_mm, idb = (sem(n) for n in "xq_done tr_mm tr_cp h_mm h_done f_done y_mm idb".split())

    TOT = [bk[1][:, 0:1], bk[7][:, 0:1]]

    with nc.Block() as block:
        @block.gpsimd
        def _(pool):
            env["ln_gpsimd"](2)
            pool.wait_ge(ss_done, 1)
            pool.tensor_tensor(rn[:, 0, :], ssg[:, 0, :], mhalf[:, 0:B], ALU.pow).then_inc(rn_done, 1)
            for b in range(B):
                pool.wait_ge(ss_done, b + 2)
                pool.tensor_tensor(rn[:, 1, b:b + 1], ssg[:, 1, b:b + 1], mhalf[:, 0:1], ALU.pow).then_inc(rn_done, 1)

        @block.scalar
        def _(act):
            act.wait_ge(w_in, 32)
            act.activation(wr[0][:], w[0][:], ACT.Abs, accum_out=wsum[:, 0:1]).then_inc(wsum_done, 1)
            act.wait_ge(s["ln_xn"], B * 3)
            for b in range(B):
                act.activation(xs[:, b, 0:D], xn[:, b, :], ACT.Square, accum_out=ss[:, 0, b:b + 1]).then_inc(sq_done, 1)
            act.activation(wr[1][:], w[1][:], ACT.Abs, accum_out=wsum[:, 1:2]).then_inc(wsum_done, 1)
            act.wait_ge(tr_mm, 1)
            act.copy(xqT[:, 0:DC, :].rearrange("p c t -> p (c t)"), bk[0].bitcast(BF16)[:, 0:DC * TOK]).then_inc(tr_cp, 1)
            act.wait_ge(f_done, 1)
            for b in range(B):
                act.wait_ge(h_mm, b + 1)
                for n in range(2):
                    alink(act.activation(H[:, b, n * 512:(n + 1) * 512], bk[2 + 2 * b + n], ACT.Gelu, scale=f[:, 0, b:b + 1]))
                act.activation(H[:, b, :], H[:, b, :], ACT.Gelu).then_inc(h_done, 1)
                act.wait_ge(h_done, b + 1)
                act.activation(xs[:, b, :], H[:, b, :], ACT.Square, accum_out=ss[:, 1, b:b + 1]).then_inc(sq_done, 1)
            for n in range(2):
                act.wait_ge(tr_mm, 2 + n)
                act.copy(xqT[:, 4 * n:4 * n + 4, :].rearrange("p c t -> p (c t)"), bk[n].bitcast(BF16)).then_inc(tr_cp, 1)

        @block.tensor
        def _(pe):
            for k in range(2):
                pe.wait_ge(wsum_done, k + 1)
                pe.matmul(TOT[k], ones[:], wsum[:, k:k + 1], start=True, stop=True).then_inc(tot_mm, 1)
            pe.wait_ge(idb, 1)
            pe.wait_ge(xq_done, B)
            for c in range(DC):
                for b in range(B):
                    last = pe.transpose(bk[0].bitcast(BF16)[:, c * TOK + b * P:c * TOK + (b + 1) * P],
                                        xq[:, b, c * P:(c + 1) * P], identb[:])
            last.then_inc(tr_mm, 1)
            pe.wait_ge(tr_cp, 1)
            pe.wait_ge(wq_done, 1)
            for b in range(B):
                for n in range(2):
                    for c in range(DC):
                        last = pe.matmul(bk[2 + 2 * b + n], xqT[:, c, b * P:(b + 1) * P],
                                         wq[0][:, c * C_IN + n * 512:c * C_IN + (n + 1) * 512], start=(c == 0), stop=(c == DC - 1))
                last.then_inc(h_mm, 1)
            pe.wait_ge(xq_done, 2 * B)
            for n in range(2):
                for c in range(4):
                    for b in range(B):
                        last = pe.transpose(bk[n].bitcast(BF16)[:, c * TOK + b * P:c * TOK + (b + 1) * P],
                                            xq[:, b, (4 * n + c) * P:(4 * n + c + 1) * P], identb[:])
                last.then_inc(tr_mm, 1)
            pe.wait_ge(tr_cp, 3)
            pe.wait_ge(wq_done, 2)
            for b in range(B):
                for c in range(FC):
                    last = pe.matmul(bk[6][:, b * D:(b + 1) * D], xqT[:, c, b * P:(b + 1) * P], wq[1][:, c * D:(c + 1) * D],
                                     start=(c == 0), stop=(c == FC - 1))
            last.then_inc(y_mm, 1)

        @block.vector
        def _(dve):
            dve.tensor_copy(identb[:], cst[:, C_ID:C_ID + P]).then_inc(idb, 1)
            env["ln_vector"](2)

            def quantise(k, src, n, first, end, turn):
                bs = slice(first, end)
                dve.wait_ge(sq_done, B * k + end)
                dve.tensor_scalar(ssg[:, k, bs], ss[:, k, bs], 1e-24, None, ALU.max).then_inc(ss_done, 1)
                dve.wait_ge(rn_done, turn)
                for b in range(first, end):
                    link(dve.tensor_scalar(xs[:, b, 0:n], src[:, b, :], rn[:, k, b:b + 1], float(n) ** 0.5, ALU.mult, ALU.mult))
                link(dve.tensor_reduce(am[:, k, bs], xs[:, bs, 0:n], AX, ALU.max, apply_absolute_value=True))
                link(dve.tensor_scalar(am[:, k, bs], am[:, k, bs], 1e-5, None, ALU.max))
                link(dve.reciprocal(sc[:, k, bs], am[:, k, bs]))
                link(dve.tensor_scalar(sc[:, k, bs], sc[:, k, bs], 127.0, None, ALU.mult))
                for b in range(first, end):
                    link(dve.tensor_scalar(xr[:, b, 0:n], xs[:, b, 0:n], sc[:, k, b:b + 1], ROUND, ALU.mult, ALU.add))
                    link(dve.tensor_scalar(xr[:, b, 0:n], xr[:, b, 0:n], -ROUND, 127.0, ALU.add, ALU.min))
                    dve.tensor_scalar(xq[:, b, 0:n], xr[:, b, 0:n], -128.0, None, ALU.max).then_inc(xq_done, 1)

            def product_scale(k):
                dve.tensor_scalar(f[:, k, :], am[:, k, :], wmean[:, k:k + 1], 1.0 / 127.0, ALU.mult, ALU.mult).then_inc(f_done, 1)

            def quantise_weights(k):
                dve.wait_ge(tot_mm, k + 1)
                link(dve.tensor_scalar(wmean[:, k:k + 1], TOT[k], 1.0 / (C_IN * D), 1e-5, ALU.mult, ALU.max))
                link(dve.reciprocal(wscale[:, k:k + 1], wmean[:, k:k + 1]))
                link(dve.tensor_scalar(wr[k][:], w[k][:], wscale[:, k:k + 1], ROUND, ALU.mult, ALU.add))
                link(dve.tensor_scalar(wr[k][:], wr[k][:], -ROUND, 1.0, ALU.add, ALU.min))
                dve.tensor_scalar(wq[k][:], wr[k][:], -1.0, None, ALU.max).then_inc(wq_done, 1)

            quantise_weights(0)
            quantise(0, xn, D, 0, B, 1)
            product_scale(0)
            quantise_weights(1)
            for b in range(B):
                quantise(1, H, C_IN, b, b + 1, b + 2)
            product_scale(1)
            dve.wait_ge(f_done, 2)
            dve.wait_ge(y_mm, 1)
            for b in range(B):
                link(dve.scalar_tensor_tensor(X[:, b, :], bk[6][:, b * D:(b + 1) * D], f[:, 1, b:b + 1], X[:, b, :], ALU.mult, ALU.add))


def early_d(a, sb, sb_bc, sem, nc, link):
    w = dict(
        KV=sb("d_KV", [P, KT, B, 2, LAT]), w128=[sb(f"d_w128{x}", [P, DC * X_K + X_CQ]) for x in range(2)],
        w64=[sb(f"d_w64{x}", [X_R, X_CQ + LAT]) for x in range(2)], raw=sb_bc("d_raw", [P, KT, B, LAT]),
        swapped=sb_bc("d_swapped", [P, KT, B, LAT]), rope=sb_bc("d_rope", [P, 2, KT, LAT]),
        raw_in=sem("d_raw_in"), rope_in=sem("d_rope_in"), kv_done=sem("d_kv_done"), w_in=[sem(f"d_w_in{x}") for x in range(2)])

    def load(sp):
        sp.dma_start(w["raw"][:], a["d_ctx"]).then_inc(w["raw_in"], 16)
        sp.dma_start(w["rope"][:], a["rope"]).then_inc(w["rope_in"], 16)
        for x in range(2):
            sp.dma_start(w["w128"][x][:], a["d_w128"][x]).then_inc(w["w_in"][x], 16)
            sp.dma_start(w["w64"][x][:], a["d_w64"][x]).then_inc(w["w_in"][x], 16)

    def rotate_latents():
        HL = LAT // 2
        cos, sin = (w["rope"][:, k].unsqueeze(2).to_broadcast([P, KT, B, LAT]) for k in range(2))
        nc.gpsimd.wait_ge(w["raw_in"], 16)
        nc.gpsimd.wait_ge(w["rope_in"], 16)
        nc.gpsimd.tensor_tensor(w["swapped"][:, :, :, 0:HL], w["raw"][:, :, :, HL:LAT], sin[:, :, :, 0:HL], ALU.mult)
        link(nc.gpsimd.tensor_tensor(w["swapped"][:, :, :, HL:LAT], w["raw"][:, :, :, 0:HL], sin[:, :, :, HL:LAT], ALU.mult))
        link(nc.gpsimd.tensor_tensor(w["raw"][:], w["raw"][:], cos, ALU.mult))
        twice = [w[name][:].rearrange("p t b d -> p (t b) d").unsqueeze(2).to_broadcast([P, KT * B, 2, LAT]) for name in ("raw", "swapped")]
        nc.gpsimd.tensor_tensor(w["KV"][:].rearrange("p t b h d -> p (t b) h d"), *twice, ALU.add).then_inc(w["kv_done"], 1)

    w.update(load=load, rotate_latents=rotate_latents)
    return w


def stage_d(nc, a, env, own):
    X, xnT, bk, ident, cst, s, scores = (env[k] for k in ("X", "xnT", "bk", "ident", "cst", "s", "scores"))
    link, alink = env["dve_link"], env["act_link"]
    HP = X_H // 2
    KG = KT // 4

    def sb(name, shape, dt=F32):
        return own.enter_context(nc.sbuf_tensor("d_" + name, shape, dt))

    def two(name, shape, dt=F32):
        return [sb(f"{name}{x}", shape, dt) for x in range(2)]

    def sem(name):
        env["used"].append(own.enter_context(nc.semaphore("d_" + name)))
        return env["used"][-1]

    KV, w128, w64, w_in = env["w_d"]["KV"], env["w_d"]["w128"], env["w_d"]["w64"], env["w_d"]["w_in"]
    KHM = two("KHM", [P, CTX], BF16)
    KLH = two("KLH", [P, CTX], BF16)
    kh, km, kr = two("kh", [P, 512], BF16), two("km", [P, 512], BF16), two("kr", [P, 512])
    qh, wc = sb("qh", [P, TOK]), sb("wc", [XQ, 2, P])
    r1, r2, qr = sb("r1", [XQ, 2, TOK]), sb("r2", [XQ, 2, TOK]), sb("qr", [XQ, 2, TOK])
    QHH, QMM, QHL = two("QHH", [P, TOK], BF16), two("QMM", [P, TOK], BF16), two("QHL", [P, TOK], BF16)
    qres = sb("qres", [P, TOK])
    Pr = two("Pr", [P, CTX])
    Pt = [sb(f"Pt{g}", [P, 4, P]) for g in range(KG)]
    nm2, negm, sums, rc = sb("nm2", [P, B, 2]), sb("negm", [P, B]), sb("sums", [P, B]), sb("rc", [P, B])
    ctxc = sb("ctxc", [P, B, X_H * LAT])
    wkv, wo = sb("wkv", [X_K, X_H, LAT]), sb("wo", [P, X_H, D])
    ccT, wlo = two("ccT", [P, TOK]), sb("wlo", [P, HP, D])

    tail_in = sem("tail_in")
    (kvt_mm, kh_done, kr_done, k_high, km_done, k_done, qh_done, f1_mm, f1_cp, f2_mm, rope_done, f3_mm, q_done, sc_mm, max_done, exp_done, rc_done, tr_mm,
     tr_act, tr_dve, pv_mm, ev_done) = (sem(n) for n in (
         "kvt_mm kh_done kr_done k_high km_done k_done qh_done f1_mm f1_cp f2_mm rope_done f3_mm q_done sc_mm max_done exp_done rc_done tr_mm "
         "tr_act tr_dve pv_mm ev_done").split())
    KB = [bk[0], bk[1], bk[2]]
    TP, CT, FB = [bk[0], bk[1]], bk[2], bk[3]

    def pairs(eng, body):
        body(0, True, False)
        with eng.Fori(1, HP - 1) as p:
            body(p, False, False)
        body(HP - 1, False, True)

    with nc.Block() as block:
        @block.sync
        def _(sp):
            sp.dma_start(wo[:], a["d_wo"]).then_inc(tail_in, 16)
            sp.dma_start(wkv[:], a["d_wkv"]).then_inc(tail_in, 16)
            env["prefetch"](sp, "d")
            with sp.Fori(0, HP - 1) as p:
                for x in range(2):
                    sp.wait_ge(f2_mm, 2 * p + x + 1)
                    sp.dma_start(w128[x][:], a["d_w128"][bass.ds(2 * p + 2 + x, 1)].rearrange("h p n -> (h p) n")).then_inc(w_in[x], 16)
                    sp.dma_start(w64[x][:], a["d_w64"][bass.ds(2 * p + 2 + x, 1)].rearrange("h p n -> (h p) n")).then_inc(w_in[x], 16)

        @block.gpsimd
        def _(pool):
            env["ln_gpsimd"](3)

        @block.tensor
        def _(pe):
            def turn_keys(k):
                if k >= 3:
                    pe.wait_ge(kr_done, k - 2)
                    pe.wait_ge(kh_done, k - 2)
                for j in range(4):
                    last = pe.transpose(KB[k % 3][:, j * P:(j + 1) * P],
                                        KV[:, 4 * (k % 4) + j, k // 4].rearrange("p h d -> p (h d)"), ident)
                last.then_inc(kvt_mm, 1)

            pe.wait_ge(env["w_d"]["kv_done"], 1)
            for k in range(3):
                turn_keys(k)
            env["ln_tensor"](3)
            pe.wait_ge(s["ln_xT"], env["turned"](3))

            def front1(p, x):
                h = 2 * p + x
                pe.wait_ge(w_in[x], 32 * p + 32)
                pe.wait_ge(q_done, h)
                for c in range(DC):
                    pe.matmul(FB[:, 0:TOK], w128[x][:, c * X_K:(c + 1) * X_K], xnT[:, c, :], start=(c == 0), stop=(c == DC - 1))
                for half in range(2):
                    last = pe.matmul(FB[0:XQ, TOK + half * P:TOK + (half + 1) * P].rearrange("p (b d) -> p b d", b=B),
                                     w64[x][:, half * XQ:(half + 1) * XQ],
                                     w64[x][:, X_CQ:].unsqueeze(1).to_broadcast([X_R, B, LAT]), start=True, stop=True)
                last.then_inc(f1_mm, 1)

            def front2(p, x):
                pe.wait_ge(f1_cp, 2 * p + x + 1)
                for half in range(2):
                    last = pe.matmul(FB[0:XQ, half * TOK:(half + 1) * TOK], w128[x][:, DC * X_K + half * XQ:DC * X_K + (half + 1) * XQ],
                                     qh[:], start=True, stop=True)
                last.then_inc(f2_mm, 1)

            def front3(p, x):
                pe.wait_ge(rope_done, 2 * p + x + 1)
                for half in range(2):
                    last = pe.matmul(FB[:, 0:TOK], wc[:, half, :], qr[:, half, :], start=(half == 0), stop=(half == 1))
                last.then_inc(f3_mm, 1)

            def turn(m, b, g):
                if g >= 2:
                    pe.wait_ge(tr_act, 2 * m + g - 1)
                elif not (isinstance(m, int) and m == 0):
                    pe.wait_ge(tr_dve, 2 * m + g - 1)
                for j in range(4):
                    at = (4 * g + j) * P
                    last = pe.transpose(TP[g % 2][:, j * P:(j + 1) * P], Pr[b][:, at:at + P], ident)
                last.then_inc(tr_mm, 1)

            def weigh(m, b):
                pe.wait_ge(ev_done, m)
                for g in range(KG):
                    pe.wait_ge(tr_act if g < 2 else tr_dve, 2 * m + g % 2 + 1)
                    for j in range(4):
                        t = 4 * g + j
                        last = pe.matmul(CT[:, 0:LAT], Pt[g][:, j, :], KV[:, t, b, 0, :], start=(t == 0), stop=(t == KT - 1))
                last.then_inc(pv_mm, 1)

            front1(0, 0)
            turn_keys(3)
            front2(0, 0)
            turn_keys(4)
            front3(0, 0)
            turn_keys(5)

            def body(p, first, last_pair):
                for x in range(2):
                    for b in range(B):
                        n = 4 * p + 2 * x + b
                        nxt = (p, 1) if x == 0 else (p + 1, 0)
                        more = not (last_pair and x == 1)
                        pe.wait_ge(q_done, 2 * p + x + 1)
                        pe.wait_ge(exp_done, n)
                        before = not (first and x == 0 and b == 0)
                        if first and x == 0 and b == 1:
                            pe.wait_ge(kr_done, 2 * KG)
                        if before:
                            turn(n - 1, 1 - b, 0)
                            turn(n - 1, 1 - b, 1)
                        if first and x == 0:
                            pe.wait_ge(k_done, KG * (b + 1))
                        tok = slice(b * P, (b + 1) * P)
                        for g in range(KG):
                            keys = slice(g * 512, (g + 1) * 512)
                            pe.matmul(scores[:, g, :], QHH[x][:, tok], KHM[b][:, keys], start=True, stop=False)
                            pe.matmul(scores[:, g, :], QMM[x][:, tok], KHM[b][:, keys], start=False, stop=False)
                            pe.matmul(scores[:, g, :], QHL[x][:, tok], KLH[b][:, keys], start=False, stop=True).then_inc(sc_mm, 1)
                        if first and x == 0 and b == 0:
                            turn_keys(6)
                            turn_keys(7)
                        if before:
                            turn(n - 1, 1 - b, 2)
                            turn(n - 1, 1 - b, 3)
                        if more and b == 0:
                            front1(*nxt)
                        if more and b == 1:
                            front3(*nxt)
                        if before:
                            weigh(n - 1, 1 - b)
                        if more and b == 0:
                            front2(*nxt)

            pairs(pe, body)
            pe.wait_ge(exp_done, 4 * HP)
            for g in range(KG):
                turn(4 * HP - 1, 1, g)
            weigh(4 * HP - 1, 1)

        @block.scalar
        def _(act):
            def split_keys(k):
                b, keys, bank = k // 4, slice(k % 4 * 512, (k % 4 + 1) * 512), KB[k % 3]
                act.wait_ge(kvt_mm, k + 1)
                if k >= 2:
                    act.wait_ge(kr_done, k - 1)
                act.copy(kh[k % 2][:], bank).then_inc(kh_done, 1)
                act.wait_ge(kh_done, k + 1)
                act.copy(KHM[b][0:LAT, keys], kh[k % 2][0:LAT, :])
                act.copy(KLH[b][LAT:P, keys], kh[k % 2][LAT:P, :]).then_inc(k_high, 1)

            split_keys(0)
            split_keys(1)
            split_keys(2)
            env["ln_scalar"](3)

            def front1(p, x):
                act.wait_ge(f1_mm, 2 * p + x + 1)
                act.copy(qh[:], FB[:, 0:TOK])
                act.copy(wc[:].rearrange("p f d -> p (f d)"), FB[0:XQ, TOK:2 * TOK]).then_inc(f1_cp, 1)

            def front3(p, x):
                act.wait_ge(f3_mm, 2 * p + x + 1)
                act.copy(QHL[x][0:LAT, :], FB[0:LAT, 0:TOK])
                act.copy(QHH[x][:], FB[:, 0:TOK]).then_inc(qh_done, 1)

            def keep(m, h, b):
                act.wait_ge(rc_done, m + 1)
                act.wait_ge(pv_mm, m + 1)
                at = slice(h * LAT, (h + 1) * LAT) if isinstance(h, int) else bass.ds(h * LAT, LAT)
                act.activation(ctxc[:, b, at], CT[:, 0:LAT], ACT.Copy, scale=rc[:, b:b + 1]).then_inc(ev_done, 1)

            def turn(m):
                for g in range(2):
                    act.wait_ge(tr_mm, 4 * m + g + 1)
                    act.copy(Pt[g][:].rearrange("p j q -> p (j q)"), TP[g]).then_inc(tr_act, 1)

            front1(0, 0)
            split_keys(3)
            front3(0, 0)
            split_keys(4)
            split_keys(5)

            def body(p, first, last_pair):
                for x in range(2):
                    for b in range(B):
                        n = 4 * p + 2 * x + b
                        nxt = (p, 1) if x == 0 else (p + 1, 0)
                        more = not (last_pair and x == 1)
                        if not (first and x == 0 and b == 0):
                            turn(n - 1)
                        if first and x == 0 and b == 0:
                            split_keys(6)
                            split_keys(7)
                        if more:
                            (front1 if b == 0 else front3)(*nxt)
                        act.wait_ge(max_done, n + 1)
                        act.activation(Pr[b][:], scores[:].rearrange("p g k -> p (g k)"), ACT.Exp, bias=negm[:, b:b + 1],
                                       accum_out=sums[:, b:b + 1]).then_inc(exp_done, 1)
                        if not (first and x == 0 and b == 0):
                            keep(n - 1, 2 * p + x - (b == 0), 1 - b)

            pairs(act, body)
            turn(4 * HP - 1)
            keep(4 * HP - 1, X_H - 1, 1)

        @block.vector
        def _(dve):
            env["ln_vector"](3)

            def split_keys(k):
                b, keys, kx = k // 4, slice(k % 4 * 512, (k % 4 + 1) * 512), k % 2
                dve.wait_ge(kh_done, k + 1)
                dve.tensor_tensor(kr[kx][:], KB[k % 3], kh[kx][:], ALU.subtract).then_inc(kr_done, 1)
                dve.wait_ge(kr_done, k + 1)
                dve.tensor_copy(KHM[b][LAT:P, keys], kr[kx][LAT:P, :])
                dve.tensor_copy(km[kx][0:LAT, :], kr[kx][0:LAT, :]).then_inc(km_done, 1)
                dve.wait_ge(km_done, k + 1)
                dve.wait_ge(k_high, k + 1)
                dve.tensor_tensor(KLH[b][0:LAT, keys], kr[kx][0:LAT, :], km[kx][0:LAT, :], ALU.subtract).then_inc(k_done, 1)

            def split_queries(p, x):
                dve.wait_ge(qh_done, 2 * p + x + 1)
                link(dve.tensor_tensor(qres[:], FB[:, 0:TOK], QHH[x][:], ALU.subtract))
                link(dve.tensor_copy(QMM[x][:], qres[:]))
                dve.tensor_tensor(QHL[x][LAT:P, :], qres[LAT:P, :], QMM[x][LAT:P, :], ALU.subtract).then_inc(q_done, 1)

            for k in range(4):
                split_keys(k)

            def rotate(p, x):
                dve.wait_ge(f2_mm, 2 * p + x + 1)
                q = FB[0:XQ].rearrange("p (f t) -> p f t", f=2)
                cq = cst[0:XQ, C_CQ:C_CQ + 2 * TOK].rearrange("p (f t) -> p f t", f=2)
                sq = cst[0:XQ, C_SQ:C_SQ + 2 * TOK].rearrange("p (f t) -> p f t", f=2)
                dve.tensor_tensor(r1[:], q, cq, ALU.mult)
                for half in range(2):
                    last = dve.tensor_tensor(r2[:, half, :], q[:, 1 - half, :], sq[:, half, :], ALU.mult)
                link(last)
                dve.tensor_tensor(qr[:], r1[:], r2[:], ALU.add).then_inc(rope_done, 1)

            def turn(m):
                for g in range(2, KG):
                    dve.wait_ge(tr_mm, 4 * m + g + 1)
                    dve.tensor_copy(Pt[g][:].rearrange("p j q -> p (j q)"), TP[g % 2]).then_inc(tr_dve, 1)

            rotate(0, 0)
            split_keys(4)
            split_queries(0, 0)
            split_keys(5)

            def body(p, first, last_pair):
                for x in range(2):
                    for b in range(B):
                        n = 4 * p + 2 * x + b
                        nxt = (p, 1) if x == 0 else (p + 1, 0)
                        more = not (last_pair and x == 1)
                        if b == 1 and more:
                            rotate(*nxt)
                        for k in range(2):
                            dve.wait_ge(sc_mm, 4 * n + 2 * k + 2)
                            last = dve.tensor_reduce(nm2[:, b, k:k + 1], scores[:, 2 * k:2 * k + 2, :].rearrange("p g k -> p (g k)"),
                                                     AX, ALU.max, negate=True)
                        link(last)
                        dve.tensor_tensor(negm[:, b:b + 1], nm2[:, b, 0:1], nm2[:, b, 1:2], ALU.min).then_inc(max_done, 1)
                        if not (first and x == 0 and b == 0):
                            dve.wait_ge(exp_done, n)
                            dve.reciprocal(rc[:, 1 - b:2 - b], sums[:, 1 - b:2 - b]).then_inc(rc_done, 1)
                            turn(n - 1)
                        if first and x == 0 and b == 0:
                            split_keys(6)
                            split_keys(7)
                        if b == 1 and more:
                            split_queries(*nxt)

            body(0, True, False)
            per = 10
            with dve.Fori(1, HP - 1) as p:
                link.enter(p, 1, per)
                body(p, False, False)
                link.leave(HP - 2)
            body(HP - 1, False, True)
            dve.wait_ge(exp_done, 4 * HP)
            dve.reciprocal(rc[:, 1:2], sums[:, 1:2]).then_inc(rc_done, 1)
            turn(4 * HP - 1)

    ct_mm, ct_cp, w_mm, w_cp, y_mm = (sem(n) for n in "ct_mm ct_cp w_mm w_cp y_mm".split())
    with nc.Block() as block:
        @block.tensor
        def _(pe):
            pe.wait_ge(tail_in, 32)
            for q in range(HP + 1):
                if q < HP:
                    if q >= 2:
                        pe.wait_ge(ct_cp, q - 1)
                    for b in range(B):
                        last = pe.transpose(bk[q % 2][:, b * P:(b + 1) * P], ctxc[:, b, q * P:(q + 1) * P], ident)
                    last.then_inc(ct_mm, 1)
                    if q >= 2:
                        pe.wait_ge(w_cp, q - 1)
                    for hh in range(2):
                        last = pe.matmul(bk[2 + q % 2][hh * LAT:(hh + 1) * LAT, 0:D], wkv[:, 2 * q + hh, :], wo[:, 2 * q + hh, :],
                                         start=True, stop=True)
                    last.then_inc(w_mm, 1)
                if q >= 1:
                    k = q - 1
                    pe.wait_ge(ct_cp, k + 1)
                    pe.wait_ge(w_cp, k + 1)
                    for b in range(B):
                        last = pe.matmul(bk[4 + b][:, 0:D], ccT[k % 2][:, b * P:(b + 1) * P], wlo[:, k, :],
                                         start=(k == 0), stop=(k == HP - 1))
                    last.then_inc(y_mm, 1)

        @block.scalar
        def _(act):
            for k in range(HP):
                act.wait_ge(w_mm, k + 1)
                act.copy(wlo[:, k, :], bk[2 + k % 2][:, 0:D]).then_inc(w_cp, 1)

        @block.vector
        def _(dve):
            for k in range(HP):
                dve.wait_ge(ct_mm, k + 1)
                if k >= 2:
                    dve.wait_ge(y_mm, k - 1)
                dve.tensor_copy(ccT[k % 2][:], bk[k % 2][:, 0:TOK]).then_inc(ct_cp, 1)
            dve.wait_ge(y_mm, HP)
            for b in range(B):
                link(dve.tensor_tensor(X[:, b, :], X[:, b, :], bk[4 + b][:, 0:D], ALU.add))


def early_e(a, sb, sem):
    QH, RH = E_QR // 2, E_ROPE // 2
    w = dict(
        wkvd=sb("e_wkvd", [P, DC, LAT]), wqd=sb("e_wqd", [P, DC, E_QR]),
        wkn=sb("e_wkn", [LAT, E_KV * E_NOPE]), wv=sb("e_wv", [LAT, E_KV * E_V]),
        wkr=sb("e_wkr", [LAT, E_KV, 2, 2, E_ROPE]),
        wqn=sb("e_wqn", [QH, 2, E_H * E_NOPE]),
        wqr=sb("e_wqr", [QH, 2, 2, E_H, E_ROPE]),
        wo=sb("e_wo", [P, E_H, D]), w_in=sem("e_w_in"), loads=5 + 2 * 3 + 2 * 3 + 1)

    def load(sp):
        for t, d in ((w["wkvd"], "e_wkvd"), (w["wqd"], "e_wqd"), (w["wkn"], "e_wkn"), (w["wv"], "e_wv"), (w["wqn"], "e_wqn")):
            sp.dma_start(t[:], a[d]).then_inc(w["w_in"], 16)
        kr = a["e_wkr"].rearrange("l (n e) -> l n e", n=E_KV)
        for twice in range(2):
            sp.dma_start(w["wkr"][:, :, 0, twice, :], kr).then_inc(w["w_in"], 16)
            for half in range(2):
                sp.dma_start(w["wkr"][:, :, 1, twice, half * RH:(half + 1) * RH], kr[:, :, (1 - half) * RH:(2 - half) * RH]).then_inc(w["w_in"], 16)
        for c in range(2):
            qr = a["e_wqr"][:, c, :].rearrange("p (h e) -> p h e", h=E_H)
            sp.dma_start(w["wqr"][:, c, 0], qr).then_inc(w["w_in"], 16)
            for half in range(2):
                sp.dma_start(w["wqr"][:, c, 1, :, half * RH:(half + 1) * RH], qr[:, :, (1 - half) * RH:(2 - half) * RH]).then_inc(w["w_in"], 16)
        sp.dma_start(w["wo"][:], a["e_wo"]).then_inc(w["w_in"], 16)

    w["load"] = load
    return w


def stage_e(nc, a, env, own):
    X, xnT, bk, ident, cst, s = (env[k] for k in ("X", "xnT", "bk", "ident", "cst", "s"))
    link = env["dve_link"]
    QH, RH = E_QR // 2, E_ROPE // 2
    NP = E_REP // 2

    def sb(name, shape, dt=F32):
        return own.enter_context(nc.sbuf_tensor("e_" + name, shape, dt))

    def two(name, shape):
        return [sb(f"{name}{x}", shape) for x in range(2)]

    def sem(name):
        env["used"].append(own.enter_context(nc.semaphore("e_" + name)))
        return env["used"][-1]

    w = env["w_e"]
    wkvd, wqd, wkn, wv, wkr, wqn, wqr, wo, w_in = w["wkvd"], w["wqd"], w["wkn"], w["wv"], w["wkr"], w["wqn"], w["wqr"], w["wo"], w["w_in"]
    kvcT, qcT = sb("kvcT", [LAT, TOK]), sb("qcT", [QH, 2, TOK])
    v = sb("v", [P, B, E_KV * E_V])
    knT = two("knT", [P, TOK])
    krT = [two(f"krT{x}", [P, TOK]) for x in range(2)]
    qnT, qrT = two("qnT", [P, E_REP, TOK]), two("qrT", [P, NP, TOK])
    r1, r2 = sb("r1", [P, TOK]), sb("r2", [P, TOK])
    S, PT, oT = (two(n, [P, E_REP, P]) for n in ("S", "PT", "oT"))
    nmax, sums, rec = (two(n, [P, E_REP]) for n in ("nmax", "sums", "rec"))
    (kz, c_mm, c_cp, v_mm, v_cp, kn_mm, kr_mm, qn_mm, qr_mm, kn_cp, kr_cp, qn_cp, qr_cp, sc_mm, masked, nmax_done, exp_done,
     rec_done, norm_done, tr_mm, tr_cp, pv_mm, pv_cp, y_mm, x_acc) = (sem(n) for n in (
         "kz c_mm c_cp v_mm v_cp kn_mm kr_mm qn_mm qr_mm kn_cp kr_cp qn_cp qr_cp sc_mm masked nmax_done exp_done "
         "rec_done norm_done tr_mm tr_cp pv_mm pv_cp y_mm x_acc").split())
    KN, KR, QN, QR, SC = bk[0], bk[1], [bk[2], bk[3]], [bk[4], bk[5]], [bk[6], bk[7]]
    scale = (E_NOPE + E_ROPE) ** -0.5

    with nc.Block() as block:
        @block.sync
        def _(sp):
            env["prefetch"](sp, "e")

        @block.gpsimd
        def _(pool):
            env["ln_gpsimd"](4)
            for x in range(2):
                for hh in range(2):
                    pool.memset(krT[hh][x][:], 0.0).then_inc(kz, 1)

        @block.tensor
        def _(pe):
            env["ln_tensor"](4)
            pe.wait_ge(w_in, 16 * w["loads"])
            pe.wait_ge(s["ln_xT"], env["turned"](4))
            for c in range(DC):
                pe.matmul(KN[0:LAT, 0:TOK], wkvd[:, c, :], xnT[:, c, :], start=(c == 0), stop=(c == DC - 1))
            for half in range(2):
                for c in range(DC):
                    last = pe.matmul(KR[0:QH, half * TOK:(half + 1) * TOK], wqd[:, c, half * QH:(half + 1) * QH], xnT[:, c, :],
                                     start=(c == 0), stop=(c == DC - 1))
            last.then_inc(c_mm, 1)
            pe.wait_ge(c_cp, 2)
            for b in range(B):
                pe.matmul(SC[b], kvcT[:, b * P:(b + 1) * P], wv[:], start=True, stop=True).then_inc(v_mm, 1)

            def project(n):
                if n:
                    pe.wait_ge(kn_cp, n)
                pe.matmul(KN[:, 0:TOK], wkn[:, n * E_NOPE:(n + 1) * E_NOPE], kvcT[:], start=True, stop=True).then_inc(kn_mm, 1)
                if n:
                    pe.wait_ge(kr_cp, n)
                for sw in range(2):
                    last = pe.matmul(KR[:, sw * TOK:(sw + 1) * TOK], wkr[:, n, sw].rearrange("l t e -> l (t e)"), kvcT[:],
                                     start=True, stop=True)
                last.then_inc(kr_mm, 1)
                for k in range(NP):
                    if n:
                        pe.wait_ge(qn_cp, NP * (n - 1) + k + 1)
                    for hh in range(2):
                        h = n * E_REP + 2 * k + hh
                        for c in range(2):
                            last = pe.matmul(QN[k][:, hh * TOK:(hh + 1) * TOK], wqn[:, c, h * E_NOPE:(h + 1) * E_NOPE], qcT[:, c, :],
                                             start=(c == 0), stop=(c == 1))
                    last.then_inc(qn_mm, 1)
                for k in range(NP):
                    if n:
                        pe.wait_ge(qr_cp, NP * (n - 1) + k + 1)
                        pe.wait_ge(x_acc, n - 1)
                    h = n * E_REP + 2 * k
                    for sw in range(2):
                        for c in range(2):
                            last = pe.matmul(QR[k][:, sw * TOK:(sw + 1) * TOK], wqr[:, c, sw, h:h + 2].rearrange("p h e -> p (h e)"),
                                             qcT[:, c, :], start=(c == 0), stop=(c == 1))
                    last.then_inc(qr_mm, 1)

            project(0)
            for n in range(E_KV):
                x = n % 2
                pe.wait_ge(kn_cp, n + 1)
                pe.wait_ge(kr_cp, n + 1)
                pe.wait_ge(qn_cp, NP * (n + 1))
                pe.wait_ge(qr_cp, NP * (n + 1))
                pe.wait_ge(v_cp, B)
                for b in range(B):
                    if n:
                        pe.wait_ge(pv_cp, B * (n - 1) + b + 1)
                    tok = slice(b * P, (b + 1) * P)
                    for j in range(E_REP):
                        out = SC[b][:, j * P:(j + 1) * P]
                        pe.matmul(out, qnT[x][:, j, tok], knT[x][:, tok], start=True, stop=False)
                        last = pe.matmul(out, qrT[x][:, j // 2, tok], krT[j % 2][x][:, tok], start=False, stop=True)
                    last.then_inc(sc_mm, 1)
                if n + 1 < E_KV:
                    project(n + 1)
                for b in range(B):
                    pe.wait_ge(norm_done, B * n + b + 1)
                    for j in range(E_REP):
                        last = pe.transpose(SC[b][:, j * P:(j + 1) * P], S[b][:, j, :], ident)
                    last.then_inc(tr_mm, 1)
                for b in range(B):
                    pe.wait_ge(tr_cp, B * n + b + 1)
                    pe.matmul(SC[b], v[:, b, n * E_V:(n + 1) * E_V], PT[b][:].rearrange("p j q -> p (j q)"),
                              start=True, stop=True).then_inc(pv_mm, 1)
                pe.wait_ge(pv_cp, B * (n + 1))
                pe.wait_ge(qr_cp, min(NP * (n + 2), NP * E_KV))
                for b in range(B):
                    for j in range(E_REP):
                        last = pe.matmul(QR[0][:, b * D:(b + 1) * D], oT[b][:, j, :], wo[:, n * E_REP + j, :],
                                         start=(j == 0), stop=(j == E_REP - 1))
                last.then_inc(y_mm, 1)

        @block.scalar
        def _(act):
            env["ln_scalar"](4)
            act.wait_ge(c_mm, 1)
            act.copy(kvcT[:], KN[0:LAT, 0:TOK]).then_inc(c_cp, 1)
            act.copy(qcT[:].rearrange("p c t -> p (c t)"), KR[0:QH, :]).then_inc(c_cp, 1)
            for b in range(B):
                act.wait_ge(v_mm, b + 1)
                act.copy(v[:, b, :], SC[b]).then_inc(v_cp, 1)

            def copies(n):
                x = n % 2
                if n >= 2:
                    act.wait_ge(sc_mm, B * (n - 1))
                act.wait_ge(kn_mm, n + 1)
                act.copy(knT[x][:], KN[:, 0:TOK]).then_inc(kn_cp, 1)
                for k in range(NP):
                    act.wait_ge(qn_mm, NP * n + k + 1)
                    act.copy(qnT[x][:, 2 * k:2 * k + 2, :].rearrange("p h t -> p (h t)"), QN[k]).then_inc(qn_cp, 1)

            copies(0)
            for n in range(E_KV):
                for b in range(B):
                    act.wait_ge(nmax_done, B * n + b + 1)
                    for j in range(E_REP):
                        last = act.activation(S[b][:, j, :], S[b][:, j, :], ACT.Exp, bias=nmax[b][:, j:j + 1],
                                              accum_out=sums[b][:, j:j + 1])
                    last.then_inc(exp_done, 1)
                if n + 1 < E_KV:
                    copies(n + 1)
                for b in range(B):
                    act.wait_ge(pv_mm, B * n + b + 1)
                    if n:
                        act.wait_ge(y_mm, n)
                    act.copy(oT[b][:].rearrange("p j q -> p (j q)"), SC[b]).then_inc(pv_cp, 1)

        @block.vector
        def _(dve):
            env["ln_vector"](4)
            dve.wait_ge(kz, 4)
            cos, sin = cst[:, C_CE:C_CE + TOK], cst[:, C_SE:C_SE + TOK]
            causal = cst[:, C_CAUSAL:C_CAUSAL + P].unsqueeze(1).to_broadcast([P, E_REP, P])

            def rotate_keys(n):
                x = n % 2
                if n >= 2:
                    dve.wait_ge(sc_mm, B * (n - 1))
                dve.wait_ge(kr_mm, n + 1)
                dve.tensor_tensor(r1[:], KR[:, 0:TOK], cos, ALU.mult)
                link(dve.tensor_tensor(r2[:], KR[:, TOK:2 * TOK], sin, ALU.mult))
                dve.tensor_tensor(krT[0][x][0:64, :], r1[0:64, :], r2[0:64, :], ALU.add)
                dve.tensor_tensor(krT[1][x][64:P, :], r1[64:P, :], r2[64:P, :], ALU.add).then_inc(kr_cp, 1)
                dve.wait_ge(kr_cp, n + 1)

            def rotate_queries(n, pairs):
                x = n % 2
                for k in pairs:
                    dve.wait_ge(qr_mm, NP * n + k + 1)
                    dve.tensor_tensor(r1[:], QR[k][:, 0:TOK], cos, ALU.mult)
                    link(dve.tensor_tensor(r2[:], QR[k][:, TOK:2 * TOK], sin, ALU.mult))
                    dve.tensor_tensor(qrT[x][:, k, :], r1[:], r2[:], ALU.add).then_inc(qr_cp, 1)
                    dve.wait_ge(qr_cp, NP * n + k + 1)

            rotate_keys(0)
            rotate_queries(0, range(NP))
            for n in range(E_KV):
                for b in range(B):
                    if n:
                        dve.wait_ge(tr_mm, B * (n - 1) + b + 1)
                    dve.wait_ge(sc_mm, B * n + b + 1)
                    dve.scalar_tensor_tensor(S[b][:], SC[b].rearrange("p (j k) -> p j k", j=E_REP), scale, causal,
                                             ALU.mult, ALU.add).then_inc(masked, 1)
                    dve.wait_ge(masked, B * n + b + 1)
                    dve.tensor_reduce(nmax[b][:], S[b][:], AX, ALU.max, negate=True).then_inc(nmax_done, 1)
                if n + 1 < E_KV:
                    rotate_keys(n + 1)
                for b in range(B):
                    dve.wait_ge(exp_done, B * n + b + 1)
                    link(dve.reciprocal(rec[b][:], sums[b][:]))
                    dve.tensor_tensor(S[b][:], S[b][:], rec[b][:].unsqueeze(2).to_broadcast([P, E_REP, P]), ALU.mult).then_inc(norm_done, 1)
                if n + 1 < E_KV:
                    rotate_queries(n + 1, (0,))
                for b in range(B):
                    dve.wait_ge(tr_mm, B * n + b + 1)
                    dve.tensor_copy(PT[b][:].rearrange("p j q -> p (j q)"), SC[b]).then_inc(tr_cp, 1)
                if n + 1 < E_KV:
                    rotate_queries(n + 1, (1,))
                dve.wait_ge(y_mm, n + 1)
                dve.tensor_tensor(X[:].rearrange("p b d -> p (b d)"), X[:].rearrange("p b d -> p (b d)"), QR[0], ALU.add).then_inc(x_acc, 1)
                dve.wait_ge(x_acc, n + 1)


def early_f(a, sb, sem):
    ER = M_E * M_R
    EC = ER // P
    w = dict(
        wg=sb("f_wg", [P, DC, M_E]), w1=sb("f_w1", [P, DC, M_F]), w3=sb("f_w3", [P, DC, M_F]),
        a1=sb("f_a1", [P, DC, ER]), a3=sb("f_a3", [P, DC, ER]), b1=sb("f_b1", [P, EC, M_F]), b3=sb("f_b3", [P, EC, M_F]),
        w2=sb("f_w2", [P, FCH, D]), a2=sb("f_a2", [P, FCH, ER]), b2=sb("f_b2", [P, EC, D]), w_in=sem("f_w_in"))
    arrays = ((w["wg"], "f_wg"), (w["a1"], "f_a1"), (w["a3"], "f_a3"), (w["w1"], "f_w1"), (w["b1"], "f_b1"), (w["w3"], "f_w3"), (w["b3"], "f_b3"),
              (w["w2"], "f_w2"), (w["a2"], "f_a2"), (w["b2"], "f_b2"))
    w["loads"] = len(arrays)

    def load(sp):
        for t, d in arrays:
            sp.dma_start(t[:], a[d]).then_inc(w["w_in"], 16)

    w["load"] = load
    return w


def stage_f(nc, a, env, own):
    X, xnT, bk, ident, cst, s = (env[k] for k in ("X", "xnT", "bk", "ident", "cst", "s"))
    link = env["dve_link"]
    ER = M_E * M_R
    EC = ER // P
    KTOK = M_K * TOK

    def sb(name, shape, dt=F32):
        return own.enter_context(nc.sbuf_tensor("f_" + name, shape, dt))

    def sem(name):
        env["used"].append(own.enter_context(nc.semaphore("f_" + name)))
        return env["used"][-1]

    w = env["w_f"]
    wg, w1, w3, a1, a3, b1, b3, w2, a2, b2, w_in = w["wg"], w["w1"], w["w3"], w["a1"], w["a3"], w["b1"], w["b3"], w["w2"], w["a2"], w["b2"], w["w_in"]
    nm, sums, rs = sb("nm", [P, B]), sb("sums", [P, B]), sb("rs", [P, B])
    pr = [sb(f"pr{k}", [P, B, M_E]) for k in range(3)]
    eq, oh = sb("eq", [P, B, M_E]), sb("oh", [P, M_K, B, M_E])
    top, ix, tot, rw = sb("top", [P, M_K, B]), sb("ix", [P, B]), sb("tot", [P, B]), sb("rw", [P, M_K, B])
    mk = sb("mk", [P, M_K * B, M_E, M_R])
    mkT = sb("mkT", [P, EC, KTOK])
    am = [sb(f"am{k}", [P, EC, KTOK]) for k in range(3)]
    g1 = [sb(f"g1{k}", [P, KTOK]) for k in range(2)]
    base = [sb(f"base{k}", [P, 2, TOK]) for k in range(2)]
    x2, x2s = sb("x2", [P, FCH, KTOK]), sb("x2s", [P, FCH, TOK])
    rwt, ams = sb("rwt", [P, KTOK]), sb("ams", [P, EC, TOK])
    (lg_mm, nm_done, ex_done, mk_done, mt_mm, mt_cp, a_mm, am_done, base_mm, base_cp, x1_mm, x3_mm, h1_done, h3_done, g_done, gated,
     rw_done, rw_mm, rw_cp, x2_done, x2s_done, a2_mm, a2_done, ams_done, y_mm) = (sem(n) for n in (
         "lg_mm nm_done ex_done mk_done mt_mm mt_cp a_mm am_done base_mm base_cp x1_mm x3_mm h1_done h3_done g_done gated "
         "rw_done rw_mm rw_cp x2_done x2s_done a2_mm a2_done ams_done y_mm").split())
    G1, G3 = [bk[2], bk[3]], [bk[4], bk[5]]

    def slots(ap):
        return ap.unsqueeze(1).to_broadcast([P, M_K, TOK])

    with nc.Block() as block:
        @block.gpsimd
        def _(pool):
            env["ln_gpsimd"](5)

        @block.tensor
        def _(pe):
            env["ln_tensor"](5)
            pe.wait_ge(w_in, 16 * w["loads"])
            pe.wait_ge(s["ln_xT"], env["turned"](5))
            for b in range(B):
                for c in range(DC):
                    last = pe.matmul(bk[0][:, b * M_E:(b + 1) * M_E], xnT[:, c, b * P:(b + 1) * P], wg[:, c, :],
                                     start=(c == 0), stop=(c == DC - 1))
            last.then_inc(lg_mm, 1)
            for k, low in enumerate((a1, a3)):
                for e in range(EC):
                    for c in range(DC):
                        last = pe.matmul(bk[6 + k][:, e * TOK:(e + 1) * TOK], low[:, c, e * P:(e + 1) * P], xnT[:, c, :],
                                         start=(c == 0), stop=(c == DC - 1))
                last.then_inc(a_mm, 1)
            pe.wait_ge(mk_done, M_K * B)
            for e in range(EC):
                for kb in range(M_K * B):
                    last = pe.transpose(bk[e][:, kb * P:(kb + 1) * P], mk[:, kb].rearrange("p e r -> p (e r)")[:, e * P:(e + 1) * P], ident)
                last.then_inc(mt_mm, 1)
            pe.wait_ge(mt_cp, EC)
            for f in range(FCH):
                cols = slice(f * P, (f + 1) * P)
                if f >= 2:
                    pe.wait_ge(base_cp, f - 1)
                for k, wide in enumerate((w1, w3)):
                    for c in range(DC):
                        last = pe.matmul(bk[f % 2][:, k * TOK:(k + 1) * TOK], wide[:, c, cols], xnT[:, c, :], start=(c == 0), stop=(c == DC - 1))
                last.then_inc(base_mm, 1)
                for bank, low, m, free, done in ((G1, b1, am[0], h1_done, x1_mm), (G3, b3, am[1], h3_done, x3_mm)):
                    if f >= 2:
                        pe.wait_ge(free, f - 1)
                    if f == 0:
                        pe.wait_ge(am_done, EC * (1 if m is am[0] else 2))
                    for e in range(EC):
                        last = pe.matmul(bank[f % 2], low[:, e, cols], m[:, e, :], start=(e == 0), stop=(e == EC - 1))
                    last.then_inc(done, 1)
                if f == 0:
                    pe.wait_ge(rw_done, 1)
                    for k in range(M_K):
                        for b in range(B):
                            last = pe.matmul(bk[7][:, (k * B + b) * P:(k * B + b + 1) * P], rw[:, k, b:b + 1].to_broadcast([P, P]), ident,
                                             start=True, stop=True)
                    last.then_inc(rw_mm, 1)
            pe.wait_ge(rw_cp, 1)
            for e in range(EC):
                for f in range(FCH):
                    pe.wait_ge(x2_done, f + 1)
                    last = pe.matmul(bk[6 + e], a2[:, f, e * P:(e + 1) * P], x2[:, f, :], start=(f == 0), stop=(f == FCH - 1))
                last.then_inc(a2_mm, 1)
            pe.wait_ge(base_cp, FCH)
            for b in range(B):
                t = slice(b * P, (b + 1) * P)
                for f in range(FCH):
                    pe.wait_ge(x2s_done, f + 1)
                    pe.matmul(bk[b][:, 0:D], x2s[:, f, t], w2[:, f, :], start=(f == 0), stop=False)
            for b in range(B):
                t = slice(b * P, (b + 1) * P)
                for e in range(EC):
                    pe.wait_ge(ams_done, e + 1)
                    last = pe.matmul(bk[b][:, 0:D], ams[:, e, t], b2[:, e, :], start=False, stop=(e == EC - 1))
                last.then_inc(y_mm, 1)

        @block.scalar
        def _(act):
            env["ln_scalar"](5)
            act.wait_ge(nm_done, 1)
            for b in range(B):
                last = act.activation(pr[0][:, b, :], bk[0][:, b * M_E:(b + 1) * M_E], ACT.Exp, bias=nm[:, b:b + 1],
                                      accum_out=sums[:, b:b + 1])
            last.then_inc(ex_done, 1)
            for e in range(EC):
                act.wait_ge(mt_mm, e + 1)
                act.copy(mkT[:, e, :], bk[e]).then_inc(mt_cp, 1)
            for f in range(FCH):
                act.wait_ge(base_mm, f + 1)
                if f >= 2:
                    act.wait_ge(h3_done, f - 1)
                act.copy(base[f % 2][:].rearrange("p k t -> p (k t)"), bk[f % 2]).then_inc(base_cp, 1)
                act.wait_ge(h1_done, f + 1)
                act.activation(g1[f % 2][:], g1[f % 2][:], ACT.Silu).then_inc(g_done, 1)
                if f == 0:
                    act.wait_ge(rw_mm, 1)
                    act.copy(rwt[:], bk[7]).then_inc(rw_cp, 1)

        @block.vector
        def _(dve):
            env["ln_vector"](5)
            dve.wait_ge(lg_mm, 1)
            dve.tensor_reduce(nm[:], bk[0][:, 0:B * M_E].rearrange("p (b e) -> p b e", b=B), AX, ALU.max, negate=True).then_inc(nm_done, 1)
            dve.wait_ge(ex_done, 1)
            link(dve.reciprocal(rs[:], sums[:]))
            link(dve.tensor_tensor(pr[1][:], pr[0][:], rs[:].unsqueeze(2).to_broadcast([P, B, M_E]), ALU.mult))
            iota = cst[:, C_IOTA:C_IOTA + M_E].unsqueeze(1).to_broadcast([P, B, M_E])
            for k in range(M_K):
                p = pr[1 + k]
                link(dve.tensor_reduce(top[:, k, :], p[:], AX, ALU.max))
                link(dve.tensor_tensor(eq[:], p[:], top[:, k, :].unsqueeze(2).to_broadcast([P, B, M_E]), ALU.is_equal))
                link(dve.tensor_tensor(eq[:], eq[:], iota, ALU.mult))
                link(dve.tensor_reduce(ix[:], eq[:], AX, ALU.min))
                link(dve.tensor_tensor(oh[:, k], iota, ix[:].unsqueeze(2).to_broadcast([P, B, M_E]), ALU.is_equal))
                if k == 0:
                    link(dve.scalar_tensor_tensor(pr[2][:], oh[:, 0], -4.0, pr[1][:], ALU.mult, ALU.add))
            for k in range(M_K):
                for b in range(B):
                    dve.tensor_copy(mk[:, k * B + b], oh[:, k, b, :].unsqueeze(2).to_broadcast([P, M_E, M_R])).then_inc(mk_done, 1)
            link(dve.tensor_tensor(tot[:], top[:, 0, :], top[:, 1, :], ALU.add))
            link(dve.reciprocal(tot[:], tot[:]))
            dve.tensor_tensor(rw[:], top[:], tot[:].unsqueeze(1).to_broadcast([P, M_K, B]), ALU.mult).then_inc(rw_done, 1)
            for k in range(2):
                dve.wait_ge(a_mm, k + 1)
                for e in range(EC):
                    dve.wait_ge(mt_cp, e + 1)
                    dve.tensor_tensor(am[k][:, e, :].rearrange("p (k t) -> p k t", k=M_K), slots(bk[6 + k][:, e * TOK:(e + 1) * TOK]),
                                      mkT[:, e, :].rearrange("p (k t) -> p k t", k=M_K), ALU.mult).then_inc(am_done, 1)
            for f in range(FCH):
                for bank, k, ready, dst, done in ((G1, 0, x1_mm, g1[f % 2][:], h1_done), (G3, 1, x3_mm, x2[:, f, :], h3_done)):
                    dve.wait_ge(ready, f + 1)
                    dve.wait_ge(base_cp, f + 1)
                    if k == 0 and f >= 2:
                        dve.wait_ge(gated, f - 1)
                    dve.tensor_tensor(dst.rearrange("p (k t) -> p k t", k=M_K), bank[f % 2].rearrange("p (k t) -> p k t", k=M_K),
                                      slots(base[f % 2][:, k, :]), ALU.add).then_inc(done, 1)
                dve.wait_ge(g_done, f + 1)
                dve.wait_ge(h3_done, f + 1)
                dve.tensor_tensor(x2[:, f, :], g1[f % 2][:], x2[:, f, :], ALU.mult).then_inc(gated, 1)
                dve.wait_ge(gated, f + 1)
                dve.wait_ge(rw_cp, 1)
                dve.tensor_tensor(x2[:, f, :], x2[:, f, :], rwt[:], ALU.mult).then_inc(x2_done, 1)
                dve.wait_ge(x2_done, f + 1)
                dve.tensor_tensor(x2s[:, f, :], x2[:, f, 0:TOK], x2[:, f, TOK:KTOK], ALU.add).then_inc(x2s_done, 1)
            for e in range(EC):
                dve.wait_ge(a2_mm, e + 1)
                dve.tensor_tensor(am[2][:, e, :], bk[6 + e], mkT[:, e, :], ALU.mult).then_inc(a2_done, 1)
                dve.wait_ge(a2_done, e + 1)
                dve.tensor_tensor(ams[:, e, :], am[2][:, e, 0:TOK], am[2][:, e, TOK:KTOK], ALU.add).then_inc(ams_done, 1)
            for b in range(B):
                dve.wait_ge(y_mm, b + 1)
                link(dve.tensor_tensor(X[:, b, :], bk[b][:, 0:D], X[:, b, :], ALU.add))


def _constants():
    import numpy as np
    i = np.arange(P)
    c = np.zeros((P, C_ALL), np.float32)
    c[:, C_ID:C_ID + P] = np.eye(P)
    c[:, C_UP:C_UP + P] = i[:, None] <= i[None, :]
    c[:, C_LOW:C_LOW + P] = i[:, None] > i[None, :]
    c[:, C_CAUSAL:C_CAUSAL + P] = np.where(i[None, :] <= i[:, None], 0.0, MASKED)
    for level in range(LEVELS):
        w = 1 << level
        m = (i[:, None] // (2 * w) == i[None, :] // (2 * w)) & (i[:, None] // w % 2 == 1) & (i[None, :] // w % 2 == 0)
        c[:, C_LV + level * P:C_LV + (level + 1) * P] = m
        c[:, C_LVT + level * P:C_LVT + (level + 1) * P] = m.T
    inv = (1.0 / 10000.0 ** (np.arange(0, X_CQ, 2, dtype=np.float32) / X_CQ)).astype(np.float32)
    ang = np.repeat(i[:, None].astype(np.float32) * inv[None, :], 2, axis=-1)
    for half in range(2):
        cs = np.cos(ang[:, half * XQ:(half + 1) * XQ]).T
        sn = np.sin(ang[:, half * XQ:(half + 1) * XQ]).T * (-1.0 if half == 0 else 1.0)
        for b in range(B):
            c[0:XQ, C_CQ + half * TOK + b * P:C_CQ + half * TOK + (b + 1) * P] = cs
            c[0:XQ, C_SQ + half * TOK + b * P:C_SQ + half * TOK + (b + 1) * P] = sn
    theta = (1.0 / 10000.0 ** (np.arange(0, E_ROPE, 2, dtype=np.float32) / E_ROPE)).astype(np.float32)
    ang = i[:, None].astype(np.float32) * theta[None, :]
    cs, sn = np.cos(ang).T, np.sin(ang).T
    for b in range(B):
        c[:, C_CE + b * P:C_CE + (b + 1) * P] = np.concatenate([cs] * 4)
        c[:, C_SE + b * P:C_SE + (b + 1) * P] = np.concatenate([-sn, sn, -sn, sn])
    c[:, C_IOTA:C_IOTA + M_E] = np.arange(M_E) - BIG
    inv = (1.0 / 10000.0 ** (np.arange(0, LAT, 2, dtype=np.float32) / LAT)).astype(np.float32)
    ang = np.repeat(np.arange(CTX, dtype=np.float32)[:, None] * inv[None, :], 2, axis=-1)
    cs, sn = np.cos(ang), np.sin(ang)
    sn[:, 0:LAT // 2] = -sn[:, 0:LAT // 2]
    rope = np.stack([cs.reshape(KT, P, LAT).transpose(1, 0, 2), sn.reshape(KT, P, LAT).transpose(1, 0, 2)], 1)
    return c, np.ascontiguousarray(rope.astype(np.float32))


def _kmajor(w):
    k, n = w.shape
    return w.reshape(k // P, P, n).transpose(1, 0, 2)


def kernel(**inputs):
    import numpy as np
    import concourse.bacc as _bacc
    from concourse.bass_utils import run_bass_kernel_spmd as _run

    t = {k: np.asarray(v) for k, v in inputs.items()}
    cst, rope = _constants()
    ctx = t["ctx_512"]
    w = t["L0_attn_W_qkvz"].reshape(G_QK, 6 * P, DC, P)
    conv = t["L0_attn_conv_w"]
    nq = G_QK * G_HD
    conv = np.stack([conv[0:nq].reshape(G_QK, P, TAPS), conv[nq:2 * nq].reshape(G_QK, P, TAPS)]
                    + [conv[2 * nq:].reshape(G_QK, RATIO, P, TAPS)[:, r] for r in range(RATIO)], 2)
    ba = t["L0_attn_W_ba"].reshape(G_QK, 2, RATIO, D).transpose(1, 0, 2, 3).reshape(2 * G_V, D)
    arrays = {
        "x": t["x"], "cst": cst, "rope": rope,
        "a_ctxT": ctx[:, 0:P].transpose(2, 0, 1),
        "a_wq": _kmajor(t["L0_xattn_Wq"].T), "a_wkv": t["L0_xattn_Wkv_expand"].T, "a_wo": _kmajor(t["L0_xattn_Wout"].T),
        "b_slab": np.concatenate([w[:, 0:4 * P].transpose(0, 3, 2, 1).reshape(G_QK, P, DC * 4 * P),
                                  conv.reshape(G_QK, P, 4 * TAPS)], 2),
        "b_wz": w[:, 4 * P:6 * P].transpose(0, 3, 2, 1).reshape(G_QK, P, DC * 2 * P),
        "b_wo": t["L0_attn_W_out"].T.reshape(G_QK, RATIO, P, D).transpose(0, 2, 1, 3).reshape(G_QK, P, RATIO * D),
        "b_wba": _kmajor(ba.T),
        "b_dt": t["L0_attn_dt_bias"].reshape(1, G_V), "b_alog": t["L0_attn_A_log"].reshape(1, G_V),
        "b_norm": t["L0_attn_norm_w"].reshape(P, 1),
        "c_w1": _kmajor(t["L0_ffn_w1"].T), "c_w2": _kmajor(t["L0_ffn_w2"].T),
        "d_ctx": ctx.reshape(B, KT, P, LAT).transpose(2, 1, 0, 3),
        "d_w128": np.concatenate([t["L1_xattn_Wq"].reshape(X_H, X_K, DC, P).transpose(0, 3, 2, 1).reshape(X_H, P, DC * X_K),
                                  t["L1_xattn_w_kc_q"]], 2),
        "d_w64": np.concatenate([t["L1_xattn_W_qr"].transpose(0, 2, 1), t["L1_xattn_W_kr"].transpose(0, 2, 1)], 2),
        "d_wkv": t["L1_xattn_w_kc_kv"].transpose(1, 0, 2),
        "d_wo": t["L1_xattn_Wo"].T.reshape(X_H, X_K, D).transpose(1, 0, 2),
        "e_wkvd": _kmajor(t["L1_attn_W_kv_down"]), "e_wqd": _kmajor(t["L1_attn_W_q_down"]),
        "e_wkn": t["L1_attn_W_k_nope"], "e_wkr": t["L1_attn_W_k_rope"], "e_wv": t["L1_attn_W_v"],
        "e_wqn": t["L1_attn_W_q_nope"].reshape(2, 96, E_H * E_NOPE).transpose(1, 0, 2),
        "e_wqr": t["L1_attn_W_q_rope"].reshape(2, 96, E_H * E_ROPE).transpose(1, 0, 2),
        "e_wo": t["L1_attn_W_o"].reshape(E_H, P, D).transpose(1, 0, 2),
        "f_wg": _kmajor(t["L1_ffn_Wg"].T),
        "f_w1": _kmajor(t["L1_ffn_W1"].T), "f_w3": _kmajor(t["L1_ffn_W3"].T), "f_w2": _kmajor(t["L1_ffn_W2"].T),
        "f_a1": _kmajor(t["L1_ffn_A1"].reshape(M_E * M_R, D).T), "f_a3": _kmajor(t["L1_ffn_A3"].reshape(M_E * M_R, D).T),
        "f_b1": _kmajor(t["L1_ffn_B1"].transpose(0, 2, 1).reshape(M_E * M_R, M_F)),
        "f_b3": _kmajor(t["L1_ffn_B3"].transpose(0, 2, 1).reshape(M_E * M_R, M_F)),
        "f_a2": _kmajor(t["L1_ffn_A2"].reshape(M_E * M_R, M_F).T),
        "f_b2": _kmajor(t["L1_ffn_B2"].transpose(0, 2, 1).reshape(M_E * M_R, D)),
    }
    nc = _bacc.Bacc("TRN2", target_bir_lowering=False, num_devices=1)
    arrays = {k: np.ascontiguousarray(v) for k, v in arrays.items()}
    a = {k: nc.dram_tensor(f"in_{k}", v.shape, mybir.dt.from_np(v.dtype), kind="ExternalInput").ap()
         for k, v in arrays.items()}
    a["out"] = nc.dram_tensor("out_0", (B, P, D), F32, kind="ExternalOutput").ap()
    build(nc, a, UPTO)
    r = _run(nc, [{f"in_{k}": v for k, v in arrays.items()}], core_ids=[0])
    return r.results[0]["out_0"]


UPTO = 6
```
